# Optimizing a Trainium2 kernel written in Bass

```python
import numpy as np
import jax
import jax.numpy as jnp

def _softmax(x, axis=-1):
    return jax.nn.softmax(x, axis=axis)

def _gelu(x):
    return jax.nn.gelu(x, approximate=True)

def _silu(x):
    return jax.nn.silu(x)

def _sigmoid(x):
    return jax.nn.sigmoid(x)

def _layernorm(x, axis=-1, eps=1e-05):
    m = jnp.mean(x, axis=axis, keepdims=True)
    v = jnp.var(x, axis=axis, keepdims=True)
    return (x - m) / jnp.sqrt(v + eps)

def _scatter_add(tgt, idx, src, axis=0):
    return tgt.at[idx].add(src)

def _segment_sum(src, seg, n):
    return jax.ops.segment_sum(src, seg, n)
kernel_name = 'mk_perceiver_d1_seqx_r8_a252f5'

def setup_inputs(seed: int=0):
    np.random.seed(seed)
    _w = jnp.asarray

    def _rec_inputs():
        import jax
        import jax.numpy as jnp
        _rk = jax.random.key(seed)
        x = -0.0002928 + 1 * jax.random.normal(jax.random.fold_in(_rk, 1), (4, 128, 128), jnp.float32)
        _lenS = 128 - jax.random.randint(jax.random.fold_in(_rk, 7), (4,), 0, max(1, 128 // 4) + 1, jnp.int32)
        _lenS2 = 2048 - jax.random.randint(jax.random.fold_in(_rk, 8), (4,), 0, max(1, 2048 // 4) + 1, jnp.int32)
        _ctx_1024P = jax.random.normal(jax.random.fold_in(_rk, 11), (4, 16, 128), jnp.float32)
        _ctx_1024c = jax.random.dirichlet(jax.random.fold_in(_rk, 511), 0.3 * jnp.ones((16,), jnp.float32), (4, 2048))
        _ctx_1024t = jnp.einsum('bsk,bkd->bsd', _ctx_1024c, _ctx_1024P)
        _ctx_1024t = _ctx_1024t * jax.lax.rsqrt(jnp.mean(jnp.square(_ctx_1024t)) + 1e-12) * 0.953939
        ctx_1024 = -1.39393e-06 + 0.999914 * (_ctx_1024t + 0.3 * jax.random.normal(jax.random.fold_in(_rk, 611), (4, 2048, 128), jnp.float32))
        return (x, ctx_1024)
    x, ctx_1024 = _rec_inputs()

    def _L0_xattn_setup():
        import jax, jax.numpy as jnp
        import numpy as np
        HIDDEN, HEADS, HEAD_DIM = (128, 16, 64)
        BSZ, SEQ = (2, 256)
        SCALE = HEAD_DIM ** (-0.5)
        CAUSAL = True
        key = jax.random.key(seed)
        ks = jax.random.split(key, 7)
        inner = HEADS * HEAD_DIM
        init = lambda k, shape: jax.random.normal(k, shape, dtype=jnp.float32) * shape[0] ** (-0.5)
        return {'query': jax.random.normal(ks[0], (BSZ, SEQ, HIDDEN), dtype=jnp.float32), 'key': jax.random.normal(ks[1], (BSZ, SEQ, HIDDEN), dtype=jnp.float32), 'value': jax.random.normal(ks[2], (BSZ, SEQ, HIDDEN), dtype=jnp.float32), 'w_q': init(ks[3], (HIDDEN, inner)), 'w_k': init(ks[4], (HIDDEN, inner)), 'w_v': init(ks[5], (HIDDEN, inner)), 'w_o': init(ks[6], (inner, HIDDEN))}
    _L0_xattn_all = _L0_xattn_setup()
    _L0_xattn_in = {k: v for k, v in _L0_xattn_all.items() if k in ('w_q', 'w_k', 'w_v', 'w_o')}
    del _L0_xattn_all

    def _L0_attn_setup():
        import math
        import jax, jax.numpy as jnp
        import numpy as np
        D = 128
        B, L = (4, 512)

        def _linear(x, W, b):
            return jnp.einsum('bld,ed->ble', x, W) + b

        def _ma_k_activation(x, k=0.02):
            x = x / math.sqrt(x.shape[-1])
            return jax.nn.sigmoid(x * k)

        def _ma_q_activation(x):
            x = -x / math.sqrt(x.shape[-1])
            return -jnp.where(x >= 0, x, 0.02 * x)
        key = jax.random.key(seed)
        ks = jax.random.split(key, 9)
        s = 1.0 / math.sqrt(D)
        return {'x': jax.random.normal(ks[0], (B, L, D), dtype=jnp.float32), 'Wq1': jax.random.uniform(ks[1], (D, D), jnp.float32, -s, s), 'bq1': jax.random.uniform(ks[2], (D,), jnp.float32, -s, s), 'Wk1': jax.random.uniform(ks[3], (D, D), jnp.float32, -s, s), 'bk1': jax.random.uniform(ks[4], (D,), jnp.float32, -s, s), 'Wk2': jax.random.uniform(ks[5], (D, D), jnp.float32, -s, s), 'bk2': jax.random.uniform(ks[6], (D,), jnp.float32, -s, s), 'Wproj': jax.random.uniform(ks[7], (D, D), jnp.float32, -s, s), 'bproj': jax.random.uniform(ks[8], (D,), jnp.float32, -s, s)}
    _L0_attn_all = _L0_attn_setup()
    _L0_attn_in = {k: v for k, v in _L0_attn_all.items() if k in ('Wq1', 'bq1', 'Wk1', 'bk1', 'Wk2', 'bk2', 'Wproj', 'bproj')}
    del _L0_attn_all

    def _L0_ffn_setup():
        import jax, jax.numpy as jnp
        import numpy as np
        key = jax.random.key(seed)
        k0, k1, k2, k3 = jax.random.split(key, 4)
        B, S, D, F, E = (8, 256, 128, 256, 8)
        x = jax.random.normal(k0, (B, S, D), dtype=jnp.float32)
        Wg = jax.random.normal(k1, (D, E), dtype=jnp.float32) * 0.02
        W1 = jax.random.normal(k2, (E, D, F), dtype=jnp.float32) * 0.02
        W2 = jax.random.normal(k3, (E, F, D), dtype=jnp.float32) * 0.02
        return {'x': x, 'Wg': Wg, 'W1': W1, 'W2': W2}
    _L0_ffn_all = _L0_ffn_setup()
    _L0_ffn_in = {k: v for k, v in _L0_ffn_all.items() if k in ('Wg', 'W1', 'W2')}
    del _L0_ffn_all
    return {'x': x, 'ctx_1024': ctx_1024, 'L0_xattn_w_q': _L0_xattn_in['w_q'], 'L0_xattn_w_k': _L0_xattn_in['w_k'], 'L0_xattn_w_v': _L0_xattn_in['w_v'], 'L0_xattn_w_o': _L0_xattn_in['w_o'], 'L0_attn_Wq1': _L0_attn_in['Wq1'], 'L0_attn_bq1': _L0_attn_in['bq1'], 'L0_attn_Wk1': _L0_attn_in['Wk1'], 'L0_attn_bk1': _L0_attn_in['bk1'], 'L0_attn_Wk2': _L0_attn_in['Wk2'], 'L0_attn_bk2': _L0_attn_in['bk2'], 'L0_attn_Wproj': _L0_attn_in['Wproj'], 'L0_attn_bproj': _L0_attn_in['bproj'], 'L0_ffn_Wg': _L0_ffn_in['Wg'], 'L0_ffn_W1': _L0_ffn_in['W1'], 'L0_ffn_W2': _L0_ffn_in['W2']}

def reference(x, ctx_1024, L0_xattn_w_q, L0_xattn_w_k, L0_xattn_w_v, L0_xattn_w_o, L0_attn_Wq1, L0_attn_bq1, L0_attn_Wk1, L0_attn_bk1, L0_attn_Wk2, L0_attn_bk2, L0_attn_Wproj, L0_attn_bproj, L0_ffn_Wg, L0_ffn_W1, L0_ffn_W2):
    import jax
    import jax.numpy as jnp

    def _L0_xattn_ref(query, key, value, w_q, w_k, w_v, w_o):
        import jax, jax.numpy as jnp
        import numpy as np
        HIDDEN, HEADS, HEAD_DIM = (128, 16, 64)
        BSZ, SEQ = (2, 256)
        SCALE = HEAD_DIM ** (-0.5)
        CAUSAL = True
        bsz, q_len, _ = query.shape
        k_len = key.shape[1]

        def split_heads(x):
            return x.reshape(x.shape[0], x.shape[1], HEADS, HEAD_DIM).transpose(0, 2, 1, 3)
        q = split_heads(query @ w_q)
        k = split_heads(key @ w_k)
        v = split_heads(value @ w_v)
        scores = jnp.einsum('bhqd,bhkd->bhqk', q, k) * SCALE
        if CAUSAL:
            q_pos = jnp.arange(q_len)
            k_pos = jnp.arange(k_len)
            mask = (k_pos[None, :] <= q_pos[:, None]).astype(scores.dtype)
            scores = scores + (1.0 - mask)[None, None, :, :] * -10000.0
        weights = jax.nn.softmax(scores, axis=-1)
        out = jnp.einsum('bhqk,bhkd->bhqd', weights, v)
        out = out.transpose(0, 2, 1, 3).reshape(bsz, q_len, HEADS * HEAD_DIM)
        return out @ w_o

    def _L0_attn_ref(x, Wq1, bq1, Wk1, bk1, Wk2, bk2, Wproj, bproj):
        import math
        import jax, jax.numpy as jnp
        import numpy as np
        D = 128
        B, L = (4, 512)

        def _linear(x, W, b):
            return jnp.einsum('bld,ed->ble', x, W) + b

        def _ma_k_activation(x, k=0.02):
            x = x / math.sqrt(x.shape[-1])
            return jax.nn.sigmoid(x * k)

        def _ma_q_activation(x):
            x = -x / math.sqrt(x.shape[-1])
            return -jnp.where(x >= 0, x, 0.02 * x)
        V = x
        K = jnp.exp(_linear(x, Wk1, bk1))
        K_cum = jnp.cumsum(K, axis=1) + 1e-06
        S = jnp.cumsum(K * V, axis=1) / K_cum
        Q = jax.nn.sigmoid(_linear(x, Wq1, bq1))
        O_ar = S * Q
        zero = jnp.zeros_like(x[:, :1, :])
        E = jnp.concatenate([zero, V[:, 1:, :] - O_ar[:, :-1, :]], axis=1)
        qk2_in = jnp.concatenate([zero, x[:, :-1, :]], axis=1)
        K2 = _ma_k_activation(_linear(qk2_in, Wk2, bk2))
        S2 = jnp.cumsum(K2 * E, axis=1)
        Q2 = _ma_q_activation(Q)
        Q2 = jnp.concatenate([zero, Q2[:, :-1, :]], axis=1)
        O_ma = S2 * Q2
        return _linear(O_ar + O_ma, Wproj, bproj)

    def _L0_ffn_ref(x, Wg, W1, W2):
        import jax, jax.numpy as jnp
        import numpy as np
        B, S, D = x.shape
        E = Wg.shape[1]
        T = B * S
        cap = max(1, T // E)
        xt = x.reshape(T, D)
        logits = xt @ Wg
        probs = jax.nn.softmax(logits, axis=-1)
        pT = probs.T
        _, top_idx = jax.lax.top_k(pT, cap)
        sel = jnp.zeros((E, T), dtype=bool).at[jnp.arange(E)[:, None], top_idx].set(True)
        masked = jnp.where(sel, pT, -jnp.inf)
        assigned = sel.any(axis=0)
        tok2exp = jnp.where(assigned, jnp.argmax(masked, axis=0), jnp.argmax(pT, axis=0))
        weights = jnp.take_along_axis(probs, tok2exp[:, None], axis=1)[:, 0]
        out = jnp.zeros_like(xt)
        for e in range(E):
            gate = jnp.where(tok2exp == e, weights, 0.0)
            h = jax.nn.gelu(xt @ W1[e], approximate=False) @ W2[e]
            out = out + gate[:, None] * h
        return out.reshape(B, S, D)
    x = x + _L0_xattn_ref(_layernorm(x, axis=-1), ctx_1024, ctx_1024, L0_xattn_w_q, L0_xattn_w_k, L0_xattn_w_v, L0_xattn_w_o)
    x = x + _L0_attn_ref(_layernorm(x, axis=-1), L0_attn_Wq1, L0_attn_bq1, L0_attn_Wk1, L0_attn_bk1, L0_attn_Wk2, L0_attn_bk2, L0_attn_Wproj, L0_attn_bproj)
    x = x + _L0_ffn_ref(_layernorm(x, axis=-1), L0_ffn_Wg, L0_ffn_W1, L0_ffn_W2)
    return x

_drawn_inputs = setup_inputs


def setup_inputs(seed=0):
    import zlib

    import numpy as np

    out = dict(_drawn_inputs(seed))
    spreads = {}
    factors = {'L0_attn_bq1': 8.0,
     'L0_attn_bk1': 200.0,
     'L0_attn_Wk2': 200.0,
     'L0_attn_bk2': 200.0,
     'L0_ffn_Wg': 8.0,
     'L0_ffn_W1': 8.0,
     'L0_ffn_W2': 8.0}
    for name, (base, spread) in spreads.items():
        noise = np.random.default_rng([zlib.crc32(name.encode()), seed]).standard_normal(out[name].shape)
        drawn = base * np.exp(spread * noise) if base else spread * noise
        out[name] = jnp.asarray(drawn.astype(out[name].dtype))
    for name, factor in factors.items():
        out[name] = (out[name] * factor).astype(out[name].dtype)
    return out
```

```python
from contextlib import ExitStack

import concourse.bass as bass
from concourse import mybir

ALU = mybir.AluOpType
ACT = mybir.ActivationFunctionType
F32 = mybir.dt.float32
BF16 = mybir.dt.bfloat16
I32 = mybir.dt.int32
AX_X = mybir.AxisListType.X

P = 128
EPS_LN = 1e-5
EPS_CUM = 1e-6
LEAK = 0.02
MASK_A, MASK_B = 100.0, -100.0
SCORE_LIMIT = 4900.0


def perceiver_layer(nc, x, ctx, ctx_t, w_q, w_k, w_v, w_o, attn_w, attn_b, b_proj, w_g, w_1, w_2, out):
    B, T, D = x.shape
    KEYS = ctx.shape[1]
    INNER = w_q.shape[1]
    HD = 64
    H = INNER // HD
    NE, _, FF = w_1.shape
    FC = FF // P
    NT = B * T
    CAP = NT // NE
    IC = INNER // P
    KB = KEYS // P
    assert T == P and D == P and B == 4 and H == 16
    QSCALE = HD ** -0.5
    K2_SCALE = LEAK / D ** 0.5
    GROUPS = ((0, 1), (2, 3))
    NG = len(GROUPS)
    SETS = 2 * B
    UNITS = 2 * SETS
    GUARD_CHUNKS = 16
    GUARD_W = B * KEYS // P // GUARD_CHUNKS * D
    GUARD_LOADS = 4
    GUARD_LIMIT = SCORE_LIMIT ** 2 / (D * QSCALE ** 2)

    with ExitStack() as es:
        def sb(name, shape, dt=F32):
            return es.enter_context(nc.sbuf_tensor(name, shape, dt))

        def sem(name):
            return es.enter_context(nc.semaphore(name))

        score_ps = [es.enter_context(nc.psum_tensor(f"score_ps{i}", [P, 512], F32)) for i in range(4)]
        turn_ps = [es.enter_context(nc.psum_tensor(f"turn_ps{i}", [P, 512], F32)) for i in range(2)]
        head_ps = es.enter_context(nc.psum_tensor("head_ps", [P, 512], F32))
        misc_ps = es.enter_context(nc.psum_tensor("misc_ps", [P, 512], F32))

        x_sb = sb("x_sb", [P, B, D])
        ctxk_sb = sb("ctxk_sb", [P, B, T])
        ctx_sb = sb("ctx_sb", [P, GUARD_CHUNKS, GUARD_W])
        sq_sb = sb("sq_sb", [P, 2, GUARD_W])
        wq_sb = sb("wq_sb", [P, INNER])
        wk_sb = sb("wk_sb", [P, INNER])
        wv_sb = sb("wv_sb", [P, INNER])
        wo_sb = sb("wo_sb", [P, IC, D])
        aw_sb = sb("aw_sb", [P, 4, D])
        ab_sb = sb("ab_sb", [P, 3])
        bproj_sb = sb("bproj_sb", [P, D])
        wg_sb = sb("wg_sb", [P, NE])
        w1_sb = sb("w1_sb", [P, NE, FF])
        w2_sb = sb("w2_sb", [P, NE, FC, D])

        ident = sb("ident", [P, P])
        ident_a = sb("ident_a", [P, P], BF16)
        causal_b = sb("causal_b", [P, 4, P], BF16)
        ones = sb("ones", [P, P])
        minus_half = sb("minus_half", [P, 4])

        stats = sb("stats", [P, B, 6])
        mv = sb("mv", [P, B, 2])
        rstd = sb("rstd", [P, B])
        xn_sb = sb("xn_sb", [P, B, D])
        xnT_sb = sb("xnT_sb", [P, B, T])
        kT_sb = sb("kT_sb", [P, IC, NT])
        qT_sb = sb("qT_sb", [P, IC, NT])
        v_sb = sb("v_sb", [P, B, H, HD + 1])

        negmax = sb("negmax", [P, UNITS, 4])
        probs = sb("probs", [P, 4, 4, T])
        probsT = sb("probsT", [P, 2, 4, T])
        rsum = sb("rsum", [P, UNITS, 4])
        wsq_sb = probs[:].rearrange("p a b c -> p (a b c)").rearrange("p (w h d) -> p w h d", w=2, h=H)
        ksum = sb("ksum", [P, GUARD_CHUNKS])
        kmax = sb("kmax", [P, 1])
        wsum = sb("wsum", [P, 2 * H])
        bound = sb("bound", [1, 2 * H + 3])
        flag = sb("flag", [1, 1], I32)
        gone = ctx_sb[:].rearrange("p a b -> p (a b)")
        heads = gone[:, 0:B * INNER].rearrange("p (b h d) -> p b h d", b=B, h=H)
        headsT = gone[:, B * INNER:2 * B * INNER].rearrange("p (c b t) -> p c b t", c=IC, b=B)

        key_room = kT_sb[:].rearrange("p c t -> p (c t)")
        query_room = qT_sb[:].rearrange("p c t -> p (c t)")
        value_room = v_sb[:].rearrange("p b h d -> p (b h d)")
        all_ctx = key_room[:, 0:KEYS]
        all_keys = key_room[0:HD, KEYS:2 * KEYS]
        all_probs = query_room[:, 0:KEYS]
        all_probsT = query_room[:, KEYS:2 * KEYS]
        all_values = value_room[:, 0:KB * HD]
        head_w = value_room[:, KB * HD:(KB + 3) * HD].rearrange("p (w d) -> p w d", w=3)
        batch_x = value_room[:, (KB + 3) * HD:(KB + 5) * HD]
        head_q = value_room[0:HD, (KB + 5) * HD:(KB + 7) * HD]
        all_negmax = sb("all_negmax", [P, 1])
        all_sum = sb("all_sum", [P, 2])
        spare = sb("spare", [P, 1])
        heads_flat = gone[:, 0:B * INNER]

        x1_sb = sb("x1_sb", [P, B, D])
        x1b_sb = sb("x1b_sb", [P, B, D])
        stats2 = sb("stats2", [P, B, 6])
        mv2 = sb("mv2", [P, B, 2])
        rstd2 = sb("rstd2", [P, B])
        xa_sb = sb("xa_sb", [P, B, D])
        xaT = sb("xaT", [P, B, T])
        hb_sb = sb("hb_sb", [P, 2])
        K_sb = sb("K_sb", [P, B, T])
        KV_sb = sb("KV_sb", [P, B, T])
        Kc_sb = sb("Kc_sb", [P, B, T])
        KVc_sb = sb("KVc_sb", [P, B, T])
        tq_sb = sb("tq_sb", [P, B, T])
        tk_sb = sb("tk_sb", [P, B, T])
        Q_sb = sb("Q_sb", [P, B, T])
        Q2_sb = sb("Q2_sb", [P, B, T])
        K2_sb = sb("K2_sb", [P, B, T])
        S_sb = KVc_sb
        Oar_sb = sb("Oar_sb", [P, B, T])
        E_sb = sb("E_sb", [P, B, T])
        S2_sb = sb("S2_sb", [P, B, T])
        Oma_sb = S_sb
        x2_sb = sb("x2_sb", [P, B, D])
        stats3 = sb("stats3", [P, B, 6])
        mv3 = sb("mv3", [P, B, 2])
        rstd3 = sb("rstd3", [P, B])
        xf_sb = sb("xf_sb", [P, B, D])
        xfT = sb("xfT", [P, B, T])

        lmax = sb("lmax", [P, B])
        lsh = sb("lsh", [P, B, NE])
        lexp = sb("lexp", [P, B, NE])
        lsum = sb("lsum", [P, B])
        lrec = sb("lrec", [P, B])
        prob = sb("prob", [P, B, NE])
        probE = sb("probE", [NE, NT])
        work = [sb(f"work{i}", [NE, CAP + NT]) for i in range(2)]
        sel_gt = sb("sel_gt", [NE, NT])
        sel_eq = sb("sel_eq", [NE, NT])
        n_gt = sb("n_gt", [NE, 1])
        room = sb("room", [NE, 1])
        tie_rank = sb("tie_rank", [NE, NT])
        sel = sb("sel", [NE, NT])
        ones_e = sb("ones_e", [NE, NT])
        assigned = sb("assigned", [P, B])
        free_tok = sb("free_tok", [P, B])
        m_sb = sb("m_sb", [P, B, NE])
        m1_sb = sb("m1_sb", [P, B, NE])
        pm_sb = sb("pm_sb", [P, B, NE])
        val_sb = sb("val_sb", [P, B, NE])
        vmax = sb("vmax", [P, B])
        veq = sb("veq", [P, B, NE])
        order_sb = sb("order_sb", [P, B, NE])
        code = sb("code", [P, B, NE])
        cmax = sb("cmax", [P, B])
        onehot = sb("onehot", [P, B, NE])
        gate = sb("gate", [P, B, NE])
        gelu_sb = sb("gelu_sb", [P, 4, FC, 2 * T])
        h_sb = kT_sb[:].rearrange("p (b x) (e d) -> p b (x e) d", b=B, d=D)
        y_sb = x_sb

        names = """ld_x ld_ctxk ld_wk ld_wv ld_wq ld_wo ld_attn ld_ffn1 ld_ffn2 stored
            consts_ident consts_done zero_done
            ln1_stats ln1_mv ln1_var ln1_rstd ln1_out ln1_T xnT_ready proj proj_act proj_dve
            scores maxes probs_done probs_T pt_act pt_dve pv rsums heads_done headsT_ps headsT_done
            attn_ps x1_done ln2_stats ln2_mv ln2_var ln2_rstd ln2_out x1b_done ln2_T xaT_done
            kq_ps k2_ps K_done tq_done tk_done Q_done Q2_done K2_done hb_done
            KV_done Kc_done KVc_done Kce_done Krec_done S_done Oar_done E0_done E_done K2E_done S2_done Oma_done O_done
            proj_ps x2_done ln3_stats ln3_mv ln3_var ln3_rstd ln3_out ln3_T xfT_done
            logits_ps lmax_done lsh_done lexp_done lsum_done lrec_done prob_done probE_ps probE_done
            top_step sel_done selT_ps route_step gates_done
            h1_ps gelu_done h2_ps h_act h_dve y_done
            ctx_squared w_squared ksum_done wsum_done bound_ps bound_step flag_ready
            g_room g_ctx g_staged g_qk_ps g_qk g_scores_ps g_masked g_max g_values g_exp g_turned g_turned_sb g_pv g_rec g_head""".split()
        s = {n: sem(n) for n in names}
        (ld_x, ld_ctxk, ld_wk, ld_wv, ld_wq, ld_wo, ld_attn, ld_ffn1, ld_ffn2, stored,
         consts_ident, consts_done, zero_done,
         ln1_stats, ln1_mv, ln1_var, ln1_rstd, ln1_out, ln1_T, xnT_ready, proj, proj_act, proj_dve,
         scores, maxes, probs_done, probs_T, pt_act, pt_dve, pv, rsums, heads_done, headsT_ps, headsT_done,
         attn_ps, x1_done, ln2_stats, ln2_mv, ln2_var, ln2_rstd, ln2_out, x1b_done, ln2_T, xaT_done,
         kq_ps, k2_ps, K_done, tq_done, tk_done, Q_done, Q2_done, K2_done, hb_done,
         KV_done, Kc_done, KVc_done, Kce_done, Krec_done, S_done, Oar_done, E0_done, E_done, K2E_done, S2_done, Oma_done, O_done,
         proj_ps, x2_done, ln3_stats, ln3_mv, ln3_var, ln3_rstd, ln3_out, ln3_T, xfT_done,
         logits_ps, lmax_done, lsh_done, lexp_done, lsum_done, lrec_done, prob_done, probE_ps, probE_done,
         top_step, sel_done, selT_ps, route_step, gates_done,
         h1_ps, gelu_done, h2_ps, h_act, h_dve, y_done,
         ctx_squared, w_squared, ksum_done, wsum_done, bound_ps, bound_step, flag_ready,
         g_room, g_ctx, g_staged, g_qk_ps, g_qk, g_scores_ps, g_masked, g_max, g_values, g_exp, g_turned, g_turned_sb,
         g_pv, g_rec, g_head) = [s[n] for n in names]
        ld_ctx = [sem(f"ld_ctx{i}") for i in range(GUARD_LOADS)]

        y_step = [sem(f"y_step{i}") for i in range(2)]
        N_PROJ = 3 * IC
        PROJ_V, PROJ_Q = IC, 2 * IC

        def unit(i):
            return i // 4, i // 2 % 2, i % 2

        SQ0 = 3
        POST_SLOT = (6, SETS + 2)

        def out_ps(g, q, n):
            return (score_ps[2 + n] if q == 0 else turn_ps[n])[:]

        def four(ap):
            return ap.rearrange("p (a b) -> p a b", a=4)

        def read_flag(eng):
            eng.wait_ge(flag_ready, 1)
            return eng.value_load(flag[0:1, 0:1], min_val=0, max_val=1)

        block = es.enter_context(nc.Block())

        @block.sync
        def _(sp):
            sp.dma_start(x_sb[:], x.rearrange("b t d -> t b d")).then_inc(ld_x, 16)
            sp.dma_start(wk_sb[:], w_k).then_inc(ld_wk, 16)
            sp.dma_start(wv_sb[:], w_v).then_inc(ld_wv, 16)
            sp.dma_start(wq_sb[:], w_q).then_inc(ld_wq, 16)
            guard_rows = ctx.rearrange("b k d -> (b k) d").rearrange("(p r) d -> p (r d)", p=P)
            w = GUARD_CHUNKS * GUARD_W // GUARD_LOADS
            for n in range(GUARD_LOADS):
                sp.dma_start(ctx_sb[:].rearrange("p a b -> p (a b)")[:, n * w:(n + 1) * w],
                             guard_rows[:, n * w:(n + 1) * w]).then_inc(ld_ctx[n], 16)
            sp.dma_start(wo_sb[:], w_o.rearrange("(c p) n -> p c n", p=P)).then_inc(ld_wo, 16)
            sp.dma_start(aw_sb[:], attn_w.rearrange("w i o -> i w o")).then_inc(ld_attn, 16)
            sp.dma_start(ab_sb[:], attn_b).then_inc(ld_attn, 16)
            sp.dma_start(bproj_sb[:], b_proj.partition_broadcast(P)).then_inc(ld_attn, 16)
            sp.dma_start(wg_sb[:], w_g).then_inc(ld_attn, 16)
            sp.dma_start(w1_sb[:], w_1.rearrange("e d f -> d e f")).then_inc(ld_ffn1, 16)
            sp.dma_start(w2_sb[:], w_2.rearrange("e (c p) d -> p e c d", p=P)).then_inc(ld_ffn2, 16)
            masked_keys_vanish = read_flag(sp)
            with sp.If(masked_keys_vanish == 0):
                with sp.Fori(0, B) as b:
                    sp.wait_ge(g_room, b * H + 1)
                    sp.dma_start(all_ctx, ctx_t[bass.ds(b, 1)].rearrange("b d k -> (b d) k")).then_inc(g_ctx, 16)
            sp.wait_ge(y_done, B)
            sp.dma_start(out.rearrange("b t d -> t b d"), y_sb[:]).then_inc(stored, 16)
            sp.wait_ge(stored, 16)

        @block.gpsimd
        def _(pool):
            nc.gpsimd.memset(ident[:], 0.0).then_inc(zero_done, 1)
            nc.gpsimd.memset(minus_half[:], -0.5).then_inc(zero_done, 1)
            nc.gpsimd.memset(ident_a[:], 0.0).then_inc(zero_done, 1)
            nc.gpsimd.memset(causal_b[:], 0.0).then_inc(zero_done, 1)
            pool.wait_ge(zero_done, 1)
            nc.gpsimd.affine_select(out=ident[:], in_=ident[:], compare_op=ALU.not_equal, fill=1.0, base=0,
                                    pattern=[[-1, P]], channel_multiplier=1).then_inc(consts_ident, 1)
            pool.wait_ge(ld_x, 16)

            def rsqrt(var_ready, n, of, to, done):
                pool.wait_ge(var_ready, n)
                nc.gpsimd.tensor_tensor(to, of, minus_half[:, 0:to.shape[1]], ALU.pow).then_inc(done, 1)

            pool.wait_ge(zero_done, 4)
            rsqrt(ln1_var, 1, mv[:, :, 1], rstd[:], ln1_rstd)
            nc.gpsimd.affine_select(out=ident_a[:], in_=ident_a[:], compare_op=ALU.not_equal, fill=MASK_A, base=0,
                                    pattern=[[-1, P]], channel_multiplier=1).then_inc(consts_done, 1)
            nc.gpsimd.affine_select(out=causal_b[:], in_=causal_b[:], compare_op=ALU.is_ge, fill=MASK_B, base=0,
                                    pattern=[[0, 4], [-1, P]], channel_multiplier=1).then_inc(consts_done, 1)
            nc.gpsimd.memset(ones[:], 1.0).then_inc(consts_done, 1)
            nc.gpsimd.memset(ones_e[:], 1.0).then_inc(consts_done, 1)
            nc.gpsimd.memset(v_sb[:, :, :, HD:HD + 1], 1.0).then_inc(consts_done, 1)
            for e in range(NE):
                nc.gpsimd.memset(order_sb[:, :, e:e + 1], float(NE - e)).then_inc(consts_done, 1)
            nc.gpsimd.memset(E_sb[:, :, 0:1], 0.0).then_inc(E0_done, 1)
            for n, (w, ready) in enumerate(((wk_sb, ld_wk), (wq_sb, ld_wq))):
                pool.wait_ge(ready, 16)
                nc.gpsimd.tensor_tensor(wsq_sb[:, n].rearrange("p h d -> p (h d)"), w[:], w[:], ALU.mult).then_inc(w_squared, 1)
            pool.wait_ge(ld_attn, 64)
            nc.gpsimd.tensor_scalar(hb_sb[:, 0:1], ab_sb[:, 1:2], 0.5, None, ALU.mult).then_inc(hb_done, 1)
            nc.gpsimd.tensor_scalar(hb_sb[:, 1:2], ab_sb[:, 2:3], 0.5 * K2_SCALE, None, ALU.mult).then_inc(hb_done, 1)

            for g, bs in enumerate(GROUPS):
                b0, n = bs[0], len(bs)
                bb = slice(b0, b0 + n)
                rsqrt(ln2_var, g + 1, mv2[:, bb, 1], rstd2[:, bb], ln2_rstd)
                bias = bproj_sb[:].unsqueeze(1).to_broadcast([P, n, D])
                nc.gpsimd.tensor_tensor(x1b_sb[:, bb], x1_sb[:, bb], bias, ALU.add).then_inc(x1b_done, 1)
                pool.wait_ge(tq_done, g + 1)
                nc.gpsimd.tensor_scalar(Q_sb[:, bb], tq_sb[:, bb], 0.5, 0.5, ALU.mult, ALU.add).then_inc(Q_done, 1)
                pool.wait_ge(tk_done, g + 1)
                nc.gpsimd.tensor_scalar(K2_sb[:, bb], tk_sb[:, bb], 0.5, 0.5, ALU.mult, ALU.add).then_inc(K2_done, 1)
                pool.wait_ge(Q_done, g + 1)
                nc.gpsimd.tensor_scalar(Q2_sb[:, bb], Q_sb[:, bb], LEAK / D ** 0.5, None, ALU.mult).then_inc(Q2_done, 1)
                rsqrt(ln3_var, g + 1, mv3[:, bb, 1], rstd3[:, bb], ln3_rstd)

        @block.scalar
        def _(act):
            act.dma_start(ctxk_sb[:], ctx_t[:, :, 0:T].rearrange("b d k -> d b k")).then_inc(ld_ctxk, 16)

            def square(c):
                if c % (GUARD_CHUNKS // GUARD_LOADS) == 0:
                    act.wait_ge(ld_ctx[c * GUARD_LOADS // GUARD_CHUNKS], 16)
                if c >= 2:
                    act.wait_ge(ctx_squared, c - 1)
                nc.scalar.activation(sq_sb[:, c % 2], ctx_sb[:, c], ACT.Square, accum_out=ksum[:, c:c + 1]).then_inc(ctx_squared, 1)

            for j in range(0, N_PROJ, 2):
                if SQ0 <= j // 2 < SQ0 + GUARD_CHUNKS // 2:
                    square(j - 2 * SQ0)
                    square(j - 2 * SQ0 + 1)
                act.wait_ge(proj, j + 1)
                src = score_ps[j % 4][:]
                if j < PROJ_V:
                    nc.scalar.activation(kT_sb[:, j, :], src, ACT.Copy).then_inc(proj_act, 1)
                elif j < PROJ_Q:
                    b, hf = (j - PROJ_V) // 2, (j - PROJ_V) % 2
                    nc.scalar.activation(v_sb[:, b, 8 * hf:8 * hf + 8, 0:HD],
                                         src.rearrange("p (h d) -> p h d", h=8), ACT.Copy).then_inc(proj_act, 1)
                else:
                    nc.scalar.activation(qT_sb[:, j - PROJ_Q, :], src, ACT.Copy, scale=QSCALE).then_inc(proj_act, 1)

            def exps(i):
                act.wait_ge(maxes, i + 1)
                if i >= 4:
                    act.wait_ge(probs_T, i - 3)
                for j in range(4):
                    a = nc.scalar.activation(probs[:, i % 4, j, :], score_ps[i % 4][:, j * T:(j + 1) * T], ACT.Exp,
                                             bias=negmax[:, i, j:j + 1])
                a.then_inc(probs_done, 1)

            def turned(i):
                act.wait_ge(probs_T, i + 1)
                if i >= 2:
                    act.wait_ge(pv, i - 1)
                nc.scalar.activation(probsT[:, i % 2].rearrange("p a b -> p (a b)"), turn_ps[i % 2][:],
                                     ACT.Copy).then_inc(pt_act, 1)

            def heads_turned(u):
                b, hf = u // 2, u % 2
                act.wait_ge(headsT_ps, u + 1)
                nc.scalar.activation(headsT[:, 4 * hf:4 * hf + 4, b, :], four(misc_ps[:]), ACT.Copy).then_inc(headsT_done, 1)

            def post_input(g):
                b0, n = GROUPS[g][0], len(GROUPS[g])
                bb = slice(b0, b0 + n)
                act.wait_ge(ln2_T, g + 1)
                nc.scalar.activation(xaT[:, bb], misc_ps[:, 0:n * T].rearrange("p (a b) -> p a b", a=n),
                                     ACT.Copy).then_inc(xaT_done, 1)

            def post_gates(g):
                b0, n = GROUPS[g][0], len(GROUPS[g])
                bb = slice(b0, b0 + n)
                act.wait_ge(kq_ps, g + 1)
                act.wait_ge(ld_attn, 64)
                nc.scalar.activation(K_sb[:, bb], misc_ps[:, 0:n * T].rearrange("p (a b) -> p a b", a=n),
                                     ACT.Exp, bias=ab_sb[:, 0:1]).then_inc(K_done, 1)
                act.wait_ge(hb_done, 2)
                nc.scalar.activation(tq_sb[:, bb], misc_ps[:, 256:256 + n * T].rearrange("p (a b) -> p a b", a=n),
                                     ACT.Tanh, bias=hb_sb[:, 0:1], scale=0.5).then_inc(tq_done, 1)
                act.wait_ge(k2_ps, g + 1)
                nc.scalar.activation(tk_sb[:, bb], misc_ps[:, 0:n * T].rearrange("p (a b) -> p a b", a=n),
                                     ACT.Tanh, bias=hb_sb[:, 1:2], scale=0.5 * K2_SCALE).then_inc(tk_done, 1)

            def post_router(g):
                b0, n = GROUPS[g][0], len(GROUPS[g])
                bb = slice(b0, b0 + n)
                act.wait_ge(ln3_T, g + 1)
                nc.scalar.activation(xfT[:, bb], misc_ps[:, 0:n * T].rearrange("p (a b) -> p a b", a=n),
                                     ACT.Copy).then_inc(xfT_done, 1)
                act.wait_ge(lsh_done, g + 1)
                nc.scalar.activation(lexp[:, bb], lsh[:, bb], ACT.Exp).then_inc(lexp_done, 1)

            def gelu(g, e):
                m = g * NE + e
                act.wait_ge(h1_ps, m + 1)
                if m >= 4:
                    act.wait_ge(h2_ps, m - 3)
                nc.scalar.activation(gelu_sb[:, m % 4].rearrange("p a b -> p (a b)"), score_ps[m % 2][:],
                                     ACT.Gelu).then_inc(gelu_done, 1)

            def expert_out(g, q):
                act.wait_ge(h2_ps, g * NE + 4 * q + 4)
                nc.scalar.activation(h_sb[:, GROUPS[g][0], 4 * q:4 * q + 4, :], four(out_ps(g, q, 0)),
                                     ACT.Copy).then_inc(h_act, 1)

            def general():
                with act.Fori(0, B * H) as t:
                    act.wait_ge(g_qk_ps, t + 1)
                    nc.scalar.activation(head_q, misc_ps[0:HD, 0:T], ACT.Copy, scale=QSCALE)
                    for c in range(4):
                        a = nc.scalar.activation(all_keys[:, c * 512:(c + 1) * 512], score_ps[c][0:HD, :], ACT.Copy)
                    a.then_inc(g_qk, 1)
                    act.wait_ge(g_max, t + 1)
                    nc.scalar.activation(all_probs, all_probs, ACT.Exp, bias=all_negmax[:], accum_out=all_sum[:, 0:1]).then_inc(g_exp, 1)
                act.wait_ge(g_head, B * H)
                nc.scalar.activation(spare[:], all_negmax[:], ACT.Copy).then_inc(probs_done, UNITS)

            def slots(attention):
                for sl in range(SETS + 5):
                    if attention and 1 <= sl <= SETS:
                        turned(2 * sl - 2)
                    if attention and sl < SETS:
                        exps(2 * sl)
                        exps(2 * sl + 1)
                    if 2 <= sl < SETS + 2:
                        heads_turned(sl - 2)
                    for g in range(NG):
                        if sl == POST_SLOT[g]:
                            post_input(g)
                        if sl == POST_SLOT[g] + 1:
                            post_gates(g)
                        if sl == POST_SLOT[g] + 2:
                            post_router(g)

            masked_keys_vanish = read_flag(act)
            with act.If(masked_keys_vanish == 0):
                general()
                slots(attention=False)
            with act.Else():
                slots(attention=True)
            for g in range(NG):
                for e in range(NE):
                    gelu(g, e)
                    if e in (3, 7):
                        expert_out(g, e // 4)

        @block.tensor
        def _(pe):
            pe.wait_ge(consts_ident, 1)
            misc_reader = []

            def take_misc(reader, count):
                if misc_reader:
                    pe.wait_ge(*misc_reader.pop())
                misc_reader.append((reader, count))

            def proj_bank(j):
                if j >= 4:
                    pe.wait_ge(proj_act if j % 2 == 0 else proj_dve, (j - 4) // 2 + 1)
                return score_ps[j % 4][:]

            pe.wait_ge(ld_ctxk, 16)
            pe.wait_ge(ld_wk, 16)
            for c in range(IC):
                nc.tensor.matmul(proj_bank(c), wk_sb[:, c * P:(c + 1) * P], ctxk_sb[:].rearrange("p b k -> p (b k)"),
                                 start=True, stop=True).then_inc(proj, 1)
            for b in range(B):
                pe.wait_ge(ln1_out, b + 1)
                t = nc.tensor.transpose(turn_ps[0][:, b * T:(b + 1) * T], xn_sb[:, b, :], ident[:])
            t.then_inc(ln1_T, 1)
            pe.wait_ge(ld_wv, 16)
            for b in range(B):
                for hf in range(2):
                    nc.tensor.matmul(proj_bank(PROJ_V + 2 * b + hf), ctxk_sb[:, b, :], wv_sb[:, hf * 512:(hf + 1) * 512],
                                     start=True, stop=True).then_inc(proj, 1)
            pe.wait_ge(ld_wq, 16)
            pe.wait_ge(xnT_ready, 1)
            for c in range(IC):
                nc.tensor.matmul(proj_bank(PROJ_Q + c), wq_sb[:, c * P:(c + 1) * P],
                                 xnT_sb[:].rearrange("p b k -> p (b k)"), start=True, stop=True).then_inc(proj, 1)

            pe.wait_ge(wsum_done, 1)
            pe.wait_ge(consts_done, 3)
            nc.tensor.matmul(misc_ps[0:1, 0:2 * H], ones[:, 0:1], wsum[:], start=True, stop=True)
            pe.wait_ge(ksum_done, 1)
            nc.tensor.matmul(misc_ps[0:1, P:2 * P], kmax[:], ident[:], start=True, stop=True).then_inc(bound_ps, 1)

            def general():
                pe.wait_ge(proj_act, N_PROJ // 2)
                pe.wait_ge(proj_dve, N_PROJ // 2)
                nc.tensor.transpose(turn_ps[0][:, 0:P], ident[:], ident[:]).then_inc(g_room, 1)
                with pe.Fori(0, B) as b:
                    with pe.Fori(0, H) as h:
                        t1 = b * H + h + 1
                        pe.wait_ge(g_ctx, b * 16 + 16)
                        pe.wait_ge(g_staged, t1)
                        nc.tensor.matmul(misc_ps[0:HD, 0:T], head_w[:, 0], batch_x, start=True, stop=True)
                        for c in range(4):
                            m = nc.tensor.matmul(score_ps[c][0:HD, :], head_w[:, 1], all_ctx[:, c * 512:(c + 1) * 512],
                                                 start=True, stop=True)
                        m.then_inc(g_qk_ps, 1)
                        for k in range(KB):
                            nc.tensor.matmul(turn_ps[k // 8][:, k % 8 * HD:(k % 8 + 1) * HD], all_ctx[:, k * P:(k + 1) * P],
                                             head_w[:, 2], start=True, stop=True)
                        pe.wait_ge(g_qk, t1)
                        for c in range(4):
                            m = nc.tensor.matmul(score_ps[c][:], head_q, all_keys[:, c * 512:(c + 1) * 512],
                                                 start=True, stop=True)
                        m.then_inc(g_scores_ps, 1)
                        pe.wait_ge(g_exp, t1)
                        for k in range(KB):
                            m = nc.tensor.transpose(score_ps[k // 4][:, k % 4 * T:(k % 4 + 1) * T],
                                                    all_probs[:, k * P:(k + 1) * P], ident[:])
                        m.then_inc(g_turned, 1)
                        pe.wait_ge(g_turned_sb, t1)
                        for k in range(KB):
                            m = nc.tensor.matmul(head_ps[:, 0:HD], all_probsT[:, k * T:(k + 1) * T],
                                                 all_values[:, k * HD:(k + 1) * HD], start=(k == 0), stop=(k == KB - 1))
                        m.then_inc(g_pv, 1)
                        nc.tensor.transpose(misc_ps[:, P:2 * P], ident[:], ident[:]).then_inc(g_room, 1)

            def score_set(u):
                b, hf = u // 2, u % 2
                if u == 0:
                    pe.wait_ge(consts_done, 5)
                if u < 2:
                    pe.wait_ge(proj_act, N_PROJ // 2)
                    pe.wait_ge(proj_dve, N_PROJ // 2)
                else:
                    pe.wait_ge(probs_done, 2 * u - 2)
                for par in range(2):
                    nc.tensor.matmul(score_ps[(2 * u + par) % 4][:], ident_a[:], causal_b[:].rearrange("p a b -> p (a b)"),
                                     start=True, stop=False, skip_group_check=True)
                for j in range(4):
                    for par in range(2):
                        r = slice(par * HD, (par + 1) * HD)
                        m = nc.tensor.matmul(score_ps[(2 * u + par) % 4][:, j * T:(j + 1) * T],
                                             qT_sb[r, 4 * hf + j, b * T:(b + 1) * T], kT_sb[r, 4 * hf + j, b * T:(b + 1) * T],
                                             start=False, stop=(j == 3), skip_group_check=True)
                        if j == 3:
                            m.then_inc(scores, 1)

            def turn_probs(i):
                pe.wait_ge(probs_done, i + 1)
                if i >= 2:
                    pe.wait_ge(pt_act if i % 2 == 0 else pt_dve, i // 2)
                for j in range(4):
                    t = nc.tensor.transpose(turn_ps[i % 2][:, j * T:(j + 1) * T], probs[:, i % 4, j, :], ident[:])
                t.then_inc(probs_T, 1)

            def weigh_values(i):
                b, hf, par = unit(i)
                pe.wait_ge(pt_act if i % 2 == 0 else pt_dve, i // 2 + 1)
                if i >= 1:
                    pe.wait_ge(heads_done, i)
                for j in range(4):
                    m = nc.tensor.matmul(head_ps[:, j * (HD + 1):(j + 1) * (HD + 1)], probsT[:, i % 2, j, :],
                                         v_sb[:, b, 8 * hf + 2 * j + par, :], start=True, stop=True)
                m.then_inc(pv, 1)

            def turn_heads(u):
                b, hf = u // 2, u % 2
                pe.wait_ge(heads_done, 2 * u + 2)
                take_misc(headsT_done, u + 1)
                for c in range(4):
                    t = nc.tensor.transpose(misc_ps[:, c * T:(c + 1) * T],
                                            heads[:, b, 8 * hf + 2 * c:8 * hf + 2 * c + 2, :].rearrange("p h d -> p (h d)"),
                                            ident[:])
                t.then_inc(headsT_ps, 1)

            def post_out(g):
                if g == 0:
                    pe.wait_ge(ld_wo, 16)
                take_misc(x1_done, g + 1)
                for n, b in enumerate(GROUPS[g]):
                    for c in range(IC):
                        m = nc.tensor.matmul(misc_ps[:, n * D:(n + 1) * D], headsT[:, c, b, :], wo_sb[:, c, :],
                                             start=(c == 0), stop=(c == IC - 1))
                m.then_inc(attn_ps, 1)

            def post_turn(g, ready, rows, done, reader):
                pe.wait_ge(ready, GROUPS[g][-1] + 1)
                take_misc(reader, g + 1)
                for n, b in enumerate(GROUPS[g]):
                    t = nc.tensor.transpose(misc_ps[:, n * T:(n + 1) * T], rows[:, b, :], ident[:])
                t.then_inc(done, 1)

            def post_gates(g):
                n = len(GROUPS[g])
                rhs = xaT[:, GROUPS[g][0]:GROUPS[g][0] + n].rearrange("p b t -> p (b t)")
                if g == 0:
                    pe.wait_ge(ld_attn, 64)
                take_misc(tq_done, g + 1)
                nc.tensor.matmul(misc_ps[:, 0:n * T], aw_sb[:, 0, :], rhs, start=True, stop=True)
                nc.tensor.matmul(misc_ps[:, 256:256 + n * T], aw_sb[:, 1, :], rhs, start=True, stop=True).then_inc(kq_ps, 1)
                take_misc(tk_done, g + 1)
                nc.tensor.matmul(misc_ps[:, 0:n * T], aw_sb[:, 2, :], rhs, start=True, stop=True).then_inc(k2_ps, 1)

            def post_proj(g):
                pe.wait_ge(O_done, g + 1)
                take_misc(x2_done, g + 1)
                for n, b in enumerate(GROUPS[g]):
                    m = nc.tensor.matmul(misc_ps[:, n * D:(n + 1) * D], Oar_sb[:, b, :], aw_sb[:, 3, :],
                                         start=True, stop=True)
                m.then_inc(proj_ps, 1)

            def post_logits(g):
                take_misc(lsh_done, g + 1)
                for n, b in enumerate(GROUPS[g]):
                    m = nc.tensor.matmul(misc_ps[:, n * NE:(n + 1) * NE], xfT[:, b, :], wg_sb[:], start=True, stop=True)
                m.then_inc(logits_ps, 1)

            def post_probs(g):
                pe.wait_ge(prob_done, g + 1)
                take_misc(probE_done, g + 1)
                for n, b in enumerate(GROUPS[g]):
                    t = nc.tensor.transpose(misc_ps[0:NE, n * T:(n + 1) * T], prob[:, b, :], ident[:])
                t.then_inc(probE_ps, 1)

            def hidden(g, e):
                m = g * NE + e
                n = len(GROUPS[g])
                if m == 0:
                    pe.wait_ge(ld_ffn1, 16)
                    pe.wait_ge(probs_done, UNITS)
                if m >= 2:
                    pe.wait_ge(gelu_done, m - 1)
                for f in range(FC):
                    mm = nc.tensor.matmul(score_ps[m % 2][:, f * n * T:(f + 1) * n * T], w1_sb[:, e, f * P:(f + 1) * P],
                                          xfT[:, GROUPS[g][0]:GROUPS[g][0] + n].rearrange("p b t -> p (b t)"),
                                          start=True, stop=True)
                mm.then_inc(h1_ps, 1)

            def answer(g, e):
                m = g * NE + e
                pe.wait_ge(gelu_done, m + 1)
                if m == 0:
                    pe.wait_ge(ld_ffn2, 16)
                if m == 4:
                    pe.wait_ge(heads_done, UNITS)
                if e == 0 and g >= 1:
                    pe.wait_ge(h_act, 2 * g - 1)
                    pe.wait_ge(h_dve, 2 * g - 1)
                if e == 4 and g >= 1:
                    pe.wait_ge(h_act, 2 * g)
                    pe.wait_ge(h_dve, 2 * g)
                for n in range(len(GROUPS[g])):
                    for f in range(FC):
                        mm = nc.tensor.matmul(out_ps(g, e // 4, n)[:, e % 4 * D:(e % 4 + 1) * D],
                                              gelu_sb[:, m % 4, f, n * T:(n + 1) * T], w2_sb[:, e, f, :],
                                              start=(f == 0), stop=(f == FC - 1))
                mm.then_inc(h2_ps, 1)

            def slots(attention):
                for sl in range(SETS + 5):
                    if attention and sl < SETS:
                        score_set(sl)
                    if attention and 1 <= sl <= SETS:
                        turn_probs(2 * sl - 2)
                        if sl > 1:
                            weigh_values(2 * sl - 3)
                        turn_probs(2 * sl - 1)
                        weigh_values(2 * sl - 2)
                    if attention and sl == SETS + 1:
                        weigh_values(UNITS - 1)
                    if 2 <= sl < SETS + 2:
                        turn_heads(sl - 2)
                    for g in range(NG):
                        if sl == POST_SLOT[g]:
                            post_out(g)
                            post_turn(g, ln2_out, xa_sb, ln2_T, xaT_done)
                        if sl == POST_SLOT[g] + 1:
                            post_gates(g)
                            post_proj(g)
                        if sl == POST_SLOT[g] + 2:
                            post_turn(g, ln3_out, xf_sb, ln3_T, xfT_done)
                            post_logits(g)
                            post_probs(g)

            masked_keys_vanish = read_flag(pe)
            with pe.If(masked_keys_vanish == 0):
                general()
                slots(attention=False)
            misc_reader.clear()
            with pe.Else():
                slots(attention=True)
            for g in range(NG):
                hidden(g, 0)
                for e in range(NE):
                    if e + 1 < NE:
                        hidden(g, e + 1)
                    answer(g, e)
            pe.wait_ge(sel_done, 1)
            take_misc(route_step, 3)
            for b in range(B):
                t = nc.tensor.transpose(misc_ps[:, b * NE:(b + 1) * NE], sel[:, b * T:(b + 1) * T], ident[0:NE, 0:NE])
            t.then_inc(selT_ps, 1)

        @block.vector
        def _(dve):
            def layer_norm(b0, n, rows, st, m, r, y, stats_done, mv_done, var_done, rstd_done, out_done, g):
                for b in range(b0, b0 + n):
                    nc.vector.bn_stats(st[:, b, :], rows[:, b, :]).then_inc(stats_done, 1)
                for b in range(b0, b0 + n):
                    dve.wait_ge(stats_done, b + 1)
                    nc.vector.bn_aggr(m[:, b, :], st[:, b, :]).then_inc(mv_done, 1)
                dve.wait_ge(mv_done, b0 + n)
                nc.vector.tensor_scalar(m[:, b0:b0 + n, 1], m[:, b0:b0 + n, 1], EPS_LN, None, ALU.add).then_inc(var_done, 1)
                dve.wait_ge(rstd_done, g + 1)
                dve.wait_ge(var_done, g + 1)
                for b in range(b0, b0 + n):
                    nc.vector.tensor_scalar(y[:, b, :], rows[:, b, :], m[:, b, 0:1], r[:, b:b + 1],
                                            ALU.subtract, ALU.mult).then_inc(out_done, 1)

            dve.wait_ge(ld_x, 16)
            layer_norm(0, B, x_sb, stats, mv, rstd, xn_sb, ln1_stats, ln1_mv, ln1_var, ln1_rstd, ln1_out, 0)

            for j in range(1, N_PROJ, 2):
                if j == PROJ_V + 1:
                    dve.wait_ge(ln1_T, 1)
                    nc.vector.tensor_copy(xnT_sb[:], four(turn_ps[0][:])).then_inc(xnT_ready, 1)
                dve.wait_ge(proj, j + 1)
                src = score_ps[j % 4][:]
                if j < PROJ_V:
                    nc.vector.tensor_copy(kT_sb[:, j, :], src).then_inc(proj_dve, 1)
                elif j < PROJ_Q:
                    b, hf = (j - PROJ_V) // 2, (j - PROJ_V) % 2
                    nc.vector.tensor_copy(v_sb[:, b, 8 * hf:8 * hf + 8, 0:HD],
                                          src.rearrange("p (h d) -> p h d", h=8)).then_inc(proj_dve, 1)
                else:
                    nc.vector.tensor_scalar(qT_sb[:, j - PROJ_Q, :], src, QSCALE, None, ALU.mult).then_inc(proj_dve, 1)

            dve.wait_ge(w_squared, 2)
            nc.vector.tensor_reduce(wsum[:], wsq_sb.rearrange("p w h d -> p (w h) d"), AX_X, ALU.add).then_inc(wsum_done, 1)
            dve.wait_ge(ctx_squared, GUARD_CHUNKS)
            nc.vector.tensor_reduce(kmax[:], ksum[:], AX_X, ALU.max).then_inc(ksum_done, 1)
            dve.wait_ge(bound_ps, 1)
            nc.vector.tensor_copy(bound[:, 0:H], misc_ps[0:1, 0:H]).then_inc(bound_step, 1)
            nc.vector.tensor_reduce(bound[:, 2 * H:2 * H + 1], misc_ps[0:1, P:2 * P], AX_X, ALU.max).then_inc(bound_step, 1)
            dve.wait_ge(bound_step, 2)
            nc.vector.tensor_tensor(bound[:, H:2 * H], misc_ps[0:1, H:2 * H], bound[:, 0:H], ALU.mult).then_inc(bound_step, 1)
            dve.wait_ge(bound_step, 3)
            nc.vector.tensor_reduce(bound[:, 2 * H + 1:2 * H + 2], bound[:, H:2 * H], AX_X, ALU.max).then_inc(bound_step, 1)
            dve.wait_ge(bound_step, 4)
            nc.vector.tensor_tensor(bound[:, 2 * H + 2:2 * H + 3], bound[:, 2 * H:2 * H + 1], bound[:, 2 * H + 1:2 * H + 2],
                                    ALU.mult).then_inc(bound_step, 1)
            dve.wait_ge(bound_step, 5)
            nc.vector.tensor_scalar(flag[:], bound[:, 2 * H + 2:2 * H + 3], GUARD_LIMIT, None, ALU.is_lt).then_inc(flag_ready, 1)

            def general():
                with dve.Fori(0, B) as b:
                    with dve.Fori(0, H) as h:
                        t1 = b * H + h + 1
                        dve.wait_ge(g_room, t1)
                        for n, w in enumerate((wq_sb, wk_sb, wv_sb)):
                            nc.vector.tensor_copy(head_w[:, n], w[:, bass.ds(h * HD, HD)])
                        nc.vector.tensor_copy(batch_x, xnT_sb[:].rearrange("p b t -> p (b t)")[:, bass.ds(b * T, T)]).then_inc(g_staged, 1)
                        dve.wait_ge(g_scores_ps, t1)
                        nc.vector.scalar_tensor_tensor(all_probs[:, 0:T], causal_b[:, 0, :], MASK_A, score_ps[0][:, 0:T],
                                                       ALU.mult, ALU.add)
                        nc.vector.tensor_scalar(all_probs[:, T:512], score_ps[0][:, T:512], MASK_A * MASK_B, None, ALU.add)
                        for c in range(1, 4):
                            m = nc.vector.tensor_scalar(all_probs[:, c * 512:(c + 1) * 512], score_ps[c][:], MASK_A * MASK_B,
                                                        None, ALU.add)
                        m.then_inc(g_masked, 1)
                        dve.wait_ge(g_masked, t1)
                        nc.vector.tensor_reduce(all_negmax[:], all_probs, AX_X, ALU.max, negate=True).then_inc(g_max, 1)
                        for c in range(2):
                            m = nc.vector.tensor_copy(all_values[:, c * 512:(c + 1) * 512], turn_ps[c][:])
                        m.then_inc(g_values, 1)
                        dve.wait_ge(g_turned, t1)
                        for c in range(4):
                            m = nc.vector.tensor_copy(all_probsT[:, c * 512:(c + 1) * 512], score_ps[c][:])
                        m.then_inc(g_turned_sb, 1)
                        nc.vector.reciprocal(all_sum[:, 1:2], all_sum[:, 0:1]).then_inc(g_rec, 1)
                        dve.wait_ge(g_rec, t1)
                        dve.wait_ge(g_pv, t1)
                        nc.vector.tensor_scalar(heads_flat[:, bass.ds((b * H + h) * HD, HD)], head_ps[:, 0:HD], all_sum[:, 1:2],
                                                None, ALU.mult).then_inc(g_head, 1)
                dve.wait_ge(g_head, B * H)
                nc.vector.tensor_copy(all_sum[:, 0:1], all_sum[:, 1:2]).then_inc(heads_done, UNITS)

            def row_max(i):
                dve.wait_ge(scores, i + 1)
                nc.vector.tensor_reduce(negmax[:, i, :], four(score_ps[i % 4][:]), AX_X, ALU.max,
                                        negate=True).then_inc(maxes, 1)

            def turned(i):
                dve.wait_ge(probs_T, i + 1)
                if i >= 2:
                    dve.wait_ge(pv, i - 1)
                nc.vector.tensor_copy(probsT[:, i % 2], four(turn_ps[i % 2][:])).then_inc(pt_dve, 1)

            def norm_heads(i):
                b, hf, par = unit(i)
                got = head_ps[:, 0:4 * (HD + 1)].rearrange("p (j d) -> p j d", j=4)
                dve.wait_ge(pv, i + 1)
                nc.vector.reciprocal(rsum[:, i, :], got[:, :, HD]).then_inc(rsums, 1)
                dve.wait_ge(rsums, i + 1)
                to = heads[:, b, 8 * hf:8 * hf + 8, :].rearrange("p (j q) d -> p j q d", q=2)[:, :, par, :]
                nc.vector.tensor_tensor(to, got[:, :, 0:HD], rsum[:, i, :].unsqueeze(2).to_broadcast([P, 4, HD]),
                                        ALU.mult).then_inc(heads_done, 1)

            def post_x1(g):
                b0, n = GROUPS[g][0], len(GROUPS[g])
                dve.wait_ge(attn_ps, g + 1)
                nc.vector.tensor_tensor(x1_sb[:, b0:b0 + n], x_sb[:, b0:b0 + n],
                                        misc_ps[:, 0:n * D].rearrange("p (a b) -> p a b", a=n), ALU.add).then_inc(x1_done, 1)
                dve.wait_ge(x1_done, g + 1)
                layer_norm(b0, n, x1_sb, stats2, mv2, rstd2, xa_sb, ln2_stats, ln2_mv, ln2_var, ln2_rstd, ln2_out, g)

            def post_gates(g):
                bs = GROUPS[g]
                b0, n = bs[0], len(bs)
                bb = slice(b0, b0 + n)
                one = ones[:]
                dve.wait_ge(K_done, g + 1)
                if g == 0:
                    dve.wait_ge(consts_done, 3)
                for b in bs:
                    nc.vector.tensor_tensor_scan(Kc_sb[:, b, :], one, K_sb[:, b, :], 0.0, ALU.mult, ALU.add).then_inc(Kc_done, 1)
                dve.wait_ge(xaT_done, g + 1)
                nc.vector.tensor_tensor(KV_sb[:, bb], K_sb[:, bb], xaT[:, bb], ALU.mult).then_inc(KV_done, 1)
                dve.wait_ge(Kc_done, b0 + n)
                nc.vector.tensor_scalar(Kc_sb[:, bb], Kc_sb[:, bb], EPS_CUM, None, ALU.add).then_inc(Kce_done, 1)
                dve.wait_ge(KV_done, g + 1)
                for b in bs:
                    nc.vector.tensor_tensor_scan(KVc_sb[:, b, :], one, KV_sb[:, b, :], 0.0, ALU.mult, ALU.add).then_inc(KVc_done, 1)
                dve.wait_ge(Kce_done, g + 1)
                nc.vector.reciprocal(Kc_sb[:, bb], Kc_sb[:, bb]).then_inc(Krec_done, 1)
                dve.wait_ge(Krec_done, g + 1)
                dve.wait_ge(KVc_done, b0 + n)
                nc.vector.tensor_tensor(S_sb[:, bb], KVc_sb[:, bb], Kc_sb[:, bb], ALU.mult).then_inc(S_done, 1)
                dve.wait_ge(S_done, g + 1)
                dve.wait_ge(Q_done, g + 1)
                nc.vector.tensor_tensor(Oar_sb[:, bb], S_sb[:, bb], Q_sb[:, bb], ALU.mult).then_inc(Oar_done, 1)
                dve.wait_ge(Oar_done, g + 1)
                dve.wait_ge(E0_done, 1)
                nc.vector.tensor_tensor(E_sb[:, bb, 1:T], xaT[:, bb, 1:T], Oar_sb[:, bb, 0:T - 1],
                                        ALU.subtract).then_inc(E_done, 1)
                dve.wait_ge(E_done, g + 1)
                dve.wait_ge(K2_done, g + 1)
                nc.vector.tensor_tensor(E_sb[:, bb, 1:T], E_sb[:, bb, 1:T], K2_sb[:, bb, 0:T - 1],
                                        ALU.mult).then_inc(K2E_done, 1)
                dve.wait_ge(K2E_done, g + 1)
                for b in bs:
                    nc.vector.tensor_tensor_scan(S2_sb[:, b, :], one, E_sb[:, b, :], 0.0, ALU.mult, ALU.add).then_inc(S2_done, 1)
                dve.wait_ge(S2_done, b0 + n)
                dve.wait_ge(Q2_done, g + 1)
                nc.vector.tensor_tensor(Oma_sb[:, bb, 1:T], S2_sb[:, bb, 1:T], Q2_sb[:, bb, 0:T - 1],
                                        ALU.mult).then_inc(Oma_done, 1)
                dve.wait_ge(Oma_done, g + 1)
                nc.vector.tensor_tensor(Oar_sb[:, bb, 1:T], Oar_sb[:, bb, 1:T], Oma_sb[:, bb, 1:T],
                                        ALU.add).then_inc(O_done, 1)

            def post_x2(g):
                b0, n = GROUPS[g][0], len(GROUPS[g])
                dve.wait_ge(proj_ps, g + 1)
                dve.wait_ge(x1b_done, g + 1)
                nc.vector.tensor_tensor(x2_sb[:, b0:b0 + n], x1b_sb[:, b0:b0 + n],
                                        misc_ps[:, 0:n * D].rearrange("p (a b) -> p a b", a=n), ALU.add).then_inc(x2_done, 1)
                dve.wait_ge(x2_done, g + 1)
                layer_norm(b0, n, x2_sb, stats3, mv3, rstd3, xf_sb, ln3_stats, ln3_mv, ln3_var, ln3_rstd, ln3_out, g)

            def post_router(g):
                b0, n = GROUPS[g][0], len(GROUPS[g])
                bb = slice(b0, b0 + n)
                logits = misc_ps[:, 0:n * NE].rearrange("p (b e) -> p b e", b=n)
                dve.wait_ge(logits_ps, g + 1)
                nc.vector.tensor_reduce(lmax[:, bb], logits, AX_X, ALU.max).then_inc(lmax_done, 1)
                dve.wait_ge(lmax_done, g + 1)
                nc.vector.tensor_tensor(lsh[:, bb], logits, lmax[:, bb].unsqueeze(2).to_broadcast([P, n, NE]),
                                        ALU.subtract).then_inc(lsh_done, 1)
                dve.wait_ge(lexp_done, g + 1)
                nc.vector.tensor_reduce(lsum[:, bb], lexp[:, bb], AX_X, ALU.add).then_inc(lsum_done, 1)
                dve.wait_ge(lsum_done, g + 1)
                nc.vector.reciprocal(lrec[:, bb], lsum[:, bb]).then_inc(lrec_done, 1)
                dve.wait_ge(lrec_done, g + 1)
                nc.vector.tensor_tensor(prob[:, bb], lexp[:, bb], lrec[:, bb].unsqueeze(2).to_broadcast([P, n, NE]),
                                        ALU.mult).then_inc(prob_done, 1)
                dve.wait_ge(probE_ps, g + 1)
                nc.vector.tensor_copy(probE[:, b0 * T:(b0 + n) * T], misc_ps[0:NE, 0:n * T]).then_inc(probE_done, 1)

            tops = [0]

            def top_tokens(g):
                b0, n = GROUPS[g][0], len(GROUPS[g])
                w = n * T
                new = probE[:, b0 * T:(b0 + n) * T]
                cur = work[g % 2]
                old = CAP if g else 0
                dve.wait_ge(probE_done, g + 1)
                nxt = work[(g + 1) % 2]
                nc.vector.tensor_copy(cur[:, CAP:CAP + w], new).then_inc(top_step, 1)
                tops[0] += 1
                lo = CAP - old
                for r in range(CAP // 8):
                    dve.wait_ge(top_step, tops[0])
                    nc.vector.max(nxt[:, 8 * r:8 * r + 8], cur[:, lo:CAP + w]).then_inc(top_step, 1)
                    tops[0] += 1
                    if r + 1 < CAP // 8:
                        dve.wait_ge(top_step, tops[0])
                        nc.vector.match_replace(out=cur[:, lo:CAP + w], in_to_replace=nxt[:, 8 * r:8 * r + 8],
                                                in_values=cur[:, lo:CAP + w], imm_value=-1.0).then_inc(top_step, 1)
                        tops[0] += 1
                return nxt[:, CAP - 1:CAP]

            def choose(least):
                dve.wait_ge(top_step, tops[0])
                nc.vector.tensor_scalar(sel_gt[:], probE[:], least, 0.0, ALU.is_gt, ALU.add, accum_out=n_gt[:]).then_inc(top_step, 1)
                nc.vector.tensor_scalar(sel_eq[:], probE[:], least, None, ALU.is_equal).then_inc(top_step, 1)
                tops[0] += 2
                dve.wait_ge(top_step, tops[0])
                nc.vector.tensor_scalar(room[:], n_gt[:], -1.0, float(CAP), ALU.mult, ALU.add).then_inc(top_step, 1)
                dve.wait_ge(consts_done, 4)
                nc.vector.tensor_tensor_scan(tie_rank[:], ones_e[:], sel_eq[:], 0.0, ALU.mult, ALU.add).then_inc(top_step, 1)
                tops[0] += 2
                dve.wait_ge(top_step, tops[0])
                nc.vector.scalar_tensor_tensor(tie_rank[:], tie_rank[:], room[:], sel_eq[:], ALU.is_le,
                                               ALU.mult).then_inc(top_step, 1)
                tops[0] += 1
                dve.wait_ge(top_step, tops[0])
                nc.vector.tensor_tensor(sel[:], sel_gt[:], tie_rank[:], ALU.add).then_inc(sel_done, 1)

            def gates():
                picked = misc_ps[:, 0:B * NE].rearrange("p (b e) -> p b e", b=B)
                steps = [0]

                def done(ins):
                    ins.then_inc(route_step, 1)
                    steps[0] += 1

                def wait():
                    dve.wait_ge(route_step, steps[0])

                def wide(ap):
                    return ap.unsqueeze(2).to_broadcast([P, B, NE])

                dve.wait_ge(selT_ps, 1)
                done(nc.vector.tensor_reduce(assigned[:], picked, AX_X, ALU.max))
                wait()
                done(nc.vector.tensor_scalar(free_tok[:], assigned[:], -1.0, 1.0, ALU.mult, ALU.add))
                wait()
                done(nc.vector.tensor_tensor(m_sb[:], picked, wide(free_tok[:]), ALU.max))
                wait()
                done(nc.vector.tensor_scalar(m1_sb[:], m_sb[:], -1.0, None, ALU.add))
                done(nc.vector.tensor_tensor(pm_sb[:], prob[:], m_sb[:], ALU.mult))
                wait()
                done(nc.vector.tensor_tensor(val_sb[:], pm_sb[:], m1_sb[:], ALU.add))
                wait()
                done(nc.vector.tensor_reduce(vmax[:], val_sb[:], AX_X, ALU.max))
                wait()
                done(nc.vector.tensor_tensor(veq[:], val_sb[:], wide(vmax[:]), ALU.is_equal))
                wait()
                dve.wait_ge(consts_done, 5 + NE)
                done(nc.vector.tensor_tensor(code[:], veq[:], order_sb[:], ALU.mult))
                wait()
                done(nc.vector.tensor_reduce(cmax[:], code[:], AX_X, ALU.max))
                wait()
                done(nc.vector.tensor_tensor(onehot[:], code[:], wide(cmax[:]), ALU.is_equal))
                wait()
                nc.vector.tensor_tensor(gate[:], onehot[:], wide(vmax[:]), ALU.mult).then_inc(gates_done, 1)

            def expert_out(g, q):
                dve.wait_ge(h2_ps, g * NE + 4 * q + 4)
                nc.vector.tensor_copy(h_sb[:, GROUPS[g][1], 4 * q:4 * q + 4, :], four(out_ps(g, q, 1))).then_inc(h_dve, 1)

            def slots(attention):
                for sl in range(SETS + 5):
                    if attention and sl < SETS:
                        row_max(2 * sl)
                        row_max(2 * sl + 1)
                    if attention and 1 <= sl <= SETS:
                        if sl > 1:
                            norm_heads(2 * sl - 3)
                        turned(2 * sl - 1)
                        norm_heads(2 * sl - 2)
                    if attention and sl == SETS + 1:
                        norm_heads(UNITS - 1)
                    for g in range(NG):
                        if sl == POST_SLOT[g]:
                            post_x1(g)
                        if sl == POST_SLOT[g] + 1:
                            post_gates(g)
                            post_x2(g)
                        if sl == POST_SLOT[g] + 2:
                            post_router(g)

            masked_keys_vanish = read_flag(dve)
            with dve.If(masked_keys_vanish == 0):
                general()
                slots(attention=False)
            with dve.Else():
                slots(attention=True)
            for g in range(NG):
                if g + 1 == NG:
                    least = top_tokens(g)
                    choose(least)
                else:
                    top_tokens(g)
                expert_out(g, 0)
                expert_out(g, 1)
            gates()
            dve.wait_ge(gates_done, 1)
            dve.wait_ge(h_act, 2 * NG)
            for b in range(B):
                for e in range(NE):
                    src = x2_sb if e == 0 else y_sb
                    if e:
                        dve.wait_ge(y_step[b % 2], b // 2 * (NE - 1) + e)
                    ins = nc.vector.scalar_tensor_tensor(y_sb[:, b, :], h_sb[:, b, e, :], gate[:, b, e:e + 1], src[:, b, :],
                                                         ALU.mult, ALU.add)
                    ins.then_inc(y_done if e == NE - 1 else y_step[b % 2], 1)


_INS = ["x", "ctx", "ctx_t", "w_q", "w_k", "w_v", "w_o", "attn_w", "attn_b", "b_proj", "w_g", "w_1", "w_2"]


def kernel(x, ctx_1024, L0_xattn_w_q, L0_xattn_w_k, L0_xattn_w_v, L0_xattn_w_o, L0_attn_Wq1, L0_attn_bq1,
           L0_attn_Wk1, L0_attn_bk1, L0_attn_Wk2, L0_attn_bk2, L0_attn_Wproj, L0_attn_bproj,
           L0_ffn_Wg, L0_ffn_W1, L0_ffn_W2):
    import numpy as np
    import concourse.bacc as bacc
    from concourse.bass_utils import run_bass_kernel_spmd

    def lay(a):
        return np.ascontiguousarray(np.asarray(a))

    ctx = lay(ctx_1024)
    arrays = {
        "x": lay(x),
        "ctx": ctx,
        "ctx_t": lay(ctx.transpose(0, 2, 1)),
        "w_q": lay(L0_xattn_w_q),
        "w_k": lay(L0_xattn_w_k),
        "w_v": lay(L0_xattn_w_v),
        "w_o": lay(L0_xattn_w_o),
        "attn_w": lay(np.stack([np.asarray(w).T for w in (L0_attn_Wk1, L0_attn_Wq1, L0_attn_Wk2, L0_attn_Wproj)])),
        "attn_b": lay(np.stack([np.asarray(v) for v in (L0_attn_bk1, L0_attn_bq1, L0_attn_bk2)], axis=1)),
        "b_proj": lay(L0_attn_bproj),
        "w_g": lay(L0_ffn_Wg),
        "w_1": lay(L0_ffn_W1),
        "w_2": lay(L0_ffn_W2),
    }
    nc = bacc.Bacc("TRN2", target_bir_lowering=False, num_devices=1)
    args = [nc.dram_tensor(f"in_{n}", arrays[n].shape, mybir.dt.from_np(arrays[n].dtype), kind="ExternalInput").ap()
            for n in _INS]
    out = nc.dram_tensor("out", arrays["x"].shape, F32, kind="ExternalOutput").ap()
    perceiver_layer(nc, *args, out)
    r = run_bass_kernel_spmd(nc, [{f"in_{n}": arrays[n] for n in _INS}], core_ids=[0])
    return r.results[0]["out"]
```

```python
from contextlib import ExitStack

import concourse.bass as bass
from concourse import mybir

ALU = mybir.AluOpType
ACT = mybir.ActivationFunctionType
F32 = mybir.dt.float32
BF16 = mybir.dt.bfloat16
I32 = mybir.dt.int32
AX_X = mybir.AxisListType.X

P = 128
EPS_LN = 1e-5
EPS_CUM = 1e-6
LEAK = 0.02
MASK_A, MASK_B = 100.0, -100.0
SCORE_LIMIT = 4900.0


def perceiver_layer(nc, x, ctx, ctx_t, w_q, w_k, w_v, w_o, attn_w, attn_b, b_proj, w_g, w_1, w_2, out):
    B, T, D = x.shape
    KEYS = ctx.shape[1]
    INNER = w_q.shape[1]
    HD = 64
    H = INNER // HD
    NE, _, FF = w_1.shape
    FC = FF // P
    NT = B * T
    CAP = NT // NE
    IC = INNER // P
    KB = KEYS // P
    assert T == P and D == P and B == 4 and H == 16
    QSCALE = HD ** -0.5
    K2_SCALE = LEAK / D ** 0.5
    GROUPS = ((0, 1), (2, 3))
    NG = len(GROUPS)
    SETS = 2 * B
    UNITS = 2 * SETS
    GUARD_CHUNKS = 16
    GUARD_W = B * KEYS // P // GUARD_CHUNKS * D
    GUARD_LOADS = 4
    GUARD_LIMIT = SCORE_LIMIT ** 2 / (D * QSCALE ** 2)

    with ExitStack() as es:
        def sb(name, shape, dt=F32):
            return es.enter_context(nc.sbuf_tensor(name, shape, dt))

        def sem(name):
            return es.enter_context(nc.semaphore(name))

        score_ps = [es.enter_context(nc.psum_tensor(f"score_ps{i}", [P, 512], F32)) for i in range(4)]
        turn_ps = [es.enter_context(nc.psum_tensor(f"turn_ps{i}", [P, 512], F32)) for i in range(2)]
        head_ps = es.enter_context(nc.psum_tensor("head_ps", [P, 512], F32))
        misc_ps = es.enter_context(nc.psum_tensor("misc_ps", [P, 512], F32))

        x_sb = sb("x_sb", [P, B, D])
        ctxk_sb = sb("ctxk_sb", [P, B, T])
        ctx_sb = sb("ctx_sb", [P, GUARD_CHUNKS, GUARD_W])
        sq_sb = sb("sq_sb", [P, 2, GUARD_W])
        wq_sb = sb("wq_sb", [P, INNER])
        wk_sb = sb("wk_sb", [P, INNER])
        wv_sb = sb("wv_sb", [P, INNER])
        wo_sb = sb("wo_sb", [P, IC, D])
        aw_sb = sb("aw_sb", [P, 4, D])
        ab_sb = sb("ab_sb", [P, 3])
        bproj_sb = sb("bproj_sb", [P, D])
        wg_sb = sb("wg_sb", [P, NE])
        w1_sb = sb("w1_sb", [P, NE, FF])
        w2_sb = sb("w2_sb", [P, NE, FC, D])

        ident = sb("ident", [P, P])
        ident_a = sb("ident_a", [P, P], BF16)
        causal_b = sb("causal_b", [P, 4, P], BF16)
        ones = sb("ones", [P, P])
        minus_half = sb("minus_half", [P, 4])

        stats = sb("stats", [P, B, 6])
        mv = sb("mv", [P, B, 2])
        rstd = sb("rstd", [P, B])
        xn_sb = sb("xn_sb", [P, B, D])
        xnT_sb = sb("xnT_sb", [P, B, T])
        kT_sb = sb("kT_sb", [P, IC, NT])
        qT_sb = sb("qT_sb", [P, IC, NT])
        v_sb = sb("v_sb", [P, B, H, HD + 1])

        negmax = sb("negmax", [P, UNITS, 4])
        probs = sb("probs", [P, 4, 4, T])
        probsT = sb("probsT", [P, 2, 4, T])
        rsum = sb("rsum", [P, UNITS, 4])
        wsq_sb = probs[:].rearrange("p a b c -> p (a b c)").rearrange("p (w h d) -> p w h d", w=2, h=H)
        ksum = sb("ksum", [P, GUARD_CHUNKS])
        kmax = sb("kmax", [P, 1])
        wsum = sb("wsum", [P, 2 * H])
        bound = sb("bound", [1, 2 * H + 3])
        flag = sb("flag", [1, 1], I32)
        gone = ctx_sb[:].rearrange("p a b -> p (a b)")
        heads = gone[:, 0:B * INNER].rearrange("p (b h d) -> p b h d", b=B, h=H)
        headsT = gone[:, B * INNER:2 * B * INNER].rearrange("p (c b t) -> p c b t", c=IC, b=B)

        key_room = kT_sb[:].rearrange("p c t -> p (c t)")
        query_room = qT_sb[:].rearrange("p c t -> p (c t)")
        value_room = v_sb[:].rearrange("p b h d -> p (b h d)")
        all_ctx = key_room[:, 0:KEYS]
        all_keys = key_room[0:HD, KEYS:2 * KEYS]
        all_probs = query_room[:, 0:KEYS]
        all_probsT = query_room[:, KEYS:2 * KEYS]
        all_values = value_room[:, 0:KB * HD]
        head_w = value_room[:, KB * HD:(KB + 3) * HD].rearrange("p (w d) -> p w d", w=3)
        batch_x = value_room[:, (KB + 3) * HD:(KB + 5) * HD]
        head_q = value_room[0:HD, (KB + 5) * HD:(KB + 7) * HD]
        all_negmax = sb("all_negmax", [P, 1])
        all_sum = sb("all_sum", [P, 2])
        spare = sb("spare", [P, 1])
        heads_flat = gone[:, 0:B * INNER]

        x1_sb = sb("x1_sb", [P, B, D])
        x1b_sb = sb("x1b_sb", [P, B, D])
        stats2 = sb("stats2", [P, B, 6])
        mv2 = sb("mv2", [P, B, 2])
        rstd2 = sb("rstd2", [P, B])
        xa_sb = sb("xa_sb", [P, B, D])
        xaT = sb("xaT", [P, B, T])
        hb_sb = sb("hb_sb", [P, 2])
        K_sb = sb("K_sb", [P, B, T])
        KV_sb = sb("KV_sb", [P, B, T])
        Kc_sb = sb("Kc_sb", [P, B, T])
        KVc_sb = sb("KVc_sb", [P, B, T])
        tq_sb = sb("tq_sb", [P, B, T])
        tk_sb = sb("tk_sb", [P, B, T])
        Q_sb = sb("Q_sb", [P, B, T])
        Q2_sb = sb("Q2_sb", [P, B, T])
        K2_sb = sb("K2_sb", [P, B, T])
        S_sb = KVc_sb
        Oar_sb = sb("Oar_sb", [P, B, T])
        E_sb = sb("E_sb", [P, B, T])
        S2_sb = sb("S2_sb", [P, B, T])
        Oma_sb = S_sb
        x2_sb = sb("x2_sb", [P, B, D])
        stats3 = sb("stats3", [P, B, 6])
        mv3 = sb("mv3", [P, B, 2])
        rstd3 = sb("rstd3", [P, B])
        xf_sb = sb("xf_sb", [P, B, D])
        xfT = sb("xfT", [P, B, T])

        lmax = sb("lmax", [P, B])
        lsh = sb("lsh", [P, B, NE])
        lexp = sb("lexp", [P, B, NE])
        lsum = sb("lsum", [P, B])
        lrec = sb("lrec", [P, B])
        prob = sb("prob", [P, B, NE])
        probE = sb("probE", [NE, NT])
        work = [sb(f"work{i}", [NE, CAP + (2 * T if i < NG else 0)]) for i in range(NG + 1)]
        sel_eq = sb("sel_eq", [NE, NT])
        tie_win = sb("tie_win", [NE, CAP])
        room = sb("room", [NE, 1])
        tie_rank = sb("tie_rank", [NE, NT])
        sel = sb("sel", [NE, NT])
        ones_e = sb("ones_e", [NE, NT])
        assigned = sb("assigned", [P, B])
        free_tok = sb("free_tok", [P, B])
        m_sb = sb("m_sb", [P, B, NE])
        m1_sb = sb("m1_sb", [P, B, NE])
        pm_sb = sb("pm_sb", [P, B, NE])
        val_sb = sb("val_sb", [P, B, NE])
        vmax = sb("vmax", [P, B])
        veq = sb("veq", [P, B, NE])
        order_sb = sb("order_sb", [P, B, NE])
        code = sb("code", [P, B, NE])
        cmax = sb("cmax", [P, B])
        onehot = sb("onehot", [P, B, NE])
        gate = sb("gate", [P, B, NE])
        gelu_sb = probs[:].rearrange("p a b t -> p a (b t)").rearrange("p a (f t) -> p a f t", f=FC)
        diag = sb("diag", [P, 2, P])
        h_sb = kT_sb[:].rearrange("p (b x) (e d) -> p b (x e) d", b=B, d=D)
        y_sb = x_sb

        names = """ld_x ld_ctxk ld_wv ld_wq ld_wo ld_attn ld_ffn1 ld_ffn2 stored
            consts_ident consts_done zero_done
            ln1_stats ln1_mv ln1_var ln1_rstd ln1_out ln1_T xnT_ready proj proj_act proj_dve
            scores maxes probs_done probs_T pt_act pt_dve pv rsums heads_done headsT_ps headsT_done
            attn_ps x1_done ln2_stats ln2_mv ln2_var ln2_rstd ln2_out x1b_done ln2_T xaT_done
            kq_ps k2_ps K_done tq_done tk_done Q_done Q2_done K2_done hb_done
            KV_done Kc_done KVc_done Krec_done S_done Oar_done E0_done E_done K2E_done S2_done Oma_done O_done
            proj_ps x2_done ln3_stats ln3_mv ln3_var ln3_rstd ln3_out ln3_T xfT_done
            logits_ps lmax_done lsh_done lexp_done lsum_done lrec_done prob_done probE_ps probE_done
            top_step sel_done selT_ps route_step gates_done
            h1_ps gelu_done h2_ps h_act diag_done combined
            ctx_squared w_squared ksum_done wsum_done bound_ps bound_step flag_ready
            g_room g_ctx g_staged g_qk_ps g_qk g_scores_ps g_masked g_max g_values g_exp g_turned g_turned_sb g_pv g_rec g_head""".split()
        s = {n: sem(n) for n in names}
        (ld_x, ld_ctxk, ld_wv, ld_wq, ld_wo, ld_attn, ld_ffn1, ld_ffn2, stored,
         consts_ident, consts_done, zero_done,
         ln1_stats, ln1_mv, ln1_var, ln1_rstd, ln1_out, ln1_T, xnT_ready, proj, proj_act, proj_dve,
         scores, maxes, probs_done, probs_T, pt_act, pt_dve, pv, rsums, heads_done, headsT_ps, headsT_done,
         attn_ps, x1_done, ln2_stats, ln2_mv, ln2_var, ln2_rstd, ln2_out, x1b_done, ln2_T, xaT_done,
         kq_ps, k2_ps, K_done, tq_done, tk_done, Q_done, Q2_done, K2_done, hb_done,
         KV_done, Kc_done, KVc_done, Krec_done, S_done, Oar_done, E0_done, E_done, K2E_done, S2_done, Oma_done, O_done,
         proj_ps, x2_done, ln3_stats, ln3_mv, ln3_var, ln3_rstd, ln3_out, ln3_T, xfT_done,
         logits_ps, lmax_done, lsh_done, lexp_done, lsum_done, lrec_done, prob_done, probE_ps, probE_done,
         top_step, sel_done, selT_ps, route_step, gates_done,
         h1_ps, gelu_done, h2_ps, h_act, diag_done, combined,
         ctx_squared, w_squared, ksum_done, wsum_done, bound_ps, bound_step, flag_ready,
         g_room, g_ctx, g_staged, g_qk_ps, g_qk, g_scores_ps, g_masked, g_max, g_values, g_exp, g_turned, g_turned_sb,
         g_pv, g_rec, g_head) = [s[n] for n in names]
        ld_wk = [sem(f"ld_wk{i}") for i in range(2)]
        ld_ctx = [sem(f"ld_ctx{i}") for i in range(GUARD_LOADS)]

        y_step = [sem(f"y_step{i}") for i in range(B)]
        N_PROJ = 3 * IC
        PROJ_V, PROJ_Q = IC, 2 * IC

        def left(j):
            return (proj_act, j // 3 + 1) if j % 3 == 0 else (proj_dve, j - j // 3)

        def turner(i):
            return (pt_act, i // 2 + 1) if i % 2 == 0 else (pt_dve, i // 2 + 1)

        def unit(i):
            return i // 4, i // 2 % 2, i % 2

        BOUND_Q = 5
        SQ0 = 3
        post_bank = (misc_ps, head_ps)

        def out_ps(g, q, n):
            return (score_ps[2 + n] if q == 0 else turn_ps[n])[:]

        def four(ap):
            return ap.rearrange("p (a b) -> p a b", a=4)

        def read_flag(eng):
            eng.wait_ge(flag_ready, 1)
            return eng.value_load(flag[0:1, 0:1], min_val=0, max_val=1)

        block = es.enter_context(nc.Block())

        @block.sync
        def _(sp):
            guard_rows = ctx.rearrange("b k d -> (b k) d").rearrange("(p r) d -> p (r d)", p=P)
            w = GUARD_CHUNKS * GUARD_W // GUARD_LOADS

            def load_ctx(n):
                sp.dma_start(ctx_sb[:].rearrange("p a b -> p (a b)")[:, n * w:(n + 1) * w],
                             guard_rows[:, n * w:(n + 1) * w]).then_inc(ld_ctx[n], 16)

            for n in range(2):
                sp.dma_start(wk_sb[:, n * 512:(n + 1) * 512], w_k[:, n * 512:(n + 1) * 512]).then_inc(ld_wk[n], 16)
            sp.dma_start(x_sb[:], x.rearrange("b t d -> t b d")).then_inc(ld_x, 16)
            sp.dma_start(wv_sb[:], w_v).then_inc(ld_wv, 16)
            load_ctx(0)
            load_ctx(1)
            sp.dma_start(wq_sb[:], w_q).then_inc(ld_wq, 16)
            load_ctx(2)
            load_ctx(3)
            sp.dma_start(wo_sb[:], w_o.rearrange("(c p) n -> p c n", p=P)).then_inc(ld_wo, 16)
            sp.dma_start(aw_sb[:], attn_w.rearrange("w i o -> i w o")).then_inc(ld_attn, 16)
            sp.dma_start(ab_sb[:], attn_b).then_inc(ld_attn, 16)
            sp.dma_start(bproj_sb[:], b_proj.partition_broadcast(P)).then_inc(ld_attn, 16)
            sp.dma_start(wg_sb[:], w_g).then_inc(ld_attn, 16)
            sp.dma_start(w1_sb[:], w_1.rearrange("e d f -> d e f")).then_inc(ld_ffn1, 16)
            sp.dma_start(w2_sb[:], w_2.rearrange("e (c p) d -> p e c d", p=P)).then_inc(ld_ffn2, 16)
            masked_keys_vanish = read_flag(sp)
            with sp.If(masked_keys_vanish == 0):
                with sp.Fori(0, B) as b:
                    sp.wait_ge(g_room, b * H + 1)
                    sp.dma_start(all_ctx, ctx_t[bass.ds(b, 1)].rearrange("b d k -> (b d) k")).then_inc(g_ctx, 16)
            for b in range(B):
                sp.wait_ge(y_step[b], NE if b else 1)
            sp.dma_start(out.rearrange("b t d -> t b d"), y_sb[:]).then_inc(stored, 16)
            sp.wait_ge(stored, 16)

        @block.gpsimd
        def _(pool):
            nc.gpsimd.memset(ident[:], 0.0).then_inc(zero_done, 1)
            nc.gpsimd.memset(minus_half[:], -0.5).then_inc(zero_done, 1)
            nc.gpsimd.memset(ident_a[:], 0.0).then_inc(zero_done, 1)
            nc.gpsimd.memset(causal_b[:], 0.0).then_inc(zero_done, 1)
            pool.wait_ge(zero_done, 1)
            nc.gpsimd.affine_select(out=ident[:], in_=ident[:], compare_op=ALU.not_equal, fill=1.0, base=0,
                                    pattern=[[-1, P]], channel_multiplier=1).then_inc(consts_ident, 1)
            pool.wait_ge(ld_x, 16)

            def rsqrt(var_ready, n, of, to, done):
                pool.wait_ge(var_ready, n)
                nc.gpsimd.tensor_tensor(to, of, minus_half[:, 0:to.shape[1]], ALU.pow).then_inc(done, 1)

            pool.wait_ge(zero_done, 4)
            rsqrt(ln1_var, 1, mv[:, :, 1], rstd[:], ln1_rstd)
            nc.gpsimd.affine_select(out=ident_a[:], in_=ident_a[:], compare_op=ALU.not_equal, fill=MASK_A, base=0,
                                    pattern=[[-1, P]], channel_multiplier=1).then_inc(consts_done, 1)
            nc.gpsimd.affine_select(out=causal_b[:], in_=causal_b[:], compare_op=ALU.is_ge, fill=MASK_B, base=0,
                                    pattern=[[0, 4], [-1, P]], channel_multiplier=1).then_inc(consts_done, 1)
            nc.gpsimd.memset(ones[:], 1.0).then_inc(consts_done, 1)
            nc.gpsimd.memset(ones_e[:], 1.0).then_inc(consts_done, 1)
            nc.gpsimd.memset(v_sb[:, :, :, HD:HD + 1], 1.0).then_inc(consts_done, 1)
            for e in range(NE):
                nc.gpsimd.memset(order_sb[:, :, e:e + 1], float(NE - e)).then_inc(consts_done, 1)
            nc.gpsimd.memset(E_sb[:, :, 0:1], 0.0).then_inc(E0_done, 1)
            pool.wait_ge(ld_wk[0], 16)
            pool.wait_ge(ld_wk[1], 16)
            pool.wait_ge(ld_wq, 16)
            for n, w in enumerate((wk_sb, wq_sb)):
                nc.gpsimd.tensor_tensor(wsq_sb[:, n].rearrange("p h d -> p (h d)"), w[:], w[:], ALU.mult).then_inc(w_squared, 1)
            pool.wait_ge(ld_attn, 64)
            nc.gpsimd.tensor_scalar(hb_sb[:, 0:1], ab_sb[:, 1:2], 0.5, None, ALU.mult).then_inc(hb_done, 1)
            nc.gpsimd.tensor_scalar(hb_sb[:, 1:2], ab_sb[:, 2:3], 0.5 * K2_SCALE, None, ALU.mult).then_inc(hb_done, 1)

            for g, bs in enumerate(GROUPS):
                b0, n = bs[0], len(bs)
                bb = slice(b0, b0 + n)
                rsqrt(ln2_var, g + 1, mv2[:, bb, 1], rstd2[:, bb], ln2_rstd)
                pool.wait_ge(K_done, g + 1)
                pool.wait_ge(xaT_done, g + 1)
                nc.gpsimd.tensor_tensor(KV_sb[:, bb], K_sb[:, bb], xaT[:, bb], ALU.mult).then_inc(KV_done, 1)
                pool.wait_ge(tq_done, g + 1)
                nc.gpsimd.tensor_scalar(Q_sb[:, bb], tq_sb[:, bb], 0.5, 0.5, ALU.mult, ALU.add).then_inc(Q_done, 1)
                pool.wait_ge(Q_done, g + 1)
                pool.wait_ge(KVc_done, b0 + n)
                nc.gpsimd.tensor_tensor(S_sb[:, bb], KVc_sb[:, bb], Q_sb[:, bb], ALU.mult).then_inc(S_done, 1)
                pool.wait_ge(tk_done, g + 1)
                nc.gpsimd.tensor_scalar(K2_sb[:, bb], tk_sb[:, bb], 0.5, 0.5, ALU.mult, ALU.add).then_inc(K2_done, 1)
                nc.gpsimd.tensor_scalar(Q2_sb[:, bb], Q_sb[:, bb], LEAK / D ** 0.5, None, ALU.mult).then_inc(Q2_done, 1)
                bias = bproj_sb[:].unsqueeze(1).to_broadcast([P, n, D])
                nc.gpsimd.tensor_tensor(x1b_sb[:, bb], x1_sb[:, bb], bias, ALU.add).then_inc(x1b_done, 1)
                rsqrt(ln3_var, g + 1, mv3[:, bb, 1], rstd3[:, bb], ln3_rstd)

        @block.scalar
        def _(act):
            act.dma_start(ctxk_sb[:], ctx_t[:, :, 0:T].rearrange("b d k -> d b k")).then_inc(ld_ctxk, 16)

            def square(c):
                if c % (GUARD_CHUNKS // GUARD_LOADS) == 0:
                    act.wait_ge(ld_ctx[c * GUARD_LOADS // GUARD_CHUNKS], 16)
                if c >= 2:
                    act.wait_ge(ctx_squared, c - 1)
                nc.scalar.activation(sq_sb[:, c % 2], ctx_sb[:, c], ACT.Square, accum_out=ksum[:, c:c + 1]).then_inc(ctx_squared, 1)

            for j in range(0, N_PROJ, 3):
                act.wait_ge(proj, j + 1)
                src = score_ps[j % 4][:]
                if j < PROJ_V:
                    nc.scalar.activation(kT_sb[:, j, :], src, ACT.Copy).then_inc(proj_act, 1)
                elif j < PROJ_Q:
                    b, hf = (j - PROJ_V) // 2, (j - PROJ_V) % 2
                    nc.scalar.activation(v_sb[:, b, 8 * hf:8 * hf + 8, 0:HD],
                                         src.rearrange("p (h d) -> p h d", h=8), ACT.Copy).then_inc(proj_act, 1)
                else:
                    nc.scalar.activation(qT_sb[:, j - PROJ_Q, :], src, ACT.Copy, scale=QSCALE).then_inc(proj_act, 1)
                for c in range(max(j - SQ0, 0), min(j - SQ0 + 3, GUARD_CHUNKS)):
                    square(c)

            def exps(i):
                act.wait_ge(maxes, i + 1)
                if i >= 4:
                    act.wait_ge(probs_T, i - 3)
                for j in range(4):
                    a = nc.scalar.activation(probs[:, i % 4, j, :], score_ps[i % 4][:, j * T:(j + 1) * T], ACT.Exp,
                                             bias=negmax[:, i, j:j + 1])
                a.then_inc(probs_done, 1)

            def turned(i):
                act.wait_ge(probs_T, i + 1)
                if i >= 2:
                    act.wait_ge(pv, i - 1)
                nc.scalar.activation(probsT[:, i % 2].rearrange("p a b -> p (a b)"), turn_ps[i % 2][:],
                                     ACT.Copy).then_inc(pt_act, 1)

            def heads_turned(u):
                b, hf = u // 2, u % 2
                act.wait_ge(headsT_ps, u + 1)
                nc.scalar.activation(headsT[:, 4 * hf:4 * hf + 4, b, :], four(misc_ps[:]), ACT.Copy).then_inc(headsT_done, 1)

            def post(g, width=T):
                b0, n = GROUPS[g][0], len(GROUPS[g])
                return post_bank[g][:, 0:n * width].rearrange("p (a b) -> p a b", a=n), slice(b0, b0 + n)

            def post_input(g):
                ps, bb = post(g)
                act.wait_ge(ln2_T, g + 1)
                nc.scalar.activation(xaT[:, bb], ps, ACT.Copy).then_inc(xaT_done, 1)

            def post_gates(g):
                ps, bb = post(g)
                n = len(GROUPS[g])
                act.wait_ge(kq_ps, g + 1)
                if g == 0:
                    act.wait_ge(ld_attn, 64)
                    act.wait_ge(hb_done, 2)
                nc.scalar.activation(K_sb[:, bb], ps, ACT.Exp, bias=ab_sb[:, 0:1]).then_inc(K_done, 1)
                nc.scalar.activation(tq_sb[:, bb], post_bank[g][:, 256:256 + n * T].rearrange("p (a b) -> p a b", a=n),
                                     ACT.Tanh, bias=hb_sb[:, 0:1], scale=0.5).then_inc(tq_done, 1)

            def post_gate2(g):
                ps, bb = post(g)
                act.wait_ge(k2_ps, g + 1)
                nc.scalar.activation(tk_sb[:, bb], ps, ACT.Tanh, bias=hb_sb[:, 1:2], scale=0.5 * K2_SCALE).then_inc(tk_done, 1)

            def post_input3(g):
                ps, bb = post(g)
                act.wait_ge(ln3_T, g + 1)
                nc.scalar.activation(xfT[:, bb], ps, ACT.Copy).then_inc(xfT_done, 1)

            def post_router(g):
                bb = post(g)[1]
                act.wait_ge(lsh_done, g + 1)
                nc.scalar.activation(lexp[:, bb], lsh[:, bb], ACT.Exp).then_inc(lexp_done, 1)

            def gelu(g, e):
                m = g * NE + e
                act.wait_ge(h1_ps, m + 1)
                if m == 0:
                    act.wait_ge(probs_T, UNITS)
                if m >= 4:
                    act.wait_ge(h2_ps, m - 3)
                nc.scalar.activation(gelu_sb[:, m % 4].rearrange("p a b -> p (a b)"), score_ps[m % 2][:],
                                     ACT.Gelu).then_inc(gelu_done, 1)

            def expert_out(q):
                act.wait_ge(h2_ps, 4 * q + 4)
                for n in range(2):
                    nc.scalar.activation(h_sb[:, n, 4 * q:4 * q + 4, :], four(out_ps(0, q, n)), ACT.Copy).then_inc(h_act, 1)

            def general():
                with act.Fori(0, B * H) as t:
                    act.wait_ge(g_qk_ps, t + 1)
                    nc.scalar.activation(head_q, misc_ps[0:HD, 0:T], ACT.Copy, scale=QSCALE)
                    for c in range(4):
                        a = nc.scalar.activation(all_keys[:, c * 512:(c + 1) * 512], score_ps[c][0:HD, :], ACT.Copy)
                    a.then_inc(g_qk, 1)
                    act.wait_ge(g_max, t + 1)
                    nc.scalar.activation(all_probs, all_probs, ACT.Exp, bias=all_negmax[:], accum_out=all_sum[:, 0:1]).then_inc(g_exp, 1)
                act.wait_ge(g_head, B * H)
                nc.scalar.activation(spare[:], all_negmax[:], ACT.Copy).then_inc(probs_done, UNITS)

            def slots(attention):
                for sl in range(1, SETS + 3):
                    for i in (2 * sl - 2, 2 * sl - 1):
                        if attention and i < UNITS:
                            exps(i)
                        if attention and 0 < i <= UNITS and turner(i - 1)[0] is pt_act:
                            turned(i - 1)
                    if sl == SETS + 1:
                        post_gates(0)
                    if sl >= 3:
                        heads_turned(sl - 3)
                    if sl == SETS:
                        post_input(0)
                    if sl == SETS + 2:
                        post_gate2(0)

            masked_keys_vanish = read_flag(act)
            with act.If(masked_keys_vanish == 0):
                general()
                slots(attention=False)
            with act.Else():
                slots(attention=True)
            post_input(1)
            post_input3(0)
            post_gates(1)
            post_router(0)
            post_gate2(1)
            for e in range(NE):
                gelu(0, e)
                if e == 4:
                    expert_out(0)
                if e == 5:
                    post_input3(1)
                if e == 6:
                    post_router(1)
            gelu(1, 0)
            expert_out(1)
            for e in range(1, NE):
                gelu(1, e)
            act.wait_ge(gates_done, 1)
            for e in range(NE):
                if e >= 2:
                    act.wait_ge(combined, e - 1)
                nc.scalar.activation(diag[:, e % 2], ident[:], ACT.Copy, scale=gate[:, 0, e:e + 1]).then_inc(diag_done, 1)

        @block.tensor
        def _(pe):
            pe.wait_ge(consts_ident, 1)
            readers = {}

            def take(bank, reader, count):
                if bank.name in readers:
                    pe.wait_ge(*readers[bank.name])
                readers[bank.name] = (reader, count)

            def proj_bank(j):
                if j >= 4:
                    pe.wait_ge(*left(j - 4))
                return score_ps[j % 4][:]

            pe.wait_ge(ld_ctxk, 16)
            for c in range(IC):
                if c % 4 == 0:
                    pe.wait_ge(ld_wk[c // 4], 16)
                nc.tensor.matmul(proj_bank(c), wk_sb[:, c * P:(c + 1) * P], ctxk_sb[:].rearrange("p b k -> p (b k)"),
                                 start=True, stop=True).then_inc(proj, 1)
            for b in range(B):
                pe.wait_ge(ln1_out, b + 1)
                t = nc.tensor.transpose(turn_ps[0][:, b * T:(b + 1) * T], xn_sb[:, b, :], ident[:])
            t.then_inc(ln1_T, 1)
            pe.wait_ge(ld_wv, 16)
            for b in range(B):
                for hf in range(2):
                    nc.tensor.matmul(proj_bank(PROJ_V + 2 * b + hf), ctxk_sb[:, b, :], wv_sb[:, hf * 512:(hf + 1) * 512],
                                     start=True, stop=True).then_inc(proj, 1)
            pe.wait_ge(ld_wq, 16)
            pe.wait_ge(xnT_ready, 1)
            for c in range(IC):
                if c == BOUND_Q:
                    pe.wait_ge(wsum_done, 1)
                    pe.wait_ge(consts_done, 3)
                    nc.tensor.matmul(misc_ps[0:1, 0:2 * H], ones[:, 0:1], wsum[:], start=True, stop=True)
                    pe.wait_ge(ksum_done, 1)
                    nc.tensor.matmul(misc_ps[0:1, P:2 * P], kmax[:], ident[:], start=True, stop=True).then_inc(bound_ps, 1)
                nc.tensor.matmul(proj_bank(PROJ_Q + c), wq_sb[:, c * P:(c + 1) * P],
                                 xnT_sb[:].rearrange("p b k -> p (b k)"), start=True, stop=True).then_inc(proj, 1)

            def general():
                pe.wait_ge(proj_act, N_PROJ // 3)
                pe.wait_ge(proj_dve, N_PROJ - N_PROJ // 3)
                nc.tensor.transpose(turn_ps[0][:, 0:P], ident[:], ident[:]).then_inc(g_room, 1)
                with pe.Fori(0, B) as b:
                    with pe.Fori(0, H) as h:
                        t1 = b * H + h + 1
                        pe.wait_ge(g_ctx, b * 16 + 16)
                        pe.wait_ge(g_staged, t1)
                        nc.tensor.matmul(misc_ps[0:HD, 0:T], head_w[:, 0], batch_x, start=True, stop=True)
                        for c in range(4):
                            m = nc.tensor.matmul(score_ps[c][0:HD, :], head_w[:, 1], all_ctx[:, c * 512:(c + 1) * 512],
                                                 start=True, stop=True)
                        m.then_inc(g_qk_ps, 1)
                        for k in range(KB):
                            nc.tensor.matmul(turn_ps[k // 8][:, k % 8 * HD:(k % 8 + 1) * HD], all_ctx[:, k * P:(k + 1) * P],
                                             head_w[:, 2], start=True, stop=True)
                        pe.wait_ge(g_qk, t1)
                        for c in range(4):
                            m = nc.tensor.matmul(score_ps[c][:], head_q, all_keys[:, c * 512:(c + 1) * 512],
                                                 start=True, stop=True)
                        m.then_inc(g_scores_ps, 1)
                        pe.wait_ge(g_exp, t1)
                        for k in range(KB):
                            m = nc.tensor.transpose(score_ps[k // 4][:, k % 4 * T:(k % 4 + 1) * T],
                                                    all_probs[:, k * P:(k + 1) * P], ident[:])
                        m.then_inc(g_turned, 1)
                        pe.wait_ge(g_turned_sb, t1)
                        for k in range(KB):
                            m = nc.tensor.matmul(head_ps[:, 0:HD], all_probsT[:, k * T:(k + 1) * T],
                                                 all_values[:, k * HD:(k + 1) * HD], start=(k == 0), stop=(k == KB - 1))
                        m.then_inc(g_pv, 1)
                        nc.tensor.transpose(misc_ps[:, P:2 * P], ident[:], ident[:]).then_inc(g_room, 1)

            def score_set(u, half):
                b, hf = u // 2, u % 2
                if half:
                    score_heads(u, b, hf, (2, 3))
                    return
                if u == 0:
                    pe.wait_ge(consts_done, 5)
                if u < 2:
                    pe.wait_ge(proj_act, N_PROJ // 3)
                    pe.wait_ge(proj_dve, N_PROJ - N_PROJ // 3)
                else:
                    pe.wait_ge(probs_done, 2 * u - 2)
                for par in range(2):
                    nc.tensor.matmul(score_ps[(2 * u + par) % 4][:], ident_a[:], causal_b[:].rearrange("p a b -> p (a b)"),
                                     start=True, stop=False, skip_group_check=True)
                score_heads(u, b, hf, (0, 1))

            def score_heads(u, b, hf, js):
                for j in js:
                    for par in range(2):
                        r = slice(par * HD, (par + 1) * HD)
                        m = nc.tensor.matmul(score_ps[(2 * u + par) % 4][:, j * T:(j + 1) * T],
                                             qT_sb[r, 4 * hf + j, b * T:(b + 1) * T], kT_sb[r, 4 * hf + j, b * T:(b + 1) * T],
                                             start=False, stop=(j == 3), skip_group_check=True)
                        if j == 3:
                            m.then_inc(scores, 1)

            def turn_probs(i):
                pe.wait_ge(probs_done, i + 1)
                if i >= 2:
                    pe.wait_ge(*turner(i - 2))
                for j in range(4):
                    t = nc.tensor.transpose(turn_ps[i % 2][:, j * T:(j + 1) * T], probs[:, i % 4, j, :], ident[:])
                t.then_inc(probs_T, 1)

            def weigh_values(i):
                b, hf, par = unit(i)
                pe.wait_ge(*turner(i))
                if i >= 1:
                    pe.wait_ge(heads_done, i)
                for j in range(4):
                    m = nc.tensor.matmul(head_ps[:, j * (HD + 1):(j + 1) * (HD + 1)], probsT[:, i % 2, j, :],
                                         v_sb[:, b, 8 * hf + 2 * j + par, :], start=True, stop=True)
                m.then_inc(pv, 1)

            def turn_heads(u):
                b, hf = u // 2, u % 2
                pe.wait_ge(heads_done, 2 * u + 2)
                take(misc_ps, headsT_done, u + 1)
                for c in range(4):
                    t = nc.tensor.transpose(misc_ps[:, c * T:(c + 1) * T],
                                            heads[:, b, 8 * hf + 2 * c:8 * hf + 2 * c + 2, :].rearrange("p h d -> p (h d)"),
                                            ident[:])
                t.then_inc(headsT_ps, 1)

            def post_out(g):
                if g == 0:
                    pe.wait_ge(ld_wo, 16)
                pe.wait_ge(headsT_done, 2 * GROUPS[g][-1] + 2)
                ps = post_bank[g]
                if g == 1:
                    pe.wait_ge(heads_done, UNITS)
                take(ps, x1_done, g + 1)
                for n, b in enumerate(GROUPS[g]):
                    for c in range(IC):
                        m = nc.tensor.matmul(ps[:, n * D:(n + 1) * D], headsT[:, c, b, :], wo_sb[:, c, :],
                                             start=(c == 0), stop=(c == IC - 1))
                m.then_inc(attn_ps, 1)

            def post_turn(g, ready, rows, done, reader):
                ps = post_bank[g]
                pe.wait_ge(ready, GROUPS[g][-1] + 1)
                take(ps, reader, g + 1)
                for n, b in enumerate(GROUPS[g]):
                    t = nc.tensor.transpose(ps[:, n * T:(n + 1) * T], rows[:, b, :], ident[:])
                t.then_inc(done, 1)

            def gate_input(g):
                return xaT[:, GROUPS[g][0]:GROUPS[g][-1] + 1].rearrange("p b t -> p (b t)")

            def post_gates(g):
                ps, n = post_bank[g], len(GROUPS[g])
                if g == 0:
                    pe.wait_ge(ld_attn, 64)
                take(ps, tq_done, g + 1)
                nc.tensor.matmul(ps[:, 0:n * T], aw_sb[:, 0, :], gate_input(g), start=True, stop=True)
                nc.tensor.matmul(ps[:, 256:256 + n * T], aw_sb[:, 1, :], gate_input(g), start=True, stop=True).then_inc(kq_ps, 1)

            def post_gate2(g):
                ps, n = post_bank[g], len(GROUPS[g])
                take(ps, tk_done, g + 1)
                nc.tensor.matmul(ps[:, 0:n * T], aw_sb[:, 2, :], gate_input(g), start=True, stop=True).then_inc(k2_ps, 1)

            def post_proj(g):
                ps = post_bank[g]
                pe.wait_ge(O_done, g + 1)
                take(ps, x2_done, g + 1)
                for n, b in enumerate(GROUPS[g]):
                    m = nc.tensor.matmul(ps[:, n * D:(n + 1) * D], Oar_sb[:, b, :], aw_sb[:, 3, :], start=True, stop=True)
                m.then_inc(proj_ps, 1)

            def post_logits(g):
                ps = post_bank[g]
                take(ps, lsh_done, g + 1)
                for n, b in enumerate(GROUPS[g]):
                    m = nc.tensor.matmul(ps[:, n * NE:(n + 1) * NE], xfT[:, b, :], wg_sb[:], start=True, stop=True)
                m.then_inc(logits_ps, 1)

            def post_probs(g):
                ps = post_bank[g]
                pe.wait_ge(prob_done, g + 1)
                take(ps, probE_done, g + 1)
                for n, b in enumerate(GROUPS[g]):
                    t = nc.tensor.transpose(ps[0:NE, n * T:(n + 1) * T], prob[:, b, :], ident[:])
                t.then_inc(probE_ps, 1)

            def hidden(g, e):
                m = g * NE + e
                n = len(GROUPS[g])
                if m == 0:
                    pe.wait_ge(ld_ffn1, 16)
                    pe.wait_ge(probs_done, UNITS)
                if m >= 2:
                    pe.wait_ge(gelu_done, m - 1)
                for f in range(FC):
                    mm = nc.tensor.matmul(score_ps[m % 2][:, f * n * T:(f + 1) * n * T], w1_sb[:, e, f * P:(f + 1) * P],
                                          xfT[:, GROUPS[g][0]:GROUPS[g][0] + n].rearrange("p b t -> p (b t)"),
                                          start=True, stop=True)
                mm.then_inc(h1_ps, 1)

            def answer(g, e):
                m = g * NE + e
                pe.wait_ge(gelu_done, m + 1)
                if m == 0:
                    pe.wait_ge(ld_ffn2, 16)
                if g == 1 and e % 4 == 0:
                    pe.wait_ge(h_act, e // 2 + 2)
                for n in range(len(GROUPS[g])):
                    for f in range(FC):
                        mm = nc.tensor.matmul(out_ps(g, e // 4, n)[:, e % 4 * D:(e % 4 + 1) * D],
                                              gelu_sb[:, m % 4, f, n * T:(n + 1) * T], w2_sb[:, e, f, :],
                                              start=(f == 0), stop=(f == FC - 1))
                mm.then_inc(h2_ps, 1)

            def slots(attention):
                for sl in range(SETS + 3):
                    for half in range(2):
                        if attention and sl < SETS:
                            score_set(sl, half)
                        if attention and 0 <= 2 * sl - 3 + half < UNITS:
                            turn_probs(2 * sl - 3 + half)
                        if attention and 0 <= 2 * sl - 4 + half < UNITS:
                            weigh_values(2 * sl - 4 + half)
                        if sl == SETS - 1 and half == 0:
                            post_out(0)
                        if sl == SETS + 1 and half == 0:
                            post_gates(0)
                    if sl >= 3:
                        turn_heads(sl - 3)
                    if sl == SETS:
                        post_turn(0, ln2_out, xa_sb, ln2_T, xaT_done)
                post_gate2(0)

            masked_keys_vanish = read_flag(pe)
            with pe.If(masked_keys_vanish == 0):
                general()
                slots(attention=False)
            readers.clear()
            with pe.Else():
                slots(attention=True)
            post_out(1)
            post_proj(0)
            post_turn(1, ln2_out, xa_sb, ln2_T, xaT_done)
            post_turn(0, ln3_out, xf_sb, ln3_T, xfT_done)
            post_gates(1)
            post_logits(0)
            post_gate2(1)
            hidden(0, 0)
            for e in range(NE):
                if e + 1 < NE:
                    hidden(0, e + 1)
                if e == 1:
                    post_probs(0)
                answer(0, e)
                if e == 2:
                    post_proj(1)
                if e == 4:
                    post_turn(1, ln3_out, xf_sb, ln3_T, xfT_done)
                    post_logits(1)
            hidden(1, 0)
            post_probs(1)
            for e in range(NE):
                if e + 1 < NE:
                    hidden(1, e + 1)
                answer(1, e)
            pe.wait_ge(sel_done, 1)
            take(misc_ps, route_step, 3)
            for b in range(B):
                t = nc.tensor.transpose(misc_ps[:, b * NE:(b + 1) * NE], sel[:, b * T:(b + 1) * T], ident[0:NE, 0:NE])
            t.then_inc(selT_ps, 1)
            take(head_ps, combined, NE)
            for e in range(NE):
                pe.wait_ge(diag_done, e + 1)
                nc.tensor.matmul(head_ps[:, 0:D], diag[:, e % 2], h_sb[:, 0, e, :], start=(e == 0),
                                 stop=(e == NE - 1)).then_inc(combined, 1)

        @block.vector
        def _(dve):
            def norm_stats(b0, n, rows, st, m, stats_done, mv_done, var_done):
                for b in range(b0, b0 + n):
                    nc.vector.bn_stats(st[:, b, :], rows[:, b, :]).then_inc(stats_done, 1)
                for b in range(b0, b0 + n):
                    dve.wait_ge(stats_done, b + 1)
                    nc.vector.bn_aggr(m[:, b, :], st[:, b, :]).then_inc(mv_done, 1)
                dve.wait_ge(mv_done, b0 + n)
                nc.vector.tensor_scalar(m[:, b0:b0 + n, 1], m[:, b0:b0 + n, 1], EPS_LN, None, ALU.add).then_inc(var_done, 1)

            def norm_apply(b0, n, rows, m, r, y, rstd_done, out_done, g):
                dve.wait_ge(rstd_done, g + 1)
                for b in range(b0, b0 + n):
                    nc.vector.tensor_scalar(y[:, b, :], rows[:, b, :], m[:, b, 0:1], r[:, b:b + 1],
                                            ALU.subtract, ALU.mult).then_inc(out_done, 1)

            def bound_of_scores():
                dve.wait_ge(w_squared, 2)
                nc.vector.tensor_reduce(wsum[:], wsq_sb.rearrange("p w h d -> p (w h) d"), AX_X, ALU.add).then_inc(wsum_done, 1)
                dve.wait_ge(ctx_squared, GUARD_CHUNKS)
                nc.vector.tensor_reduce(kmax[:], ksum[:], AX_X, ALU.max).then_inc(ksum_done, 1)
                dve.wait_ge(bound_ps, 1)
                nc.vector.tensor_copy(bound[:, 0:H], misc_ps[0:1, 0:H]).then_inc(bound_step, 1)
                nc.vector.tensor_reduce(bound[:, 2 * H:2 * H + 1], misc_ps[0:1, P:2 * P], AX_X, ALU.max).then_inc(bound_step, 1)
                dve.wait_ge(bound_step, 2)
                nc.vector.tensor_tensor(bound[:, H:2 * H], misc_ps[0:1, H:2 * H], bound[:, 0:H], ALU.mult).then_inc(bound_step, 1)
                dve.wait_ge(bound_step, 3)
                nc.vector.tensor_reduce(bound[:, 2 * H + 1:2 * H + 2], bound[:, H:2 * H], AX_X, ALU.max).then_inc(bound_step, 1)
                dve.wait_ge(bound_step, 4)
                nc.vector.tensor_tensor(bound[:, 2 * H + 2:2 * H + 3], bound[:, 2 * H:2 * H + 1], bound[:, 2 * H + 1:2 * H + 2],
                                        ALU.mult).then_inc(bound_step, 1)
                dve.wait_ge(bound_step, 5)
                nc.vector.tensor_scalar(flag[:], bound[:, 2 * H + 2:2 * H + 3], GUARD_LIMIT, None, ALU.is_lt).then_inc(flag_ready, 1)

            dve.wait_ge(ld_x, 16)
            norm_stats(0, B, x_sb, stats, mv, ln1_stats, ln1_mv, ln1_var)
            norm_apply(0, B, x_sb, mv, rstd, xn_sb, ln1_rstd, ln1_out, 0)

            for j in range(N_PROJ):
                if j == PROJ_Q + BOUND_Q:
                    bound_of_scores()
                if j % 3 == 0:
                    continue
                if j == PROJ_V + 2:
                    dve.wait_ge(ln1_T, 1)
                    nc.vector.tensor_copy(xnT_sb[:], four(turn_ps[0][:])).then_inc(xnT_ready, 1)
                dve.wait_ge(proj, j + 1)
                src = score_ps[j % 4][:]
                if j < PROJ_V:
                    nc.vector.tensor_copy(kT_sb[:, j, :], src).then_inc(proj_dve, 1)
                elif j < PROJ_Q:
                    b, hf = (j - PROJ_V) // 2, (j - PROJ_V) % 2
                    nc.vector.tensor_copy(v_sb[:, b, 8 * hf:8 * hf + 8, 0:HD],
                                          src.rearrange("p (h d) -> p h d", h=8)).then_inc(proj_dve, 1)
                else:
                    nc.vector.tensor_scalar(qT_sb[:, j - PROJ_Q, :], src, QSCALE, None, ALU.mult).then_inc(proj_dve, 1)

            def general():
                with dve.Fori(0, B) as b:
                    with dve.Fori(0, H) as h:
                        t1 = b * H + h + 1
                        dve.wait_ge(g_room, t1)
                        for n, w in enumerate((wq_sb, wk_sb, wv_sb)):
                            nc.vector.tensor_copy(head_w[:, n], w[:, bass.ds(h * HD, HD)])
                        nc.vector.tensor_copy(batch_x, xnT_sb[:].rearrange("p b t -> p (b t)")[:, bass.ds(b * T, T)]).then_inc(g_staged, 1)
                        dve.wait_ge(g_scores_ps, t1)
                        nc.vector.scalar_tensor_tensor(all_probs[:, 0:T], causal_b[:, 0, :], MASK_A, score_ps[0][:, 0:T],
                                                       ALU.mult, ALU.add)
                        nc.vector.tensor_scalar(all_probs[:, T:512], score_ps[0][:, T:512], MASK_A * MASK_B, None, ALU.add)
                        for c in range(1, 4):
                            m = nc.vector.tensor_scalar(all_probs[:, c * 512:(c + 1) * 512], score_ps[c][:], MASK_A * MASK_B,
                                                        None, ALU.add)
                        m.then_inc(g_masked, 1)
                        dve.wait_ge(g_masked, t1)
                        nc.vector.tensor_reduce(all_negmax[:], all_probs, AX_X, ALU.max, negate=True).then_inc(g_max, 1)
                        for c in range(2):
                            m = nc.vector.tensor_copy(all_values[:, c * 512:(c + 1) * 512], turn_ps[c][:])
                        m.then_inc(g_values, 1)
                        dve.wait_ge(g_turned, t1)
                        for c in range(4):
                            m = nc.vector.tensor_copy(all_probsT[:, c * 512:(c + 1) * 512], score_ps[c][:])
                        m.then_inc(g_turned_sb, 1)
                        nc.vector.reciprocal(all_sum[:, 1:2], all_sum[:, 0:1]).then_inc(g_rec, 1)
                        dve.wait_ge(g_rec, t1)
                        dve.wait_ge(g_pv, t1)
                        nc.vector.tensor_scalar(heads_flat[:, bass.ds((b * H + h) * HD, HD)], head_ps[:, 0:HD], all_sum[:, 1:2],
                                                None, ALU.mult).then_inc(g_head, 1)
                dve.wait_ge(g_head, B * H)
                nc.vector.tensor_copy(all_sum[:, 0:1], all_sum[:, 1:2]).then_inc(heads_done, UNITS)

            def row_max(i):
                dve.wait_ge(scores, i + 1)
                nc.vector.tensor_reduce(negmax[:, i, :], four(score_ps[i % 4][:]), AX_X, ALU.max,
                                        negate=True).then_inc(maxes, 1)

            def turned(i):
                dve.wait_ge(probs_T, i + 1)
                if i >= 2:
                    dve.wait_ge(pv, i - 1)
                nc.vector.tensor_copy(probsT[:, i % 2], four(turn_ps[i % 2][:])).then_inc(pt_dve, 1)

            def norm_heads(i):
                b, hf, par = unit(i)
                got = head_ps[:, 0:4 * (HD + 1)].rearrange("p (j d) -> p j d", j=4)
                dve.wait_ge(pv, i + 1)
                nc.vector.reciprocal(rsum[:, i, :], got[:, :, HD]).then_inc(rsums, 1)
                dve.wait_ge(rsums, i + 1)
                to = heads[:, b, 8 * hf:8 * hf + 8, :].rearrange("p (j q) d -> p j q d", q=2)[:, :, par, :]
                nc.vector.tensor_tensor(to, got[:, :, 0:HD], rsum[:, i, :].unsqueeze(2).to_broadcast([P, 4, HD]),
                                        ALU.mult).then_inc(heads_done, 1)

            def group(g, width):
                b0, n = GROUPS[g][0], len(GROUPS[g])
                return post_bank[g][:, 0:n * width].rearrange("p (a b) -> p a b", a=n), b0, n

            def post_x1(g):
                ps, b0, n = group(g, D)
                dve.wait_ge(attn_ps, g + 1)
                nc.vector.tensor_tensor(x1_sb[:, b0:b0 + n], x_sb[:, b0:b0 + n], ps, ALU.add).then_inc(x1_done, 1)
                dve.wait_ge(x1_done, g + 1)
                norm_stats(b0, n, x1_sb, stats2, mv2, ln2_stats, ln2_mv, ln2_var)

            def post_norm2(g):
                b0, n = group(g, D)[1:]
                norm_apply(b0, n, x1_sb, mv2, rstd2, xa_sb, ln2_rstd, ln2_out, g)

            def post_gates(g):
                bs = GROUPS[g]
                b0, n = bs[0], len(bs)
                bb = slice(b0, b0 + n)
                one = ones[:]
                dve.wait_ge(K_done, g + 1)
                if g == 0:
                    dve.wait_ge(consts_done, 3)
                for b in bs:
                    nc.vector.tensor_tensor_scan(Kc_sb[:, b, :], one, K_sb[:, b, :], EPS_CUM, ALU.mult, ALU.add).then_inc(Kc_done, 1)
                dve.wait_ge(KV_done, g + 1)
                for b in bs:
                    nc.vector.tensor_tensor_scan(KVc_sb[:, b, :], one, KV_sb[:, b, :], 0.0, ALU.mult, ALU.add).then_inc(KVc_done, 1)
                dve.wait_ge(Kc_done, b0 + n)
                nc.vector.reciprocal(Kc_sb[:, bb], Kc_sb[:, bb]).then_inc(Krec_done, 1)
                dve.wait_ge(Krec_done, g + 1)
                dve.wait_ge(S_done, g + 1)
                nc.vector.tensor_tensor(Oar_sb[:, bb], S_sb[:, bb], Kc_sb[:, bb], ALU.mult).then_inc(Oar_done, 1)
                dve.wait_ge(Oar_done, g + 1)
                dve.wait_ge(E0_done, 1)
                nc.vector.tensor_tensor(E_sb[:, bb, 1:T], xaT[:, bb, 1:T], Oar_sb[:, bb, 0:T - 1],
                                        ALU.subtract).then_inc(E_done, 1)
                dve.wait_ge(E_done, g + 1)
                dve.wait_ge(K2_done, g + 1)
                nc.vector.tensor_tensor(E_sb[:, bb, 1:T], E_sb[:, bb, 1:T], K2_sb[:, bb, 0:T - 1],
                                        ALU.mult).then_inc(K2E_done, 1)
                dve.wait_ge(K2E_done, g + 1)
                for b in bs:
                    nc.vector.tensor_tensor_scan(S2_sb[:, b, :], one, E_sb[:, b, :], 0.0, ALU.mult, ALU.add).then_inc(S2_done, 1)
                dve.wait_ge(S2_done, b0 + n)
                dve.wait_ge(Q2_done, g + 1)
                nc.vector.tensor_tensor(Oma_sb[:, bb, 1:T], S2_sb[:, bb, 1:T], Q2_sb[:, bb, 0:T - 1],
                                        ALU.mult).then_inc(Oma_done, 1)
                dve.wait_ge(Oma_done, g + 1)
                nc.vector.tensor_tensor(Oar_sb[:, bb, 1:T], Oar_sb[:, bb, 1:T], Oma_sb[:, bb, 1:T],
                                        ALU.add).then_inc(O_done, 1)

            def post_x2(g):
                ps, b0, n = group(g, D)
                dve.wait_ge(proj_ps, g + 1)
                dve.wait_ge(x1b_done, g + 1)
                nc.vector.tensor_tensor(x2_sb[:, b0:b0 + n], x1b_sb[:, b0:b0 + n], ps, ALU.add).then_inc(x2_done, 1)
                dve.wait_ge(x2_done, g + 1)
                norm_stats(b0, n, x2_sb, stats3, mv3, ln3_stats, ln3_mv, ln3_var)

            def post_norm3(g):
                b0, n = group(g, D)[1:]
                norm_apply(b0, n, x2_sb, mv3, rstd3, xf_sb, ln3_rstd, ln3_out, g)

            def post_shift(g):
                logits, b0, n = group(g, NE)
                bb = slice(b0, b0 + n)
                dve.wait_ge(logits_ps, g + 1)
                nc.vector.tensor_reduce(lmax[:, bb], logits, AX_X, ALU.max).then_inc(lmax_done, 1)
                dve.wait_ge(lmax_done, g + 1)
                nc.vector.tensor_tensor(lsh[:, bb], logits, lmax[:, bb].unsqueeze(2).to_broadcast([P, n, NE]),
                                        ALU.subtract).then_inc(lsh_done, 1)

            def post_prob(g):
                b0, n = group(g, NE)[1:]
                bb = slice(b0, b0 + n)
                dve.wait_ge(lexp_done, g + 1)
                nc.vector.tensor_reduce(lsum[:, bb], lexp[:, bb], AX_X, ALU.add).then_inc(lsum_done, 1)
                dve.wait_ge(lsum_done, g + 1)
                nc.vector.reciprocal(lrec[:, bb], lsum[:, bb]).then_inc(lrec_done, 1)
                dve.wait_ge(lrec_done, g + 1)
                nc.vector.tensor_tensor(prob[:, bb], lexp[:, bb], lrec[:, bb].unsqueeze(2).to_broadcast([P, n, NE]),
                                        ALU.mult).then_inc(prob_done, 1)

            def post_probE(g):
                b0, n = group(g, NE)[1:]
                dve.wait_ge(probE_ps, g + 1)
                nc.vector.tensor_copy(probE[:, b0 * T:(b0 + n) * T], post_bank[g][0:NE, 0:n * T]).then_inc(probE_done, 1)

            tops = [0]

            def top_start(g):
                b0, n = GROUPS[g][0], len(GROUPS[g])
                dve.wait_ge(probE_done, g + 1)
                nc.vector.tensor_copy(work[g][:, CAP:CAP + n * T], probE[:, b0 * T:(b0 + n) * T]).then_inc(top_step, 1)
                tops[0] += 1

            def top_rounds(g, rounds):
                cur, nxt = work[g], work[g + 1]
                here = slice(0 if g else CAP, CAP + len(GROUPS[g]) * T)
                for r in rounds:
                    eight = nxt[:, 8 * r:8 * r + 8]
                    dve.wait_ge(top_step, tops[0])
                    nc.vector.max(eight, cur[:, here]).then_inc(top_step, 1)
                    tops[0] += 1
                    if r + 1 < CAP // 8:
                        dve.wait_ge(top_step, tops[0])
                        nc.vector.match_replace(out=cur[:, here], in_to_replace=eight, in_values=cur[:, here],
                                                imm_value=-1.0).then_inc(top_step, 1)
                        tops[0] += 1

            def choose():
                won = work[NG]
                least = won[:, CAP - 1:CAP]
                dve.wait_ge(top_step, tops[0])
                nc.vector.tensor_scalar(sel_eq[:], probE[:], least, None, ALU.is_equal).then_inc(top_step, 1)
                nc.vector.tensor_scalar(tie_win[:], won[:], least, 0.0, ALU.is_equal, ALU.add, accum_out=room[:]).then_inc(top_step, 1)
                tops[0] += 2
                dve.wait_ge(top_step, tops[0])
                nc.vector.tensor_tensor_scan(tie_rank[:], ones_e[:], sel_eq[:], 0.0, ALU.mult, ALU.add).then_inc(top_step, 1)
                tops[0] += 1
                dve.wait_ge(top_step, tops[0])
                nc.vector.scalar_tensor_tensor(tie_rank[:], tie_rank[:], room[:], sel_eq[:], ALU.is_le,
                                               ALU.mult).then_inc(top_step, 1)
                tops[0] += 1
                dve.wait_ge(top_step, tops[0])
                nc.vector.scalar_tensor_tensor(sel[:], probE[:], least, tie_rank[:], ALU.is_gt, ALU.add).then_inc(sel_done, 1)

            def gates():
                picked = misc_ps[:, 0:B * NE].rearrange("p (b e) -> p b e", b=B)
                steps = [0]

                def done(ins):
                    ins.then_inc(route_step, 1)
                    steps[0] += 1

                def wait():
                    dve.wait_ge(route_step, steps[0])

                def wide(ap):
                    return ap.unsqueeze(2).to_broadcast([P, B, NE])

                dve.wait_ge(selT_ps, 1)
                done(nc.vector.tensor_reduce(assigned[:], picked, AX_X, ALU.max))
                wait()
                done(nc.vector.tensor_scalar(free_tok[:], assigned[:], -1.0, 1.0, ALU.mult, ALU.add))
                wait()
                done(nc.vector.tensor_tensor(m_sb[:], picked, wide(free_tok[:]), ALU.max))
                wait()
                done(nc.vector.tensor_scalar(m1_sb[:], m_sb[:], -1.0, None, ALU.add))
                done(nc.vector.tensor_tensor(pm_sb[:], prob[:], m_sb[:], ALU.mult))
                wait()
                done(nc.vector.tensor_tensor(val_sb[:], pm_sb[:], m1_sb[:], ALU.add))
                wait()
                done(nc.vector.tensor_reduce(vmax[:], val_sb[:], AX_X, ALU.max))
                wait()
                done(nc.vector.tensor_tensor(veq[:], val_sb[:], wide(vmax[:]), ALU.is_equal))
                wait()
                dve.wait_ge(consts_done, 5 + NE)
                done(nc.vector.tensor_tensor(code[:], veq[:], order_sb[:], ALU.mult))
                wait()
                done(nc.vector.tensor_reduce(cmax[:], code[:], AX_X, ALU.max))
                wait()
                done(nc.vector.tensor_tensor(onehot[:], code[:], wide(cmax[:]), ALU.is_equal))
                wait()
                nc.vector.tensor_tensor(gate[:], onehot[:], wide(vmax[:]), ALU.mult).then_inc(gates_done, 1)

            def slots(attention):
                for sl in range(1, SETS + 3):
                    for i in (2 * sl - 2, 2 * sl - 1):
                        if attention and i < UNITS:
                            row_max(i)
                    for i in (2 * sl - 3, 2 * sl - 2):
                        if attention and 0 <= i < UNITS and turner(i)[0] is pt_dve:
                            turned(i)
                        if attention and 1 <= i <= UNITS:
                            norm_heads(i - 1)
                    if sl == SETS - 1:
                        post_x1(0)
                    if sl == SETS:
                        post_norm2(0)

            masked_keys_vanish = read_flag(dve)
            with dve.If(masked_keys_vanish == 0):
                general()
                slots(attention=False)
            with dve.Else():
                slots(attention=True)
            post_gates(0)
            post_x1(1)
            post_x2(0)
            post_norm2(1)
            post_norm3(0)
            post_shift(0)
            post_prob(0)
            post_gates(1)
            post_probE(0)
            top_start(0)
            post_x2(1)
            top_rounds(0, range(0, 3))
            post_norm3(1)
            top_rounds(0, range(3, 7))
            post_shift(1)
            top_rounds(0, range(7, 8))
            post_prob(1)
            post_probE(1)
            top_start(1)
            top_rounds(1, range(8))
            choose()
            gates()
            dve.wait_ge(gates_done, 1)
            dve.wait_ge(h_act, 4)
            for e in range(NE):
                for b in range(1, B):
                    g, n = b // 2, b % 2
                    if g == 0:
                        answer = h_sb[:, b, e, :]
                    else:
                        dve.wait_ge(h2_ps, NE + e // 4 * 4 + 4)
                        answer = out_ps(1, e // 4, n)[:, e % 4 * D:(e % 4 + 1) * D]
                    if e:
                        dve.wait_ge(y_step[b], e)
                    nc.vector.scalar_tensor_tensor(y_sb[:, b, :], answer, gate[:, b, e:e + 1], (y_sb if e else x2_sb)[:, b, :],
                                                   ALU.mult, ALU.add).then_inc(y_step[b], 1)
            dve.wait_ge(combined, NE)
            nc.vector.tensor_tensor(y_sb[:, 0, :], head_ps[:, 0:D], x2_sb[:, 0, :], ALU.add).then_inc(y_step[0], 1)


_INS = ["x", "ctx", "ctx_t", "w_q", "w_k", "w_v", "w_o", "attn_w", "attn_b", "b_proj", "w_g", "w_1", "w_2"]


def kernel(x, ctx_1024, L0_xattn_w_q, L0_xattn_w_k, L0_xattn_w_v, L0_xattn_w_o, L0_attn_Wq1, L0_attn_bq1,
           L0_attn_Wk1, L0_attn_bk1, L0_attn_Wk2, L0_attn_bk2, L0_attn_Wproj, L0_attn_bproj,
           L0_ffn_Wg, L0_ffn_W1, L0_ffn_W2):
    import numpy as np
    import concourse.bacc as bacc
    from concourse.bass_utils import run_bass_kernel_spmd

    def lay(a):
        return np.ascontiguousarray(np.asarray(a))

    ctx = lay(ctx_1024)
    arrays = {
        "x": lay(x),
        "ctx": ctx,
        "ctx_t": lay(ctx.transpose(0, 2, 1)),
        "w_q": lay(L0_xattn_w_q),
        "w_k": lay(L0_xattn_w_k),
        "w_v": lay(L0_xattn_w_v),
        "w_o": lay(L0_xattn_w_o),
        "attn_w": lay(np.stack([np.asarray(w).T for w in (L0_attn_Wk1, L0_attn_Wq1, L0_attn_Wk2, L0_attn_Wproj)])),
        "attn_b": lay(np.stack([np.asarray(v) for v in (L0_attn_bk1, L0_attn_bq1, L0_attn_bk2)], axis=1)),
        "b_proj": lay(L0_attn_bproj),
        "w_g": lay(L0_ffn_Wg),
        "w_1": lay(L0_ffn_W1),
        "w_2": lay(L0_ffn_W2),
    }
    nc = bacc.Bacc("TRN2", target_bir_lowering=False, num_devices=1)
    args = [nc.dram_tensor(f"in_{n}", arrays[n].shape, mybir.dt.from_np(arrays[n].dtype), kind="ExternalInput").ap()
            for n in _INS]
    out = nc.dram_tensor("out", arrays["x"].shape, F32, kind="ExternalOutput").ap()
    perceiver_layer(nc, *args, out)
    r = run_bass_kernel_spmd(nc, [{f"in_{n}": arrays[n] for n in _INS}], core_ids=[0])
    return r.results[0]["out"]
```

```python
from contextlib import ExitStack

import concourse.bass as bass
from concourse import mybir

ALU = mybir.AluOpType
ACT = mybir.ActivationFunctionType
F32 = mybir.dt.float32
BF16 = mybir.dt.bfloat16
I32 = mybir.dt.int32
AX_X = mybir.AxisListType.X

P = 128
EPS_LN = 1e-5
EPS_CUM = 1e-6
LEAK = 0.02
MASK_A, MASK_B = 100.0, -100.0
SCORE_LIMIT = 4900.0


def perceiver_layer(nc, x, ctx, ctx_t, w_q, w_k, w_v, w_o, attn_w, attn_b, b_proj, w_g, w_1, w_2, out):
    B, T, D = x.shape
    KEYS = ctx.shape[1]
    INNER = w_q.shape[1]
    HD = 64
    H = INNER // HD
    NE, _, FF = w_1.shape
    FC = FF // P
    NT = B * T
    CAP = NT // NE
    IC = INNER // P
    KB = KEYS // P
    assert T == P and D == P and B == 4 and H == 16
    QSCALE = HD ** -0.5
    K2_SCALE = LEAK / D ** 0.5
    GROUPS = ((0, 1), (2, 3))
    NG = len(GROUPS)
    SETS = 2 * B
    UNITS = 2 * SETS
    GUARD_CHUNKS = 16
    GUARD_W = B * KEYS // P // GUARD_CHUNKS * D
    GUARD_LOADS = 4
    GUARD_LIMIT = SCORE_LIMIT ** 2 / (D * QSCALE ** 2)

    with ExitStack() as es:
        def sb(name, shape, dt=F32):
            return es.enter_context(nc.sbuf_tensor(name, shape, dt))

        def sem(name):
            return es.enter_context(nc.semaphore(name))

        score_ps = [es.enter_context(nc.psum_tensor(f"score_ps{i}", [P, 512], F32)) for i in range(4)]
        turn_ps = [es.enter_context(nc.psum_tensor(f"turn_ps{i}", [P, 512], F32)) for i in range(2)]
        head_ps = es.enter_context(nc.psum_tensor("head_ps", [P, 512], F32))
        misc_ps = es.enter_context(nc.psum_tensor("misc_ps", [P, 512], F32))

        x_sb = sb("x_sb", [P, B, D])
        ctxk_sb = sb("ctxk_sb", [P, B, T])
        ctx_sb = sb("ctx_sb", [P, GUARD_CHUNKS, GUARD_W])
        sq_sb = sb("sq_sb", [P, 2, GUARD_W])
        wq_sb = sb("wq_sb", [P, INNER])
        wk_sb = sb("wk_sb", [P, INNER])
        wv_sb = sb("wv_sb", [P, INNER])
        wo_sb = sb("wo_sb", [P, IC, D])
        aw_sb = sb("aw_sb", [P, 4, D])
        ab_sb = sb("ab_sb", [P, 3])
        bproj_sb = sb("bproj_sb", [P, D])
        wg_sb = sb("wg_sb", [P, NE])
        w1_sb = sb("w1_sb", [P, NE, FF])
        w2_sb = sb("w2_sb", [P, NE, FC, D])

        ident = sb("ident", [P, P])
        ident_a = sb("ident_a", [P, P], BF16)
        causal_b = sb("causal_b", [P, 4, P], BF16)
        ones = sb("ones", [P, P])
        minus_half = sb("minus_half", [P, 4])

        stats = sb("stats", [P, B, 6])
        mv = sb("mv", [P, B, 2])
        rstd = sb("rstd", [P, B])
        xn_sb = sb("xn_sb", [P, B, D])
        xnT_sb = sb("xnT_sb", [P, B, T])
        kT_sb = sb("kT_sb", [P, IC, NT])
        qT_sb = sb("qT_sb", [P, IC, NT])
        v_sb = sb("v_sb", [P, B, H, HD + 1])

        negmax = sb("negmax", [P, UNITS, 4])
        probs = sb("probs", [P, 4, 4, T])
        probsT = sb("probsT", [P, 2, 4, T])
        rsum = sb("rsum", [P, UNITS, 4])
        wsq_sb = probs[:].rearrange("p a b c -> p (a b c)").rearrange("p (w h d) -> p w h d", w=2, h=H)
        ksum = sb("ksum", [P, GUARD_CHUNKS])
        kmax = sb("kmax", [P, 1])
        wsum = sb("wsum", [P, 2 * H])
        bound = sb("bound", [1, 2 * H + 3])
        flag = sb("flag", [1, 1], I32)
        gone = ctx_sb[:].rearrange("p a b -> p (a b)")
        heads = gone[:, 0:B * INNER].rearrange("p (b h d) -> p b h d", b=B, h=H)
        headsT = gone[:, B * INNER:2 * B * INNER].rearrange("p (c b t) -> p c b t", c=IC, b=B)

        key_room = kT_sb[:].rearrange("p c t -> p (c t)")
        query_room = qT_sb[:].rearrange("p c t -> p (c t)")
        value_room = v_sb[:].rearrange("p b h d -> p (b h d)")
        all_ctx = key_room[:, 0:KEYS]
        all_keys = key_room[0:HD, KEYS:2 * KEYS]
        all_probs = query_room[:, 0:KEYS]
        all_probsT = query_room[:, KEYS:2 * KEYS]
        all_values = value_room[:, 0:KB * HD]
        head_w = value_room[:, KB * HD:(KB + 3) * HD].rearrange("p (w d) -> p w d", w=3)
        batch_x = value_room[:, (KB + 3) * HD:(KB + 5) * HD]
        head_q = value_room[0:HD, (KB + 5) * HD:(KB + 7) * HD]
        all_negmax = sb("all_negmax", [P, 1])
        all_sum = sb("all_sum", [P, 2])
        spare = sb("spare", [P, 1])
        heads_flat = gone[:, 0:B * INNER]

        x1_sb = sb("x1_sb", [P, B, D])
        x1b_sb = sb("x1b_sb", [P, B, D])
        stats2 = sb("stats2", [P, B, 6])
        mv2 = sb("mv2", [P, B, 2])
        rstd2 = sb("rstd2", [P, B])
        xa_sb = sb("xa_sb", [P, B, D])
        xaT = sb("xaT", [P, B, T])
        hb_sb = sb("hb_sb", [P, 2])
        K_sb = sb("K_sb", [P, B, T])
        KV_sb = sb("KV_sb", [P, B, T])
        Kc_sb = sb("Kc_sb", [P, B, T])
        KVc_sb = sb("KVc_sb", [P, B, T])
        tq_sb = sb("tq_sb", [P, B, T])
        tk_sb = sb("tk_sb", [P, B, T])
        Q_sb = sb("Q_sb", [P, B, T])
        Q2_sb = sb("Q2_sb", [P, B, T])
        K2_sb = sb("K2_sb", [P, B, T])
        S_sb = KVc_sb
        Oar_sb = sb("Oar_sb", [P, B, T])
        E_sb = sb("E_sb", [P, B, T])
        S2_sb = sb("S2_sb", [P, B, T])
        Oma_sb = S_sb
        x2_sb = sb("x2_sb", [P, B, D])
        stats3 = sb("stats3", [P, B, 6])
        mv3 = sb("mv3", [P, B, 2])
        rstd3 = sb("rstd3", [P, B])
        xf_sb = sb("xf_sb", [P, B, D])
        xfT = sb("xfT", [P, B, T])

        lmax = sb("lmax", [P, B])
        lsh = sb("lsh", [P, B, NE])
        lexp = sb("lexp", [P, B, NE])
        lsum = sb("lsum", [P, B])
        lrec = sb("lrec", [P, B])
        prob = sb("prob", [P, B, NE])
        probE = sb("probE", [NE, NT])
        work = [sb(f"work{i}", [NE, CAP + (2 * T if i < NG else 0)]) for i in range(NG + 1)]
        sel_eq = sb("sel_eq", [NE, NT])
        tie_win = sb("tie_win", [NE, CAP])
        room = sb("room", [NE, 1])
        tie_rank = sb("tie_rank", [NE, NT])
        sel = sb("sel", [NE, NT])
        ones_e = sb("ones_e", [NE, NT])
        assigned = sb("assigned", [P, B])
        m_sb = sb("m_sb", [P, B, NE])
        val_sb = sb("val_sb", [P, B, NE])
        vmax = sb("vmax", [P, B])
        veq = sb("veq", [P, B, NE])
        order_sb = sb("order_sb", [P, B, NE])
        code = sb("code", [P, B, NE])
        cmax = sb("cmax", [P, B])
        onehot = sb("onehot", [P, B, NE])
        gate = sb("gate", [P, B, NE])
        gelu_sb = probs[:].rearrange("p a b t -> p a (b t)").rearrange("p a (f t) -> p a f t", f=FC)
        diag = sq_sb[:].rearrange("p a b -> p (a b)")[:, 0:NE * P].rearrange("p (e q) -> p e q", e=NE)
        diag = (diag, heads_flat[:, 0:NE * P].rearrange("p (e q) -> p e q", e=NE))
        h_sb = kT_sb[:].rearrange("p (b x) (e d) -> p b (x e) d", b=B, d=D)
        y_sb = x_sb

        names = """ld_x ld_ctxk ld_wv ld_wq ld_wo ld_attn ld_ffn1 ld_ffn2 stored
            consts_ident consts_done zero_done
            ln1_stats ln1_mv ln1_var ln1_rstd ln1_out ln1_T xnT_ready proj proj_act proj_dve
            scores maxes probs_done probs_T pt_act pt_dve pv rsums heads_done headsT_ps headsT_done
            attn_ps x1_done ln2_stats ln2_mv ln2_var ln2_rstd ln2_out x1b_done ln2_T xaT_done
            kq_ps k2_ps K_done tq_done tk_done Q_done Q2_done K2_done hb_done
            KV_done Kc_done KVc_done Krec_done S_done Oar_done E0_done E_done K2E_done S2_done Oma_done O_done
            proj_ps x2_done ln3_stats ln3_mv ln3_var ln3_rstd ln3_out ln3_T xfT_done
            logits_ps lmax_done lsh_done lexp_done lsum_done lrec_done prob_done probE_ps probE_done
            top_step sel_done selT_ps route_step gates_done
            h1_ps gelu_done h2_ps h_act 
            ctx_squared w_squared ksum_done wsum_done bound_ps bound_step flag_ready
            g_room g_ctx g_staged g_qk_ps g_qk g_scores_ps g_masked g_max g_values g_exp g_turned g_turned_sb g_pv g_rec g_head""".split()
        s = {n: sem(n) for n in names}
        (ld_x, ld_ctxk, ld_wv, ld_wq, ld_wo, ld_attn, ld_ffn1, ld_ffn2, stored,
         consts_ident, consts_done, zero_done,
         ln1_stats, ln1_mv, ln1_var, ln1_rstd, ln1_out, ln1_T, xnT_ready, proj, proj_act, proj_dve,
         scores, maxes, probs_done, probs_T, pt_act, pt_dve, pv, rsums, heads_done, headsT_ps, headsT_done,
         attn_ps, x1_done, ln2_stats, ln2_mv, ln2_var, ln2_rstd, ln2_out, x1b_done, ln2_T, xaT_done,
         kq_ps, k2_ps, K_done, tq_done, tk_done, Q_done, Q2_done, K2_done, hb_done,
         KV_done, Kc_done, KVc_done, Krec_done, S_done, Oar_done, E0_done, E_done, K2E_done, S2_done, Oma_done, O_done,
         proj_ps, x2_done, ln3_stats, ln3_mv, ln3_var, ln3_rstd, ln3_out, ln3_T, xfT_done,
         logits_ps, lmax_done, lsh_done, lexp_done, lsum_done, lrec_done, prob_done, probE_ps, probE_done,
         top_step, sel_done, selT_ps, route_step, gates_done,
         h1_ps, gelu_done, h2_ps, h_act,
         ctx_squared, w_squared, ksum_done, wsum_done, bound_ps, bound_step, flag_ready,
         g_room, g_ctx, g_staged, g_qk_ps, g_qk, g_scores_ps, g_masked, g_max, g_values, g_exp, g_turned, g_turned_sb,
         g_pv, g_rec, g_head) = [s[n] for n in names]
        ld_wk = [sem(f"ld_wk{i}") for i in range(2)]
        ld_ctx = [sem(f"ld_ctx{i}") for i in range(GUARD_LOADS)]

        diag_done = [sem(f"diag_done{i}") for i in range(2)]
        combined = [sem(f"combined{i}") for i in range(2)]
        y_step = [sem(f"y_step{i}") for i in range(B)]
        N_PROJ = 3 * IC
        PROJ_V, PROJ_Q = IC, 2 * IC

        def left(j):
            return (proj_act, j // 3 + 1) if j % 3 == 0 else (proj_dve, j - j // 3)

        def turner(i):
            return (pt_act, i // 2 + 1) if i % 2 == 0 else (pt_dve, i // 2 + 1)

        def unit(i):
            return i // 4, i // 2 % 2, i % 2

        AT_PROBS0, AT_PROJ1, AT_TURN1, AT_LOGITS1, AT_PROBS1, AT_PICKS = 0, 4, 7, 9, 12, 11
        INPUT1_E, ROUTER1_E = 4, 5
        ROUNDS = (0, 1, 4, 5)
        WSUM_J = (14, 17)
        BOUND_Q = 6
        SQ0 = 3
        pv_bank = (head_ps,) * (UNITS - 1) + (score_ps[1],)
        turn_bank = (misc_ps,) * (SETS - 2) + (score_ps[3], score_ps[2])
        attn_bank = (misc_ps, score_ps[0])
        post_bank = (misc_ps, head_ps)
        gate2_bank = (misc_ps, score_ps[1])
        sum_ps = (head_ps, score_ps[0])

        def out_ps(g, q, n):
            return (score_ps[2 + n] if q == 0 else turn_ps[n])[:]

        def four(ap):
            return ap.rearrange("p (a b) -> p a b", a=4)

        def read_flag(eng):
            eng.wait_ge(flag_ready, 1)
            return eng.value_load(flag[0:1, 0:1], min_val=0, max_val=1)

        block = es.enter_context(nc.Block())

        @block.sync
        def _(sp):
            guard_rows = ctx.rearrange("b k d -> (b k) d").rearrange("(p r) d -> p (r d)", p=P)
            w = GUARD_CHUNKS * GUARD_W // GUARD_LOADS

            def load_ctx(n):
                sp.dma_start(ctx_sb[:].rearrange("p a b -> p (a b)")[:, n * w:(n + 1) * w],
                             guard_rows[:, n * w:(n + 1) * w]).then_inc(ld_ctx[n], 16)

            for n in range(2):
                sp.dma_start(wk_sb[:, n * 512:(n + 1) * 512], w_k[:, n * 512:(n + 1) * 512]).then_inc(ld_wk[n], 16)
            sp.dma_start(x_sb[:], x.rearrange("b t d -> t b d")).then_inc(ld_x, 16)
            sp.dma_start(wv_sb[:], w_v).then_inc(ld_wv, 16)
            load_ctx(0)
            load_ctx(1)
            sp.dma_start(wq_sb[:], w_q).then_inc(ld_wq, 16)
            load_ctx(2)
            load_ctx(3)
            sp.dma_start(wo_sb[:], w_o.rearrange("(c p) n -> p c n", p=P)).then_inc(ld_wo, 16)
            sp.dma_start(aw_sb[:], attn_w.rearrange("w i o -> i w o")).then_inc(ld_attn, 16)
            sp.dma_start(ab_sb[:], attn_b).then_inc(ld_attn, 16)
            sp.dma_start(bproj_sb[:], b_proj.partition_broadcast(P)).then_inc(ld_attn, 16)
            sp.dma_start(wg_sb[:], w_g).then_inc(ld_attn, 16)
            sp.dma_start(w1_sb[:], w_1.rearrange("e d f -> d e f")).then_inc(ld_ffn1, 16)
            sp.dma_start(w2_sb[:], w_2.rearrange("e (c p) d -> p e c d", p=P)).then_inc(ld_ffn2, 16)
            masked_keys_vanish = read_flag(sp)
            with sp.If(masked_keys_vanish == 0):
                with sp.Fori(0, B) as b:
                    sp.wait_ge(g_room, b * H + 1)
                    sp.dma_start(all_ctx, ctx_t[bass.ds(b, 1)].rearrange("b d k -> (b d) k")).then_inc(g_ctx, 16)
            for b in range(B):
                sp.wait_ge(y_step[b], 1 if b in GROUPS[0] else NE)
            sp.dma_start(out.rearrange("b t d -> t b d"), y_sb[:]).then_inc(stored, 16)
            sp.wait_ge(stored, 16)

        @block.gpsimd
        def _(pool):
            nc.gpsimd.memset(ident[:], 0.0).then_inc(zero_done, 1)
            nc.gpsimd.memset(minus_half[:], -0.5).then_inc(zero_done, 1)
            nc.gpsimd.memset(ident_a[:], 0.0).then_inc(zero_done, 1)
            nc.gpsimd.memset(causal_b[:], 0.0).then_inc(zero_done, 1)
            pool.wait_ge(zero_done, 1)
            nc.gpsimd.affine_select(out=ident[:], in_=ident[:], compare_op=ALU.not_equal, fill=1.0, base=0,
                                    pattern=[[-1, P]], channel_multiplier=1).then_inc(consts_ident, 1)
            pool.wait_ge(ld_x, 16)

            def rsqrt(var_ready, n, of, to, done):
                pool.wait_ge(var_ready, n)
                nc.gpsimd.tensor_tensor(to, of, minus_half[:, 0:to.shape[1]], ALU.pow).then_inc(done, 1)

            pool.wait_ge(zero_done, 4)
            rsqrt(ln1_var, 1, mv[:, :, 1], rstd[:], ln1_rstd)
            nc.gpsimd.affine_select(out=ident_a[:], in_=ident_a[:], compare_op=ALU.not_equal, fill=MASK_A, base=0,
                                    pattern=[[-1, P]], channel_multiplier=1).then_inc(consts_done, 1)
            nc.gpsimd.affine_select(out=causal_b[:], in_=causal_b[:], compare_op=ALU.is_ge, fill=MASK_B, base=0,
                                    pattern=[[0, 4], [-1, P]], channel_multiplier=1).then_inc(consts_done, 1)
            nc.gpsimd.memset(ones[:], 1.0).then_inc(consts_done, 1)
            nc.gpsimd.memset(ones_e[:], 1.0).then_inc(consts_done, 1)
            nc.gpsimd.memset(v_sb[:, :, :, HD:HD + 1], 1.0).then_inc(consts_done, 1)
            for e in range(NE):
                nc.gpsimd.memset(order_sb[:, :, e:e + 1], float(NE - e)).then_inc(consts_done, 1)
            nc.gpsimd.memset(E_sb[:, :, 0:1], 0.0).then_inc(E0_done, 1)
            pool.wait_ge(ld_wk[0], 16)
            pool.wait_ge(ld_wk[1], 16)
            pool.wait_ge(ld_wq, 16)
            for n, w in enumerate((wk_sb, wq_sb)):
                nc.gpsimd.tensor_tensor(wsq_sb[:, n].rearrange("p h d -> p (h d)"), w[:], w[:], ALU.mult).then_inc(w_squared, 1)
            pool.wait_ge(ld_attn, 64)
            nc.gpsimd.tensor_scalar(hb_sb[:, 0:1], ab_sb[:, 1:2], 0.5, None, ALU.mult).then_inc(hb_done, 1)
            nc.gpsimd.tensor_scalar(hb_sb[:, 1:2], ab_sb[:, 2:3], 0.5 * K2_SCALE, None, ALU.mult).then_inc(hb_done, 1)

            def norm2(g):
                b0, n = GROUPS[g][0], len(GROUPS[g])
                rsqrt(ln2_var, g + 1, mv2[:, b0:b0 + n, 1], rstd2[:, b0:b0 + n], ln2_rstd)

            def norm3(g):
                b0, n = GROUPS[g][0], len(GROUPS[g])
                rsqrt(ln3_var, g + 1, mv3[:, b0:b0 + n, 1], rstd3[:, b0:b0 + n], ln3_rstd)

            def gate_products(g):
                b0, n = GROUPS[g][0], len(GROUPS[g])
                bb = slice(b0, b0 + n)
                pool.wait_ge(K_done, g + 1)
                pool.wait_ge(xaT_done, g + 1)
                nc.gpsimd.tensor_tensor(KV_sb[:, bb], K_sb[:, bb], xaT[:, bb], ALU.mult).then_inc(KV_done, 1)
                pool.wait_ge(tq_done, g + 1)
                nc.gpsimd.tensor_scalar(Q_sb[:, bb], tq_sb[:, bb], 0.5, 0.5, ALU.mult, ALU.add).then_inc(Q_done, 1)
                pool.wait_ge(Q_done, g + 1)
                pool.wait_ge(KVc_done, b0 + n)
                nc.gpsimd.tensor_tensor(S_sb[:, bb], KVc_sb[:, bb], Q_sb[:, bb], ALU.mult).then_inc(S_done, 1)
                pool.wait_ge(tk_done, g + 1)
                nc.gpsimd.tensor_scalar(K2_sb[:, bb], tk_sb[:, bb], 0.5, 0.5, ALU.mult, ALU.add).then_inc(K2_done, 1)
                nc.gpsimd.tensor_scalar(Q2_sb[:, bb], Q_sb[:, bb], LEAK / D ** 0.5, None, ALU.mult).then_inc(Q2_done, 1)
                bias = bproj_sb[:].unsqueeze(1).to_broadcast([P, n, D])
                nc.gpsimd.tensor_tensor(x1b_sb[:, bb], x1_sb[:, bb], bias, ALU.add).then_inc(x1b_done, 1)

            norm2(0)
            gate_products(0)
            norm2(1)
            norm3(0)
            gate_products(1)
            norm3(1)
            pool.wait_ge(gates_done, 1)
            for q in range(2):
                four_e = slice(4 * q, 4 * q + 4)
                nc.gpsimd.tensor_tensor(diag[1][:, four_e], ident[:].unsqueeze(1).to_broadcast([P, 4, P]),
                                        gate[:, 1, four_e].unsqueeze(2).to_broadcast([P, 4, P]), ALU.mult).then_inc(diag_done[1], 4)

        @block.scalar
        def _(act):
            act.dma_start(ctxk_sb[:], ctx_t[:, :, 0:T].rearrange("b d k -> d b k")).then_inc(ld_ctxk, 16)

            def square(c):
                if c % (GUARD_CHUNKS // GUARD_LOADS) == 0:
                    act.wait_ge(ld_ctx[c * GUARD_LOADS // GUARD_CHUNKS], 16)
                if c >= 2:
                    act.wait_ge(ctx_squared, c - 1)
                nc.scalar.activation(sq_sb[:, c % 2], ctx_sb[:, c], ACT.Square, accum_out=ksum[:, c:c + 1]).then_inc(ctx_squared, 1)

            for j in range(0, N_PROJ, 3):
                act.wait_ge(proj, j + 1)
                src = score_ps[j % 4][:]
                if j < PROJ_V:
                    nc.scalar.activation(kT_sb[:, j, :], src, ACT.Copy).then_inc(proj_act, 1)
                elif j < PROJ_Q:
                    b, hf = (j - PROJ_V) // 2, (j - PROJ_V) % 2
                    nc.scalar.activation(v_sb[:, b, 8 * hf:8 * hf + 8, 0:HD],
                                         src.rearrange("p (h d) -> p h d", h=8), ACT.Copy).then_inc(proj_act, 1)
                else:
                    nc.scalar.activation(qT_sb[:, j - PROJ_Q, :], src, ACT.Copy, scale=QSCALE).then_inc(proj_act, 1)
                for c in range(max(j - SQ0, 0), min(j - SQ0 + 3, GUARD_CHUNKS)):
                    square(c)

            def exps(i):
                act.wait_ge(maxes, i + 1)
                if i >= 4:
                    act.wait_ge(probs_T, i - 3)
                for j in range(4):
                    a = nc.scalar.activation(probs[:, i % 4, j, :], score_ps[i % 4][:, j * T:(j + 1) * T], ACT.Exp,
                                             bias=negmax[:, i, j:j + 1])
                a.then_inc(probs_done, 1)

            def turned(i):
                act.wait_ge(probs_T, i + 1)
                if i >= 2:
                    act.wait_ge(pv, i - 1)
                nc.scalar.activation(probsT[:, i % 2].rearrange("p a b -> p (a b)"), turn_ps[i % 2][:],
                                     ACT.Copy).then_inc(pt_act, 1)

            def heads_turned(u):
                b, hf = u // 2, u % 2
                act.wait_ge(headsT_ps, u + 1)
                nc.scalar.activation(headsT[:, 4 * hf:4 * hf + 4, b, :], four(turn_bank[u][:]), ACT.Copy).then_inc(headsT_done, 1)

            def post(g, width=T):
                b0, n = GROUPS[g][0], len(GROUPS[g])
                return post_bank[g][:, 0:n * width].rearrange("p (a b) -> p a b", a=n), slice(b0, b0 + n)

            def post_input(g):
                ps, bb = post(g)
                act.wait_ge(ln2_T, g + 1)
                nc.scalar.activation(xaT[:, bb], ps, ACT.Copy).then_inc(xaT_done, 1)

            def post_gates(g):
                ps, bb = post(g)
                n = len(GROUPS[g])
                act.wait_ge(kq_ps, g + 1)
                if g == 0:
                    act.wait_ge(ld_attn, 64)
                    act.wait_ge(hb_done, 2)
                nc.scalar.activation(K_sb[:, bb], ps, ACT.Exp, bias=ab_sb[:, 0:1]).then_inc(K_done, 1)
                nc.scalar.activation(tq_sb[:, bb], post_bank[g][:, 256:256 + n * T].rearrange("p (a b) -> p a b", a=n),
                                     ACT.Tanh, bias=hb_sb[:, 0:1], scale=0.5).then_inc(tq_done, 1)

            def post_gate2(g):
                ps, bb = post(g)
                ps = gate2_bank[g][:, 0:len(GROUPS[g]) * T].rearrange("p (a b) -> p a b", b=T)
                act.wait_ge(k2_ps, g + 1)
                nc.scalar.activation(tk_sb[:, bb], ps, ACT.Tanh, bias=hb_sb[:, 1:2], scale=0.5 * K2_SCALE).then_inc(tk_done, 1)

            def post_input3(g):
                ps, bb = post(g)
                act.wait_ge(ln3_T, g + 1)
                nc.scalar.activation(xfT[:, bb], ps, ACT.Copy).then_inc(xfT_done, 1)

            def post_router(g):
                bb = post(g)[1]
                act.wait_ge(lsh_done, g + 1)
                nc.scalar.activation(lexp[:, bb], lsh[:, bb], ACT.Exp).then_inc(lexp_done, 1)

            def gelu(g, e):
                m = g * NE + e
                act.wait_ge(h1_ps, m + 1)
                if m == 0:
                    act.wait_ge(probs_T, UNITS)
                if m >= 4:
                    act.wait_ge(h2_ps, m - 3)
                nc.scalar.activation(gelu_sb[:, m % 4].rearrange("p a b -> p (a b)"), score_ps[m % 2][:],
                                     ACT.Gelu).then_inc(gelu_done, 1)

            def expert_out(q):
                act.wait_ge(h2_ps, 4 * q + 4)
                for n in range(2):
                    nc.scalar.activation(h_sb[:, n, 4 * q:4 * q + 4, :], four(out_ps(0, q, n)), ACT.Copy).then_inc(h_act, 1)

            def general():
                with act.Fori(0, B * H) as t:
                    act.wait_ge(g_qk_ps, t + 1)
                    nc.scalar.activation(head_q, misc_ps[0:HD, 0:T], ACT.Copy, scale=QSCALE)
                    for c in range(4):
                        a = nc.scalar.activation(all_keys[:, c * 512:(c + 1) * 512], score_ps[c][0:HD, :], ACT.Copy)
                    a.then_inc(g_qk, 1)
                    act.wait_ge(g_max, t + 1)
                    nc.scalar.activation(all_probs, all_probs, ACT.Exp, bias=all_negmax[:], accum_out=all_sum[:, 0:1]).then_inc(g_exp, 1)
                act.wait_ge(g_head, B * H)
                nc.scalar.activation(spare[:], all_negmax[:], ACT.Copy).then_inc(probs_done, UNITS)

            def slots(attention):
                for sl in range(1, SETS + 3):
                    for i in (2 * sl - 2, 2 * sl - 1):
                        if attention and i < UNITS:
                            exps(i)
                        if attention and 0 < i <= UNITS and turner(i - 1)[0] is pt_act:
                            turned(i - 1)
                    if 3 <= sl <= SETS:
                        heads_turned(sl - 3)
                post_input(0)
                heads_turned(SETS - 2)
                post_gates(0)
                heads_turned(SETS - 1)
                post_gate2(0)

            masked_keys_vanish = read_flag(act)
            with act.If(masked_keys_vanish == 0):
                general()
                slots(attention=False)
            with act.Else():
                slots(attention=True)
            post_input(1)
            post_gates(1)
            post_input3(0)
            post_gate2(1)
            post_router(0)
            for e in range(NE):
                gelu(0, e)
                if e == 4:
                    expert_out(0)
                if e == INPUT1_E:
                    post_input3(1)
                if e == ROUTER1_E:
                    post_router(1)
            gelu(1, 0)
            expert_out(1)
            for e in range(1, NE):
                gelu(1, e)
            act.wait_ge(gates_done, 1)
            for e in range(NE):
                nc.scalar.activation(diag[0][:, e], ident[:], ACT.Copy, scale=gate[:, 0, e:e + 1]).then_inc(diag_done[0], 1)

        @block.tensor
        def _(pe):
            pe.wait_ge(consts_ident, 1)
            readers = {}

            def take(bank, reader, count):
                if bank.name in readers:
                    pe.wait_ge(*readers[bank.name])
                readers[bank.name] = (reader, count)

            def proj_bank(j):
                if j >= 4:
                    pe.wait_ge(*left(j - 4))
                return score_ps[j % 4][:]

            pe.wait_ge(ld_ctxk, 16)
            for c in range(IC):
                if c % 4 == 0:
                    pe.wait_ge(ld_wk[c // 4], 16)
                nc.tensor.matmul(proj_bank(c), wk_sb[:, c * P:(c + 1) * P], ctxk_sb[:].rearrange("p b k -> p (b k)"),
                                 start=True, stop=True).then_inc(proj, 1)
            for b in range(B):
                pe.wait_ge(ln1_out, b + 1)
                t = nc.tensor.transpose(turn_ps[0][:, b * T:(b + 1) * T], xn_sb[:, b, :], ident[:])
            t.then_inc(ln1_T, 1)
            pe.wait_ge(ld_wv, 16)
            for b in range(B):
                for hf in range(2):
                    nc.tensor.matmul(proj_bank(PROJ_V + 2 * b + hf), ctxk_sb[:, b, :], wv_sb[:, hf * 512:(hf + 1) * 512],
                                     start=True, stop=True).then_inc(proj, 1)
            pe.wait_ge(ld_wq, 16)
            pe.wait_ge(xnT_ready, 1)
            for c in range(IC):
                if c == BOUND_Q:
                    pe.wait_ge(wsum_done, 2)
                    pe.wait_ge(consts_done, 3)
                    nc.tensor.matmul(misc_ps[0:1, 0:2 * H], ones[:, 0:1], wsum[:], start=True, stop=True)
                    pe.wait_ge(ksum_done, 1)
                    nc.tensor.matmul(misc_ps[0:1, P:2 * P], kmax[:], ident[:], start=True, stop=True).then_inc(bound_ps, 1)
                nc.tensor.matmul(proj_bank(PROJ_Q + c), wq_sb[:, c * P:(c + 1) * P],
                                 xnT_sb[:].rearrange("p b k -> p (b k)"), start=True, stop=True).then_inc(proj, 1)

            def general():
                pe.wait_ge(proj_act, N_PROJ // 3)
                pe.wait_ge(proj_dve, N_PROJ - N_PROJ // 3)
                nc.tensor.transpose(turn_ps[0][:, 0:P], ident[:], ident[:]).then_inc(g_room, 1)
                with pe.Fori(0, B) as b:
                    with pe.Fori(0, H) as h:
                        t1 = b * H + h + 1
                        pe.wait_ge(g_ctx, b * 16 + 16)
                        pe.wait_ge(g_staged, t1)
                        nc.tensor.matmul(misc_ps[0:HD, 0:T], head_w[:, 0], batch_x, start=True, stop=True)
                        for c in range(4):
                            m = nc.tensor.matmul(score_ps[c][0:HD, :], head_w[:, 1], all_ctx[:, c * 512:(c + 1) * 512],
                                                 start=True, stop=True)
                        m.then_inc(g_qk_ps, 1)
                        for k in range(KB):
                            nc.tensor.matmul(turn_ps[k // 8][:, k % 8 * HD:(k % 8 + 1) * HD], all_ctx[:, k * P:(k + 1) * P],
                                             head_w[:, 2], start=True, stop=True)
                        pe.wait_ge(g_qk, t1)
                        for c in range(4):
                            m = nc.tensor.matmul(score_ps[c][:], head_q, all_keys[:, c * 512:(c + 1) * 512],
                                                 start=True, stop=True)
                        m.then_inc(g_scores_ps, 1)
                        pe.wait_ge(g_exp, t1)
                        for k in range(KB):
                            m = nc.tensor.transpose(score_ps[k // 4][:, k % 4 * T:(k % 4 + 1) * T],
                                                    all_probs[:, k * P:(k + 1) * P], ident[:])
                        m.then_inc(g_turned, 1)
                        pe.wait_ge(g_turned_sb, t1)
                        for k in range(KB):
                            m = nc.tensor.matmul(head_ps[:, 0:HD], all_probsT[:, k * T:(k + 1) * T],
                                                 all_values[:, k * HD:(k + 1) * HD], start=(k == 0), stop=(k == KB - 1))
                        m.then_inc(g_pv, 1)
                        nc.tensor.transpose(misc_ps[:, P:2 * P], ident[:], ident[:]).then_inc(g_room, 1)
                nc.tensor.transpose(misc_ps[:, P:2 * P], ident[:], ident[:]).then_inc(probs_T, UNITS)

            def score_set(u, half):
                b, hf = u // 2, u % 2
                if half:
                    score_heads(u, b, hf, (2, 3))
                    return
                if u == 0:
                    pe.wait_ge(consts_done, 5)
                if u < 2:
                    pe.wait_ge(proj_act, N_PROJ // 3)
                    pe.wait_ge(proj_dve, N_PROJ - N_PROJ // 3)
                else:
                    pe.wait_ge(probs_done, 2 * u - 2)
                for par in range(2):
                    nc.tensor.matmul(score_ps[(2 * u + par) % 4][:], ident_a[:], causal_b[:].rearrange("p a b -> p (a b)"),
                                     start=True, stop=False, skip_group_check=True)
                score_heads(u, b, hf, (0, 1))

            def score_heads(u, b, hf, js):
                for j in js:
                    for par in range(2):
                        r = slice(par * HD, (par + 1) * HD)
                        m = nc.tensor.matmul(score_ps[(2 * u + par) % 4][:, j * T:(j + 1) * T],
                                             qT_sb[r, 4 * hf + j, b * T:(b + 1) * T], kT_sb[r, 4 * hf + j, b * T:(b + 1) * T],
                                             start=False, stop=(j == 3), skip_group_check=True)
                        if j == 3:
                            m.then_inc(scores, 1)

            def turn_probs(i):
                pe.wait_ge(probs_done, i + 1)
                if i >= 2:
                    pe.wait_ge(*turner(i - 2))
                for j in range(4):
                    t = nc.tensor.transpose(turn_ps[i % 2][:, j * T:(j + 1) * T], probs[:, i % 4, j, :], ident[:])
                t.then_inc(probs_T, 1)

            def weigh_values(i):
                b, hf, par = unit(i)
                pe.wait_ge(*turner(i))
                if i == UNITS - 1:
                    pe.wait_ge(probs_done, i - 1)
                elif i >= 1:
                    pe.wait_ge(heads_done, i)
                for j in range(4):
                    m = nc.tensor.matmul(pv_bank[i][:, j * (HD + 1):(j + 1) * (HD + 1)], probsT[:, i % 2, j, :],
                                         v_sb[:, b, 8 * hf + 2 * j + par, :], start=True, stop=True)
                m.then_inc(pv, 1)

            def turn_heads(u):
                b, hf = u // 2, u % 2
                pe.wait_ge(heads_done, 2 * u + 2)
                if u >= SETS - 2:
                    pe.wait_ge(probs_done, UNITS)
                else:
                    take(misc_ps, headsT_done, u + 1)
                for c in range(4):
                    t = nc.tensor.transpose(turn_bank[u][:, c * T:(c + 1) * T],
                                            heads[:, b, 8 * hf + 2 * c:8 * hf + 2 * c + 2, :].rearrange("p h d -> p (h d)"),
                                            ident[:])
                t.then_inc(headsT_ps, 1)

            def post_out(g, parts):
                if g == 0:
                    pe.wait_ge(ld_wo, 16)
                ps = attn_bank[g]
                for b, hf in parts:
                    n = b - GROUPS[g][0]
                    if (n, hf) == (0, 0):
                        if g == 0:
                            take(ps, x1_done, 1)
                        else:
                            pe.wait_ge(probs_done, UNITS - 3)
                    pe.wait_ge(headsT_done, 2 * b + hf + 1)
                    for c in range(4 * hf, 4 * hf + 4):
                        m = nc.tensor.matmul(ps[:, n * D:(n + 1) * D], headsT[:, c, b, :], wo_sb[:, c, :],
                                             start=(c == 0), stop=(c == IC - 1))
                    if (b, hf) == (GROUPS[g][-1], 1):
                        m.then_inc(attn_ps, 1)

            def post_turn(g, ready, rows, done, reader):
                ps = post_bank[g]
                pe.wait_ge(ready, GROUPS[g][-1] + 1)
                if g == 1:
                    pe.wait_ge(heads_done, UNITS)
                take(ps, reader, g + 1)
                for n, b in enumerate(GROUPS[g]):
                    t = nc.tensor.transpose(ps[:, n * T:(n + 1) * T], rows[:, b, :], ident[:])
                t.then_inc(done, 1)

            def gate_input(g):
                return xaT[:, GROUPS[g][0]:GROUPS[g][-1] + 1].rearrange("p b t -> p (b t)")

            def post_gates(g):
                ps, n = post_bank[g], len(GROUPS[g])
                if g == 0:
                    pe.wait_ge(ld_attn, 64)
                take(ps, tq_done, g + 1)
                nc.tensor.matmul(ps[:, 0:n * T], aw_sb[:, 0, :], gate_input(g), start=True, stop=True)
                nc.tensor.matmul(ps[:, 256:256 + n * T], aw_sb[:, 1, :], gate_input(g), start=True, stop=True).then_inc(kq_ps, 1)

            def post_gate2(g):
                ps, n = gate2_bank[g], len(GROUPS[g])
                if g == 0:
                    take(ps, tk_done, g + 1)
                nc.tensor.matmul(ps[:, 0:n * T], aw_sb[:, 2, :], gate_input(g), start=True, stop=True).then_inc(k2_ps, 1)

            def post_proj(g):
                ps = post_bank[g]
                pe.wait_ge(O_done, g + 1)
                take(ps, x2_done, g + 1)
                for n, b in enumerate(GROUPS[g]):
                    m = nc.tensor.matmul(ps[:, n * D:(n + 1) * D], Oar_sb[:, b, :], aw_sb[:, 3, :], start=True, stop=True)
                m.then_inc(proj_ps, 1)

            def post_logits(g):
                ps = post_bank[g]
                take(ps, lsh_done, g + 1)
                for n, b in enumerate(GROUPS[g]):
                    m = nc.tensor.matmul(ps[:, n * NE:(n + 1) * NE], xfT[:, b, :], wg_sb[:], start=True, stop=True)
                m.then_inc(logits_ps, 1)

            def post_probs(g):
                ps = post_bank[g]
                pe.wait_ge(prob_done, g + 1)
                take(ps, probE_done, g + 1)
                for n, b in enumerate(GROUPS[g]):
                    t = nc.tensor.transpose(ps[0:NE, n * T:(n + 1) * T], prob[:, b, :], ident[:])
                t.then_inc(probE_ps, 1)

            def hidden(g, e):
                m = g * NE + e
                n = len(GROUPS[g])
                if m == 0:
                    pe.wait_ge(ld_ffn1, 16)
                    pe.wait_ge(x1_done, NG)
                if m == 1:
                    pe.wait_ge(tk_done, NG)
                if m >= 2:
                    pe.wait_ge(gelu_done, m - 1)
                for f in range(FC):
                    mm = nc.tensor.matmul(score_ps[m % 2][:, f * n * T:(f + 1) * n * T], w1_sb[:, e, f * P:(f + 1) * P],
                                          xfT[:, GROUPS[g][0]:GROUPS[g][0] + n].rearrange("p b t -> p (b t)"),
                                          start=True, stop=True)
                mm.then_inc(h1_ps, 1)

            def answer(g, e):
                m = g * NE + e
                pe.wait_ge(gelu_done, m + 1)
                if m == 0:
                    pe.wait_ge(ld_ffn2, 16)
                if g == 1 and e % 4 == 0:
                    pe.wait_ge(h_act, e // 2 + 2)
                for n in range(len(GROUPS[g])):
                    for f in range(FC):
                        mm = nc.tensor.matmul(out_ps(g, e // 4, n)[:, e % 4 * D:(e % 4 + 1) * D],
                                              gelu_sb[:, m % 4, f, n * T:(n + 1) * T], w2_sb[:, e, f, :],
                                              start=(f == 0), stop=(f == FC - 1))
                mm.then_inc(h2_ps, 1)

            def slots(attention):
                for sl in range(SETS):
                    for half in range(2):
                        if attention:
                            score_set(sl, half)
                        i = 2 * sl - 3 + half
                        if attention and i >= 0:
                            turn_probs(i)
                        if attention and i >= 1:
                            weigh_values(i - 1)
                    if sl >= 3:
                        turn_heads(sl - 3)
                if attention:
                    turn_probs(UNITS - 3)
                    weigh_values(UNITS - 4)
                post_out(0, ((0, 0), (0, 1), (1, 0), (1, 1)))
                if attention:
                    turn_probs(UNITS - 2)
                    turn_probs(UNITS - 1)
                    weigh_values(UNITS - 3)
                turn_heads(SETS - 3)
                if attention:
                    weigh_values(UNITS - 2)
                post_turn(0, ln2_out, xa_sb, ln2_T, xaT_done)
                if attention:
                    weigh_values(UNITS - 1)
                turn_heads(SETS - 2)
                post_gates(0)
                post_out(1, ((2, 0),))
                turn_heads(SETS - 1)
                post_gate2(0)
                post_out(1, ((2, 1), (3, 0), (3, 1)))

            def post_picks():
                pe.wait_ge(sel_done, 1)
                take(misc_ps, gates_done, 1)
                for b in range(B):
                    t = nc.tensor.transpose(misc_ps[:, b * NE:(b + 1) * NE], sel[:, b * T:(b + 1) * T],
                                            ident[0:NE, 0:NE])
                t.then_inc(selT_ps, 1)

            def routing(at):
                if at == AT_PROBS0:
                    post_probs(0)
                if at == AT_PROJ1:
                    post_proj(1)
                if at == AT_TURN1:
                    post_turn(1, ln3_out, xf_sb, ln3_T, xfT_done)
                if at == AT_LOGITS1:
                    post_logits(1)
                if at == AT_PROBS1:
                    post_probs(1)

            masked_keys_vanish = read_flag(pe)
            with pe.If(masked_keys_vanish == 0):
                general()
                slots(attention=False)
            readers.clear()
            with pe.Else():
                slots(attention=True)
            post_proj(0)
            post_turn(1, ln2_out, xa_sb, ln2_T, xaT_done)
            post_gates(1)
            post_turn(0, ln3_out, xf_sb, ln3_T, xfT_done)
            post_gate2(1)
            post_logits(0)
            hidden(0, 0)
            for e in range(NE):
                if e + 1 < NE:
                    hidden(0, e + 1)
                routing(2 * e)
                answer(0, e)
                routing(2 * e + 1)
            hidden(1, 0)
            for e in range(NE):
                if e + 1 < NE:
                    hidden(1, e + 1)
                if 2 * e == AT_PICKS:
                    post_picks()
                answer(1, e)
                if 2 * e + 1 == AT_PICKS:
                    post_picks()
            pe.wait_ge(gelu_done, NG * NE)
            for q in range(2):
                for b in GROUPS[0]:
                    for e in range(4 * q, 4 * q + 4):
                        pe.wait_ge(diag_done[b], e + 1)
                        nc.tensor.matmul(sum_ps[b][:, 0:D], diag[b][:, e], h_sb[:, b, e, :], start=(e == 0),
                                         stop=(e == NE - 1)).then_inc(combined[b], 1)

        @block.vector
        def _(dve):
            def norm_stats(b0, n, rows, st, m, stats_done, mv_done, var_done):
                for b in range(b0, b0 + n):
                    nc.vector.bn_stats(st[:, b, :], rows[:, b, :]).then_inc(stats_done, 1)
                for b in range(b0, b0 + n):
                    dve.wait_ge(stats_done, b + 1)
                    nc.vector.bn_aggr(m[:, b, :], st[:, b, :]).then_inc(mv_done, 1)
                dve.wait_ge(mv_done, b0 + n)
                nc.vector.tensor_scalar(m[:, b0:b0 + n, 1], m[:, b0:b0 + n, 1], EPS_LN, None, ALU.add).then_inc(var_done, 1)

            def norm_apply(b0, n, rows, m, r, y, rstd_done, out_done, g):
                dve.wait_ge(rstd_done, g + 1)
                for b in range(b0, b0 + n):
                    nc.vector.tensor_scalar(y[:, b, :], rows[:, b, :], m[:, b, 0:1], r[:, b:b + 1],
                                            ALU.subtract, ALU.mult).then_inc(out_done, 1)

            def weight_norms(n):
                dve.wait_ge(w_squared, n + 1)
                nc.vector.tensor_reduce(wsum[:, n * H:(n + 1) * H], wsq_sb[:, n], AX_X, ALU.add).then_inc(wsum_done, 1)

            def bound_of_scores():
                dve.wait_ge(ctx_squared, GUARD_CHUNKS)
                nc.vector.tensor_reduce(kmax[:], ksum[:], AX_X, ALU.max).then_inc(ksum_done, 1)
                dve.wait_ge(bound_ps, 1)
                nc.vector.tensor_copy(bound[:, 0:H], misc_ps[0:1, 0:H]).then_inc(bound_step, 1)
                nc.vector.tensor_reduce(bound[:, 2 * H:2 * H + 1], misc_ps[0:1, P:2 * P], AX_X, ALU.max).then_inc(bound_step, 1)
                dve.wait_ge(bound_step, 2)
                nc.vector.tensor_tensor(bound[:, H:2 * H], misc_ps[0:1, H:2 * H], bound[:, 0:H], ALU.mult).then_inc(bound_step, 1)
                dve.wait_ge(bound_step, 3)
                nc.vector.tensor_reduce(bound[:, 2 * H + 1:2 * H + 2], bound[:, H:2 * H], AX_X, ALU.max).then_inc(bound_step, 1)
                dve.wait_ge(bound_step, 4)
                nc.vector.tensor_tensor(bound[:, 2 * H + 2:2 * H + 3], bound[:, 2 * H:2 * H + 1], bound[:, 2 * H + 1:2 * H + 2],
                                        ALU.mult).then_inc(bound_step, 1)
                dve.wait_ge(bound_step, 5)
                nc.vector.tensor_scalar(flag[:], bound[:, 2 * H + 2:2 * H + 3], GUARD_LIMIT, None, ALU.is_lt).then_inc(flag_ready, 1)

            dve.wait_ge(ld_x, 16)
            norm_stats(0, B, x_sb, stats, mv, ln1_stats, ln1_mv, ln1_var)
            norm_apply(0, B, x_sb, mv, rstd, xn_sb, ln1_rstd, ln1_out, 0)

            for j in range(N_PROJ):
                if j in WSUM_J:
                    weight_norms(WSUM_J.index(j))
                if j == PROJ_Q + BOUND_Q:
                    bound_of_scores()
                if j % 3 == 0:
                    continue
                if j == PROJ_V + 2:
                    dve.wait_ge(ln1_T, 1)
                    nc.vector.tensor_copy(xnT_sb[:], four(turn_ps[0][:])).then_inc(xnT_ready, 1)
                dve.wait_ge(proj, j + 1)
                src = score_ps[j % 4][:]
                if j < PROJ_V:
                    nc.vector.tensor_copy(kT_sb[:, j, :], src).then_inc(proj_dve, 1)
                elif j < PROJ_Q:
                    b, hf = (j - PROJ_V) // 2, (j - PROJ_V) % 2
                    nc.vector.tensor_copy(v_sb[:, b, 8 * hf:8 * hf + 8, 0:HD],
                                          src.rearrange("p (h d) -> p h d", h=8)).then_inc(proj_dve, 1)
                else:
                    nc.vector.tensor_scalar(qT_sb[:, j - PROJ_Q, :], src, QSCALE, None, ALU.mult).then_inc(proj_dve, 1)

            def general():
                with dve.Fori(0, B) as b:
                    with dve.Fori(0, H) as h:
                        t1 = b * H + h + 1
                        dve.wait_ge(g_room, t1)
                        for n, w in enumerate((wq_sb, wk_sb, wv_sb)):
                            nc.vector.tensor_copy(head_w[:, n], w[:, bass.ds(h * HD, HD)])
                        nc.vector.tensor_copy(batch_x, xnT_sb[:].rearrange("p b t -> p (b t)")[:, bass.ds(b * T, T)]).then_inc(g_staged, 1)
                        dve.wait_ge(g_scores_ps, t1)
                        nc.vector.scalar_tensor_tensor(all_probs[:, 0:T], causal_b[:, 0, :], MASK_A, score_ps[0][:, 0:T],
                                                       ALU.mult, ALU.add)
                        nc.vector.tensor_scalar(all_probs[:, T:512], score_ps[0][:, T:512], MASK_A * MASK_B, None, ALU.add)
                        for c in range(1, 4):
                            m = nc.vector.tensor_scalar(all_probs[:, c * 512:(c + 1) * 512], score_ps[c][:], MASK_A * MASK_B,
                                                        None, ALU.add)
                        m.then_inc(g_masked, 1)
                        dve.wait_ge(g_masked, t1)
                        nc.vector.tensor_reduce(all_negmax[:], all_probs, AX_X, ALU.max, negate=True).then_inc(g_max, 1)
                        for c in range(2):
                            m = nc.vector.tensor_copy(all_values[:, c * 512:(c + 1) * 512], turn_ps[c][:])
                        m.then_inc(g_values, 1)
                        dve.wait_ge(g_turned, t1)
                        for c in range(4):
                            m = nc.vector.tensor_copy(all_probsT[:, c * 512:(c + 1) * 512], score_ps[c][:])
                        m.then_inc(g_turned_sb, 1)
                        nc.vector.reciprocal(all_sum[:, 1:2], all_sum[:, 0:1]).then_inc(g_rec, 1)
                        dve.wait_ge(g_rec, t1)
                        dve.wait_ge(g_pv, t1)
                        nc.vector.tensor_scalar(heads_flat[:, bass.ds((b * H + h) * HD, HD)], head_ps[:, 0:HD], all_sum[:, 1:2],
                                                None, ALU.mult).then_inc(g_head, 1)
                dve.wait_ge(g_head, B * H)
                nc.vector.tensor_copy(all_sum[:, 0:1], all_sum[:, 1:2]).then_inc(heads_done, UNITS)

            def row_max(i):
                dve.wait_ge(scores, i + 1)
                nc.vector.tensor_reduce(negmax[:, i, :], four(score_ps[i % 4][:]), AX_X, ALU.max,
                                        negate=True).then_inc(maxes, 1)

            def turned(i):
                dve.wait_ge(probs_T, i + 1)
                if i >= 2:
                    dve.wait_ge(pv, i - 1)
                nc.vector.tensor_copy(probsT[:, i % 2], four(turn_ps[i % 2][:])).then_inc(pt_dve, 1)

            def norm_heads(i):
                b, hf, par = unit(i)
                got = pv_bank[i][:, 0:4 * (HD + 1)].rearrange("p (j d) -> p j d", j=4)
                dve.wait_ge(pv, i + 1)
                nc.vector.reciprocal(rsum[:, i, :], got[:, :, HD]).then_inc(rsums, 1)
                dve.wait_ge(rsums, i + 1)
                to = heads[:, b, 8 * hf:8 * hf + 8, :].rearrange("p (j q) d -> p j q d", q=2)[:, :, par, :]
                nc.vector.tensor_tensor(to, got[:, :, 0:HD], rsum[:, i, :].unsqueeze(2).to_broadcast([P, 4, HD]),
                                        ALU.mult).then_inc(heads_done, 1)

            def group(g, width):
                b0, n = GROUPS[g][0], len(GROUPS[g])
                return post_bank[g][:, 0:n * width].rearrange("p (a b) -> p a b", a=n), b0, n

            def post_x1(g):
                b0, n = group(g, D)[1:]
                ps = attn_bank[g][:, 0:n * D].rearrange("p (a b) -> p a b", a=n)
                dve.wait_ge(attn_ps, g + 1)
                nc.vector.tensor_tensor(x1_sb[:, b0:b0 + n], x_sb[:, b0:b0 + n], ps, ALU.add).then_inc(x1_done, 1)
                dve.wait_ge(x1_done, g + 1)
                norm_stats(b0, n, x1_sb, stats2, mv2, ln2_stats, ln2_mv, ln2_var)

            def post_norm2(g):
                b0, n = group(g, D)[1:]
                norm_apply(b0, n, x1_sb, mv2, rstd2, xa_sb, ln2_rstd, ln2_out, g)

            def post_sums(g):
                bs = GROUPS[g]
                b0, n = bs[0], len(bs)
                bb = slice(b0, b0 + n)
                one = ones[:]
                dve.wait_ge(K_done, g + 1)
                if g == 0:
                    dve.wait_ge(consts_done, 3)
                for b in bs:
                    nc.vector.tensor_tensor_scan(Kc_sb[:, b, :], one, K_sb[:, b, :], EPS_CUM, ALU.mult, ALU.add).then_inc(Kc_done, 1)
                dve.wait_ge(KV_done, g + 1)
                for b in bs:
                    nc.vector.tensor_tensor_scan(KVc_sb[:, b, :], one, KV_sb[:, b, :], 0.0, ALU.mult, ALU.add).then_inc(KVc_done, 1)
                dve.wait_ge(Kc_done, b0 + n)
                nc.vector.reciprocal(Kc_sb[:, bb], Kc_sb[:, bb]).then_inc(Krec_done, 1)

            def post_errors(g):
                b0, n = GROUPS[g][0], len(GROUPS[g])
                bb = slice(b0, b0 + n)
                dve.wait_ge(Krec_done, g + 1)
                dve.wait_ge(S_done, g + 1)
                nc.vector.tensor_tensor(Oar_sb[:, bb], S_sb[:, bb], Kc_sb[:, bb], ALU.mult).then_inc(Oar_done, 1)
                dve.wait_ge(Oar_done, g + 1)
                dve.wait_ge(E0_done, 1)
                nc.vector.tensor_tensor(E_sb[:, bb, 1:T], xaT[:, bb, 1:T], Oar_sb[:, bb, 0:T - 1],
                                        ALU.subtract).then_inc(E_done, 1)
                dve.wait_ge(E_done, g + 1)
                dve.wait_ge(K2_done, g + 1)
                nc.vector.tensor_tensor(E_sb[:, bb, 1:T], E_sb[:, bb, 1:T], K2_sb[:, bb, 0:T - 1],
                                        ALU.mult).then_inc(K2E_done, 1)

            def post_corrected(g):
                bs = GROUPS[g]
                b0, n = bs[0], len(bs)
                bb = slice(b0, b0 + n)
                dve.wait_ge(K2E_done, g + 1)
                for b in bs:
                    nc.vector.tensor_tensor_scan(S2_sb[:, b, :], ones[:], E_sb[:, b, :], 0.0, ALU.mult, ALU.add).then_inc(S2_done, 1)
                dve.wait_ge(S2_done, b0 + n)
                dve.wait_ge(Q2_done, g + 1)
                nc.vector.tensor_tensor(Oma_sb[:, bb, 1:T], S2_sb[:, bb, 1:T], Q2_sb[:, bb, 0:T - 1],
                                        ALU.mult).then_inc(Oma_done, 1)
                dve.wait_ge(Oma_done, g + 1)
                nc.vector.tensor_tensor(Oar_sb[:, bb, 1:T], Oar_sb[:, bb, 1:T], Oma_sb[:, bb, 1:T],
                                        ALU.add).then_inc(O_done, 1)

            def post_x2(g):
                ps, b0, n = group(g, D)
                dve.wait_ge(proj_ps, g + 1)
                dve.wait_ge(x1b_done, g + 1)
                nc.vector.tensor_tensor(x2_sb[:, b0:b0 + n], x1b_sb[:, b0:b0 + n], ps, ALU.add).then_inc(x2_done, 1)
                dve.wait_ge(x2_done, g + 1)
                norm_stats(b0, n, x2_sb, stats3, mv3, ln3_stats, ln3_mv, ln3_var)

            def post_norm3(g):
                b0, n = group(g, D)[1:]
                norm_apply(b0, n, x2_sb, mv3, rstd3, xf_sb, ln3_rstd, ln3_out, g)

            def post_shift(g):
                logits, b0, n = group(g, NE)
                bb = slice(b0, b0 + n)
                dve.wait_ge(logits_ps, g + 1)
                nc.vector.tensor_reduce(lmax[:, bb], logits, AX_X, ALU.max).then_inc(lmax_done, 1)
                dve.wait_ge(lmax_done, g + 1)
                nc.vector.tensor_tensor(lsh[:, bb], logits, lmax[:, bb].unsqueeze(2).to_broadcast([P, n, NE]),
                                        ALU.subtract).then_inc(lsh_done, 1)

            def post_prob(g):
                b0, n = group(g, NE)[1:]
                bb = slice(b0, b0 + n)
                dve.wait_ge(lexp_done, g + 1)
                nc.vector.tensor_reduce(lsum[:, bb], lexp[:, bb], AX_X, ALU.add).then_inc(lsum_done, 1)
                dve.wait_ge(lsum_done, g + 1)
                nc.vector.reciprocal(lrec[:, bb], lsum[:, bb]).then_inc(lrec_done, 1)
                dve.wait_ge(lrec_done, g + 1)
                nc.vector.tensor_tensor(prob[:, bb], lexp[:, bb], lrec[:, bb].unsqueeze(2).to_broadcast([P, n, NE]),
                                        ALU.mult).then_inc(prob_done, 1)

            def post_probE(g):
                b0, n = group(g, NE)[1:]
                dve.wait_ge(probE_ps, g + 1)
                nc.vector.tensor_copy(probE[:, b0 * T:(b0 + n) * T], post_bank[g][0:NE, 0:n * T]).then_inc(probE_done, 1)

            tops = [0]

            def top_start(g):
                b0, n = GROUPS[g][0], len(GROUPS[g])
                dve.wait_ge(probE_done, g + 1)
                nc.vector.tensor_copy(work[g][:, CAP:CAP + n * T], probE[:, b0 * T:(b0 + n) * T]).then_inc(top_step, 1)
                tops[0] += 1

            def top_rounds(g, rounds):
                cur, nxt = work[g], work[g + 1]
                here = slice(0 if g else CAP, CAP + len(GROUPS[g]) * T)
                for r in rounds:
                    eight = nxt[:, 8 * r:8 * r + 8]
                    dve.wait_ge(top_step, tops[0])
                    nc.vector.max(eight, cur[:, here]).then_inc(top_step, 1)
                    tops[0] += 1
                    if r + 1 < CAP // 8:
                        dve.wait_ge(top_step, tops[0])
                        nc.vector.match_replace(out=cur[:, here], in_to_replace=eight, in_values=cur[:, here],
                                                imm_value=-1.0).then_inc(top_step, 1)
                        tops[0] += 1

            def choose():
                won = work[NG]
                least = won[:, CAP - 1:CAP]
                dve.wait_ge(top_step, tops[0])
                nc.vector.tensor_scalar(sel_eq[:], probE[:], least, None, ALU.is_equal).then_inc(top_step, 1)
                nc.vector.tensor_scalar(tie_win[:], won[:], least, 0.0, ALU.is_equal, ALU.add, accum_out=room[:]).then_inc(top_step, 1)
                tops[0] += 2
                dve.wait_ge(top_step, tops[0])
                nc.vector.tensor_tensor_scan(tie_rank[:], ones_e[:], sel_eq[:], 0.0, ALU.mult, ALU.add).then_inc(top_step, 1)
                tops[0] += 1
                dve.wait_ge(top_step, tops[0])
                nc.vector.scalar_tensor_tensor(tie_rank[:], tie_rank[:], room[:], sel_eq[:], ALU.is_le,
                                               ALU.mult).then_inc(top_step, 1)
                tops[0] += 1
                dve.wait_ge(top_step, tops[0])
                nc.vector.scalar_tensor_tensor(sel[:], probE[:], least, tie_rank[:], ALU.is_gt, ALU.add).then_inc(sel_done, 1)

            def gates():
                picked = misc_ps[:, 0:B * NE].rearrange("p (b e) -> p b e", b=B)
                steps = [0]

                def done(ins):
                    ins.then_inc(route_step, 1)
                    steps[0] += 1

                def wait():
                    dve.wait_ge(route_step, steps[0])

                def wide(ap):
                    return ap.unsqueeze(2).to_broadcast([P, B, NE])

                dve.wait_ge(selT_ps, 1)
                done(nc.vector.tensor_reduce(assigned[:], picked, AX_X, ALU.max))
                wait()
                done(nc.vector.scalar_tensor_tensor(m_sb[:], wide(assigned[:]), 0.0, picked, ALU.is_equal, ALU.max))
                wait()
                done(nc.vector.tensor_tensor(val_sb[:], prob[:], m_sb[:], ALU.mult))
                wait()
                done(nc.vector.tensor_reduce(vmax[:], val_sb[:], AX_X, ALU.max))
                wait()
                done(nc.vector.tensor_tensor(veq[:], val_sb[:], wide(vmax[:]), ALU.is_equal))
                wait()
                dve.wait_ge(consts_done, 5 + NE)
                done(nc.vector.tensor_tensor(code[:], veq[:], order_sb[:], ALU.mult))
                wait()
                done(nc.vector.tensor_reduce(cmax[:], code[:], AX_X, ALU.max))
                wait()
                done(nc.vector.tensor_tensor(onehot[:], code[:], wide(cmax[:]), ALU.is_equal))
                wait()
                nc.vector.tensor_tensor(gate[:], onehot[:], wide(vmax[:]), ALU.mult).then_inc(gates_done, 1)

            def slots(attention):
                for sl in range(1, SETS + 3):
                    for i in (2 * sl - 2, 2 * sl - 1):
                        if attention and i < UNITS:
                            row_max(i)
                    for i in (2 * sl - 3, 2 * sl - 2):
                        if attention and 0 <= i < UNITS - 1 and turner(i)[0] is pt_dve:
                            turned(i)
                        if attention and 1 <= i <= UNITS:
                            norm_heads(i - 1)
                        if i == 2 * SETS - 3:
                            post_x1(0)
                        if i == 2 * SETS - 2:
                            if attention:
                                turned(UNITS - 1)
                            post_norm2(0)

            masked_keys_vanish = read_flag(dve)
            with dve.If(masked_keys_vanish == 0):
                general()
                slots(attention=False)
            with dve.Else():
                slots(attention=True)
            post_sums(0)
            post_errors(0)
            post_x1(1)
            post_corrected(0)
            post_norm2(1)
            post_x2(0)
            post_norm3(0)
            post_shift(0)
            post_prob(0)
            post_sums(1)
            post_errors(1)
            post_corrected(1)
            post_probE(0)
            top_start(0)
            top_rounds(0, range(0, ROUNDS[0]))
            post_x2(1)
            top_rounds(0, range(ROUNDS[0], ROUNDS[1]))
            post_norm3(1)
            top_rounds(0, range(ROUNDS[1], ROUNDS[2]))
            post_shift(1)
            top_rounds(0, range(ROUNDS[2], ROUNDS[3]))
            post_prob(1)
            top_rounds(0, range(ROUNDS[3], CAP // 8))
            post_probE(1)
            top_start(1)
            top_rounds(1, range(CAP // 8))
            choose()
            gates()
            dve.wait_ge(gates_done, 1)
            for e in range(NE):
                for n, b in enumerate(GROUPS[1]):
                    if n == 0:
                        dve.wait_ge(h2_ps, NE + e // 4 * 4 + 4)
                    if e:
                        dve.wait_ge(y_step[b], e)
                    nc.vector.scalar_tensor_tensor(y_sb[:, b, :], out_ps(1, e // 4, n)[:, e % 4 * D:(e % 4 + 1) * D],
                                                   gate[:, b, e:e + 1], (y_sb if e else x2_sb)[:, b, :],
                                                   ALU.mult, ALU.add).then_inc(y_step[b], 1)

            for b in GROUPS[0]:
                dve.wait_ge(combined[b], NE)
                nc.vector.tensor_tensor(y_sb[:, b, :], sum_ps[b][:, 0:D], x2_sb[:, b, :], ALU.add).then_inc(y_step[b], 1)


_INS = ["x", "ctx", "ctx_t", "w_q", "w_k", "w_v", "w_o", "attn_w", "attn_b", "b_proj", "w_g", "w_1", "w_2"]


def kernel(x, ctx_1024, L0_xattn_w_q, L0_xattn_w_k, L0_xattn_w_v, L0_xattn_w_o, L0_attn_Wq1, L0_attn_bq1,
           L0_attn_Wk1, L0_attn_bk1, L0_attn_Wk2, L0_attn_bk2, L0_attn_Wproj, L0_attn_bproj,
           L0_ffn_Wg, L0_ffn_W1, L0_ffn_W2):
    import numpy as np
    import concourse.bacc as bacc
    from concourse.bass_utils import run_bass_kernel_spmd

    def lay(a):
        return np.ascontiguousarray(np.asarray(a))

    ctx = lay(ctx_1024)
    arrays = {
        "x": lay(x),
        "ctx": ctx,
        "ctx_t": lay(ctx.transpose(0, 2, 1)),
        "w_q": lay(L0_xattn_w_q),
        "w_k": lay(L0_xattn_w_k),
        "w_v": lay(L0_xattn_w_v),
        "w_o": lay(L0_xattn_w_o),
        "attn_w": lay(np.stack([np.asarray(w).T for w in (L0_attn_Wk1, L0_attn_Wq1, L0_attn_Wk2, L0_attn_Wproj)])),
        "attn_b": lay(np.stack([np.asarray(v) for v in (L0_attn_bk1, L0_attn_bq1, L0_attn_bk2)], axis=1)),
        "b_proj": lay(L0_attn_bproj),
        "w_g": lay(L0_ffn_Wg),
        "w_1": lay(L0_ffn_W1),
        "w_2": lay(L0_ffn_W2),
    }
    nc = bacc.Bacc("TRN2", target_bir_lowering=False, num_devices=1)
    args = [nc.dram_tensor(f"in_{n}", arrays[n].shape, mybir.dt.from_np(arrays[n].dtype), kind="ExternalInput").ap()
            for n in _INS]
    out = nc.dram_tensor("out", arrays["x"].shape, F32, kind="ExternalOutput").ap()
    perceiver_layer(nc, *args, out)
    r = run_bass_kernel_spmd(nc, [{f"in_{n}": arrays[n] for n in _INS}], core_ids=[0])
    return r.results[0]["out"]
```
